# Optimizing a Trainium2 kernel written in Bass

```python
import numpy as np
import jax
import jax.numpy as jnp

def _softmax(x, axis=-1):
    return jax.nn.softmax(x, axis=axis)

def _gelu(x):
    return jax.nn.gelu(x, approximate=True)

def _silu(x):
    return jax.nn.silu(x)

def _sigmoid(x):
    return jax.nn.sigmoid(x)

def _layernorm(x, axis=-1, eps=1e-05):
    m = jnp.mean(x, axis=axis, keepdims=True)
    v = jnp.var(x, axis=axis, keepdims=True)
    return (x - m) / jnp.sqrt(v + eps)

def _scatter_add(tgt, idx, src, axis=0):
    return tgt.at[idx].add(src)

def _segment_sum(src, seg, n):
    return jax.ops.segment_sum(src, seg, n)
kernel_name = 'mk_adaln_d1_jaxref_r4_500914'

def setup_inputs(seed: int=0):
    np.random.seed(seed)
    _w = jnp.asarray

    def _L0_attn_setup():
        import jax, jax.numpy as jnp
        import numpy as np
        from jax import lax
        D_MODEL = 256
        D_INNER = 512
        D_STATE = 16
        DT_RANK = 128
        K = 4
        EPS = 1e-05

        def _layer_norm(x, w, b):
            mu = jnp.mean(x, axis=-1, keepdims=True)
            var = jnp.mean(jnp.square(x - mu), axis=-1, keepdims=True)
            return (x - mu) * lax.rsqrt(var + EPS) * w + b

        def _causal_depthwise_conv(x, w, b):
            L = x.shape[1]
            xp = jnp.pad(x, ((0, 0), (K - 1, 0), (0, 0)))
            out = b
            for k in range(K):
                out = out + w[:, k] * xp[:, k:k + L, :]
            return out

        def _selective_scan(u, delta, A, B, C, D):
            deltaA = jnp.exp(jnp.einsum('bld,dn->bldn', delta, A))
            deltaBu = jnp.einsum('bld,bln,bld->bldn', delta, B, u)
            bsz, _, d, n = deltaA.shape

            def step(h, inp):
                dA, dBu, Ct = inp
                h = dA * h + dBu
                y = jnp.einsum('bdn,bn->bd', h, Ct)
                return (h, y)
            h0 = jnp.zeros((bsz, d, n), u.dtype)
            _, ys = lax.scan(step, h0, (deltaA.transpose(1, 0, 2, 3), deltaBu.transpose(1, 0, 2, 3), C.transpose(1, 0, 2)))
            y = ys.transpose(1, 0, 2)
            return y + u * D
        key = jax.random.key(seed)
        ks = jax.random.split(key, 12)
        x = jax.random.normal(ks[0], (2, 256, D_MODEL), dtype=jnp.float32)
        norm_w = jnp.ones((D_MODEL,), jnp.float32)
        norm_b = jnp.zeros((D_MODEL,), jnp.float32)
        in_proj_w = jax.random.normal(ks[1], (D_MODEL, 2 * D_INNER), jnp.float32) * D_MODEL ** (-0.5)
        conv_w = jax.random.normal(ks[2], (D_INNER, K), jnp.float32) * K ** (-0.5)
        conv_b = jnp.zeros((D_INNER,), jnp.float32)
        x_proj_w = jax.random.normal(ks[3], (D_INNER, DT_RANK + 2 * D_STATE), jnp.float32) * D_INNER ** (-0.5)
        dt_init_std = DT_RANK ** (-0.5)
        dt_proj_w = jax.random.uniform(ks[4], (DT_RANK, D_INNER), jnp.float32, -dt_init_std, dt_init_std)
        dt = jnp.exp(jax.random.uniform(ks[5], (D_INNER,), jnp.float32) * (np.log(0.1) - np.log(0.001)) + np.log(0.001))
        dt_proj_b = dt + jnp.log(-jnp.expm1(-dt))
        A_log = jax.random.normal(ks[6], (D_INNER, D_STATE), jnp.float32)
        D_param = jax.random.normal(ks[7], (D_INNER,), jnp.float32)
        out_proj_w = jax.random.normal(ks[8], (D_INNER, D_MODEL), jnp.float32) * D_INNER ** (-0.5)
        return dict(x=x, norm_w=norm_w, norm_b=norm_b, in_proj_w=in_proj_w, conv_w=conv_w, conv_b=conv_b, x_proj_w=x_proj_w, dt_proj_w=dt_proj_w, dt_proj_b=dt_proj_b, A_log=A_log, D_param=D_param, out_proj_w=out_proj_w)
    _L0_attn_in = _L0_attn_setup()

    def _L0_ffn_setup():
        import jax, jax.numpy as jnp
        import numpy as np
        B, S, H = (8, 1024, 256)
        NAV = 128
        E = 8
        F = 2 * H
        key = jax.random.key(seed)
        ks = jax.random.split(key, 12)

        def w(k, shape, fan_in):
            return jax.random.normal(k, shape, dtype=jnp.float32) / np.sqrt(fan_in)
        return {'hidden_states': jax.random.normal(ks[0], (B, S, H), dtype=jnp.float32), 'Wp1': w(ks[1], (H, NAV), H), 'bp1': jnp.zeros((NAV,), jnp.float32), 'Wp2': w(ks[2], (NAV, E), NAV), 'bp2': jnp.zeros((E,), jnp.float32), 'W1': w(ks[3], (E, H, F), H), 'b1': jnp.zeros((E, F), jnp.float32), 'W2': w(ks[4], (E, F, H), F), 'b2': jnp.zeros((E, H), jnp.float32), 'Wo': w(ks[5], (H, H), H), 'bo': jnp.zeros((H,), jnp.float32)}
    _L0_ffn_in = _L0_ffn_setup()
    _L0_c = _w((lambda *s: np.random.randn(*s).astype(np.float32) * 0.05)(4, 256))
    _L0_wmod = _w((lambda *s: np.random.randn(*s).astype(np.float32) * 0.05)(256, 6 * 256) * 256 ** (-0.5))
    _d = {'L0_attn_x': _L0_attn_in['x'], 'L0_attn_norm_w': _L0_attn_in['norm_w'], 'L0_attn_norm_b': _L0_attn_in['norm_b'], 'L0_attn_in_proj_w': _L0_attn_in['in_proj_w'], 'L0_attn_conv_w': _L0_attn_in['conv_w'], 'L0_attn_conv_b': _L0_attn_in['conv_b'], 'L0_attn_x_proj_w': _L0_attn_in['x_proj_w'], 'L0_attn_dt_proj_w': _L0_attn_in['dt_proj_w'], 'L0_attn_dt_proj_b': _L0_attn_in['dt_proj_b'], 'L0_attn_A_log': _L0_attn_in['A_log'], 'L0_attn_D_param': _L0_attn_in['D_param'], 'L0_attn_out_proj_w': _L0_attn_in['out_proj_w'], 'L0_ffn_Wp1': _L0_ffn_in['Wp1'], 'L0_ffn_bp1': _L0_ffn_in['bp1'], 'L0_ffn_Wp2': _L0_ffn_in['Wp2'], 'L0_ffn_bp2': _L0_ffn_in['bp2'], 'L0_ffn_W1': _L0_ffn_in['W1'], 'L0_ffn_b1': _L0_ffn_in['b1'], 'L0_ffn_W2': _L0_ffn_in['W2'], 'L0_ffn_b2': _L0_ffn_in['b2'], 'L0_ffn_Wo': _L0_ffn_in['Wo'], 'L0_ffn_bo': _L0_ffn_in['bo'], 'L0_c': _L0_c, 'L0_wmod': _L0_wmod}
    _x0 = _d['L0_attn_x']
    _d['L0_attn_x'] = jax.random.normal(jax.random.fold_in(jax.random.key(seed), 1), (4, 1024, 256), dtype=_x0.dtype)
    del _x0
    return _d

def reference(L0_attn_x, L0_attn_norm_w, L0_attn_norm_b, L0_attn_in_proj_w, L0_attn_conv_w, L0_attn_conv_b, L0_attn_x_proj_w, L0_attn_dt_proj_w, L0_attn_dt_proj_b, L0_attn_A_log, L0_attn_D_param, L0_attn_out_proj_w, L0_ffn_Wp1, L0_ffn_bp1, L0_ffn_Wp2, L0_ffn_bp2, L0_ffn_W1, L0_ffn_b1, L0_ffn_W2, L0_ffn_b2, L0_ffn_Wo, L0_ffn_bo, L0_c, L0_wmod):

    def _L0_attn_ref(x, norm_w, norm_b, in_proj_w, conv_w, conv_b, x_proj_w, dt_proj_w, dt_proj_b, A_log, D_param, out_proj_w):
        import jax, jax.numpy as jnp
        import numpy as np
        from jax import lax
        D_MODEL = 256
        D_INNER = 512
        D_STATE = 16
        DT_RANK = 128
        K = 4
        EPS = 1e-05

        def _layer_norm(x, w, b):
            mu = jnp.mean(x, axis=-1, keepdims=True)
            var = jnp.mean(jnp.square(x - mu), axis=-1, keepdims=True)
            return (x - mu) * lax.rsqrt(var + EPS) * w + b

        def _causal_depthwise_conv(x, w, b):
            L = x.shape[1]
            xp = jnp.pad(x, ((0, 0), (K - 1, 0), (0, 0)))
            out = b
            for k in range(K):
                out = out + w[:, k] * xp[:, k:k + L, :]
            return out

        def _selective_scan(u, delta, A, B, C, D):
            deltaA = jnp.exp(jnp.einsum('bld,dn->bldn', delta, A))
            deltaBu = jnp.einsum('bld,bln,bld->bldn', delta, B, u)
            bsz, _, d, n = deltaA.shape

            def step(h, inp):
                dA, dBu, Ct = inp
                h = dA * h + dBu
                y = jnp.einsum('bdn,bn->bd', h, Ct)
                return (h, y)
            h0 = jnp.zeros((bsz, d, n), u.dtype)
            _, ys = lax.scan(step, h0, (deltaA.transpose(1, 0, 2, 3), deltaBu.transpose(1, 0, 2, 3), C.transpose(1, 0, 2)))
            y = ys.transpose(1, 0, 2)
            return y + u * D
        residual = x
        h = _layer_norm(x, norm_w, norm_b)
        xr = h @ in_proj_w
        xs, res = (xr[..., :D_INNER], xr[..., D_INNER:])
        xs = _causal_depthwise_conv(xs, conv_w, conv_b)
        xs = jax.nn.silu(xs)
        A = -jnp.exp(A_log)
        xp = xs @ x_proj_w
        dr = xp[..., :DT_RANK]
        Bm = xp[..., DT_RANK:DT_RANK + D_STATE]
        Cm = xp[..., DT_RANK + D_STATE:]
        delta = jax.nn.softplus(dr @ dt_proj_w + dt_proj_b)
        y = _selective_scan(xs, delta, A, Bm, Cm, D_param)
        y = y * jax.nn.silu(res)
        return y @ out_proj_w + residual

    def _L0_ffn_ref(hidden_states, Wp1, bp1, Wp2, bp2, W1, b1, W2, b2, Wo, bo):
        import jax, jax.numpy as jnp
        import numpy as np
        B, S, H = (8, 1024, 256)
        NAV = 128
        E = 8
        F = 2 * H
        last = hidden_states[:, -1, :]
        logits = jax.nn.gelu(last @ Wp1 + bp1, approximate=False) @ Wp2 + bp2
        action_probs = jax.nn.softmax(logits, axis=-1)
        sel = jnp.argmax(action_probs, axis=-1)
        w1 = W1[sel]
        w2 = W2[sel]
        h = jax.nn.gelu(jnp.einsum('bsh,bhf->bsf', hidden_states, w1) + b1[sel][:, None, :], approximate=False)
        reasoned = jnp.einsum('bsf,bfh->bsh', h, w2) + b2[sel][:, None, :]
        out = reasoned @ Wo + bo
        return hidden_states + 0.3 * out
    x = L0_attn_x
    mod = (_silu(L0_c) @ L0_wmod).reshape(L0_c.shape[0], 6, 1, -1)
    sa, ca, ga, sb, cb, gb = (mod[:, 0], mod[:, 1], mod[:, 2], mod[:, 3], mod[:, 4], mod[:, 5])
    ga = (2 * (ga >= 0) - 1) * jnp.maximum(jnp.abs(ga), 0.25)
    gb = (2 * (gb >= 0) - 1) * jnp.maximum(jnp.abs(gb), 0.25)
    h = _layernorm(x, axis=-1) * (1 + ca) + sa
    x = x + ga * _L0_attn_ref(h, L0_attn_norm_w, L0_attn_norm_b, L0_attn_in_proj_w, L0_attn_conv_w, L0_attn_conv_b, L0_attn_x_proj_w, L0_attn_dt_proj_w, L0_attn_dt_proj_b, L0_attn_A_log, L0_attn_D_param, L0_attn_out_proj_w)
    h = _layernorm(x, axis=-1) * (1 + cb) + sb
    x = x + gb * _L0_ffn_ref(h, L0_ffn_Wp1, L0_ffn_bp1, L0_ffn_Wp2, L0_ffn_bp2, L0_ffn_W1, L0_ffn_b1, L0_ffn_W2, L0_ffn_b2, L0_ffn_Wo, L0_ffn_bo)
    return x

_drawn_inputs = setup_inputs


def setup_inputs(seed=0):
    import zlib

    import numpy as np

    out = dict(_drawn_inputs(seed))
    spreads = {'L0_attn_norm_w': (1.0, 0.2),
     'L0_attn_norm_b': (0.0, 0.386),
     'L0_attn_conv_b': (0.0, 0.478),
     'L0_ffn_bp1': (0.0, 0.1),
     'L0_ffn_bp2': (0.0, 0.1),
     'L0_ffn_b1': (0.0, 0.8),
     'L0_ffn_b2': (0.0, 0.8),
     'L0_ffn_bo': (0.0, 0.8)}
    factors = {'L0_attn_dt_proj_w': 6.599}
    for name, (base, spread) in spreads.items():
        noise = np.random.default_rng([zlib.crc32(name.encode()), seed]).standard_normal(out[name].shape)
        drawn = base * np.exp(spread * noise) if base else spread * noise
        out[name] = jnp.asarray(drawn.astype(out[name].dtype))
    for name, factor in factors.items():
        out[name] = (out[name] * factor).astype(out[name].dtype)
    return out
```

```python
from contextlib import ExitStack

import concourse.bass as bass
from concourse import mybir

F32 = mybir.dt.float32
I32 = mybir.dt.int32
ACT = mybir.ActivationFunctionType
ALU = mybir.AluOpType
AX_X = mybir.AxisListType.X
ds = bass.ds

P = 128
NB, L, D = 4, 1024, 256
DI, NS, R, KC = 512, 16, 128, 4
NE, F = 8, 512
EPS = 1e-5
KD, KI = D // P, DI // P
CH = 256
JC = CH // P
NQ = L // CH
SPQ = NS // NQ
LT = L // P
NM = 8
VEC_LT = [0, 2, 4, 6]
ACT_LT = [1, 3, 5, 7]
NV, NA = len(VEC_LT), len(ACT_LT)
PRE_USES = 9
PRE_FREE = 5
B_FREE = 3
SEL_STEPS = 10


def build(nc, x, norm_w, norm_b, in_proj_w, conv_w, conv_b, x_proj_w, dt_proj_w, dt_proj_b, A_log, D_param,
          out_proj_w, Wp1, bp1, Wp2, bp2, W1, b1, W2, b2, Wo, bo, c, wmod, out):
    ctx = ExitStack()
    with ctx:
        def sb(name, shape, dt=F32):
            return ctx.enter_context(nc.sbuf_tensor(name, shape, dt))

        def pb_(name, shape):
            return ctx.enter_context(nc.psum_tensor(name, shape, F32))

        def sem(name):
            return ctx.enter_context(nc.semaphore(name))

        x_rows = x.rearrange("b l d -> (b l) d")
        out_rows = out.rearrange("b l d -> (b l) d")
        mods_d = nc.dram_tensor("mods_d", (NB, NM * D), F32).ap()
        brow_d = nc.dram_tensor("brow_d", (NB * NS + 1, L), F32).ap()
        hx_d = nc.dram_tensor("hx_d", (NB * L, D), F32).ap()
        y_d = nc.dram_tensor("y_d", (NB * L, DI), F32).ap()
        xs_d = nc.dram_tensor("xs_d", (NB * P, KI, L), F32).ap()
        sres_d = nc.dram_tensor("sres_d", (NB * P, KI, L), F32).ap()

        w_in = sb("w_in", [P, KD, 2 * DI])
        w_x = sb("w_x", [P, KI, R + 2 * NS])
        w_dt = sb("w_dt", [P, DI])
        w_out = sb("w_out", [P, KI, D])
        w_p1 = sb("w_p1", [P, KD, P])
        w_p2 = sb("w_p2", [P, NE])
        w_o = sb("w_o", [P, KD, D])
        w_1 = sb("w_1", [P, KD, F])
        w_2 = sb("w_2", [P, F // P, D])
        b1_c = sb("b1_c", [P, F // P])
        b2_c = sb("b2_c", [P, KD])
        nw_c = sb("nw_c", [P, KD])
        nb_c = sb("nb_c", [P, KD])
        cw_c = sb("cw_c", [P, KI, KC])
        cb_c = sb("cb_c", [P, KI])
        dtb_c = sb("dtb_c", [P, KI])
        D_c = sb("D_c", [P, KI])
        bp1_c = sb("bp1_c", [P, 1])
        bp2_r = sb("bp2_r", [1, NE])
        A_c = sb("A_c", [P, KI, NS])
        c_T = sb("c_T", [P, KD, NB])
        eps_c = sb("eps_c", [P, 1])
        ident = sb("ident", [P, P])
        iota8 = sb("iota8", [1, NE])
        pre_row = sb("pre_row", [P, 3 * D])
        post_row = sb("post_row", [P, 4 * D])
        post_col = sb("post_col", [P, 2, KD])
        delta = sb("delta", [P, 2, KI, L])
        du = sb("du", [P, 2, KI, L])
        C_t = sb("C_t", [P, 2, LT, NS])
        b_bc = sb("b_bc", [P, 2, L])
        h = sb("h", [P, 2, KI, L])
        y = sb("y", [P, LT, DI])
        q = sb("q", [P, 2, DI])
        x_t = sb("x_t", [P, JC, D])
        hm = sb("hm", [P, JC, D])
        hn = sb("hn", [P, JC, D])
        hx = sb("hx", [P, JC, D])
        hnT = sb("hnT", [P, KD, CH])
        xpre = sb("xpre", [P, KI, CH + KC - 1])
        xs = sb("xs", [P, KI, CH])
        sres = sb("sres", [P, KI, CH])
        dr = sb("dr", [P, CH])
        b_T = sb("b_T", [NS, CH])
        lp = sres
        st_p = sb("st_p", [P, JC, 6])
        mv_p = sb("mv_p", [P, JC, 2])
        rs_p = sb("rs_p", [P, 3, JC])
        y_c = sb("y_c", [P, JC, DI])
        yg = sb("yg", [P, KI, CH])
        sres_c = sb("sres_c", [P, KI, CH])
        hx_c = sb("hx_c", [P, JC, D])
        g = sb("g", [P, F // P, CH])
        x1, xh = g[:, 0:JC, :], g[:, JC:2 * JC, :]
        rr = sb("rr", [P, JC, D])
        h2T = sb("h2T", [P, KD, CH])
        r_T = h2T
        st_a = sb("st_a", [P, JC, 6])
        mv_a = sb("mv_a", [P, JC, 2])
        rs_a = sb("rs_a", [P, 3, JC])
        nav = sb("nav", [P, 1])
        sel = sb("sel", [1, 8, NE])
        sel_i = sb("sel_i", [1, 1], I32)

        pA = [pb_(f"pA{i}", [P, L]) for i in range(2)]
        pH = [pb_(f"pH{i}", [P, DI]) for i in range(2)]
        pp = pb_("pp", [P, 512])
        pq = pb_("pq", [P, 512])

        s_wt, s_cT, s_wm, s_id0, s_id = sem("s_wt"), sem("s_cT"), sem("s_wm"), sem("s_id0"), sem("s_id")
        s_cs, s_mod, s_modv, s_modw, s_Aexp, s_const = (sem("s_cs"), sem("s_mod"), sem("s_modv"), sem("s_modw"),
                                                        sem("s_Aexp"), sem("s_const"))
        s_vec0 = sem("s_vec0")
        s_pad = sem("s_pad")
        s_conv0 = sem("s_conv0")
        s_b, s_dbu, s_dA, s_scan, s_hT = sem("s_b"), sem("s_dbu"), sem("s_dA"), sem("s_scan"), sem("s_hT")
        s_yv, s_qa, s_yg = sem("s_yv"), sem("s_qa"), sem("s_yg")
        s_ysp = sem("s_ysp")
        s_prow, s_x, s_pst, s_prs, s_hm, s_hn, s_hx, s_hxd = (sem("s_prow"), sem("s_x"), sem("s_pst"), sem("s_prs"),
                                                              sem("s_hm"), sem("s_hn"), sem("s_hx"), sem("s_hxd"))
        s_pchain, s_hxc = sem("s_pchain"), sem("s_hxc")
        s_pp, s_ppf = sem("s_pp"), sem("s_ppf")
        s_conv, s_xs, s_sres, s_xsd, s_sresd, s_bT, s_bTd = (sem("s_conv"), sem("s_xs"), sem("s_sres"), sem("s_xsd"),
                                                             sem("s_sresd"), sem("s_bT"), sem("s_bTd"))
        s_lp, s_dl, s_du, s_C = sem("s_lp"), sem("s_dl"), sem("s_du"), sem("s_C")
        s_lpc = sem("s_lpc")
        s_qrow, s_wl, s_wf, s_yc, s_xc, s_sc, s_hc = (sem("s_qrow"), sem("s_wl"), sem("s_wf"), sem("s_yc"),
                                                      sem("s_xc"), sem("s_sc"), sem("s_hc"))
        s_pq, s_pqf = sem("s_pq"), sem("s_pqf")
        s_ud, s_gate, s_x1, s_ast, s_ars, s_xh, s_h2, s_rr, s_rrc = (sem("s_ud"), sem("s_gate"), sem("s_x1"),
                                                                     sem("s_ast"), sem("s_ars"), sem("s_xh"),
                                                                     sem("s_h2"), sem("s_rr"), sem("s_rrc"))
        s_achain = sem("s_achain")
        s_nav, s_se, s_schain, s_si, s_ew, s_g, s_rT, s_fin, s_out = (sem("s_nav"), sem("s_se"), sem("s_schain"),
                                                                      sem("s_si"), sem("s_ew"), sem("s_g"),
                                                                      sem("s_rT"), sem("s_fin"), sem("s_out"))
        s_wo = sem("s_wo")
        s_wof = sem("s_wof")

        def wait(eng, s, value):
            if not (isinstance(value, int) and value <= 0):
                eng.wait_ge(s, value)

        def first_q(qq):
            return isinstance(qq, int) and qq == 0

        def sections(eng, quarter, flush, unrolled=()):
            for t in range(NB + 2):
                quarter(t, 0)
                if t in unrolled:
                    for qq in range(1, NQ):
                        quarter(t, qq)
                    continue
                with eng.Fori(1, NQ) as qq:
                    quarter(t, qq)
            flush()

        def has_pre(t):
            return t < NB

        def has_scan(t):
            return 1 <= t <= NB

        def has_a(t):
            return t >= 2

        def has_b(t, qq):
            return t >= 3 or (t == 2 and not first_q(qq))

        def has_tail(t, qq, s):
            if first_q(qq) and s == 0:
                return 2 <= t <= NB + 1
            return has_scan(t)

        def chunk(t, qq):
            return NQ * t + qq

        def slot(t, qq, s):
            return SPQ * (NQ * (t - 1) + qq) + s

        def piece(t, qq):
            return NQ * (t - 2) + qq

        def piece_q(qq):
            return NQ - 1 if first_q(qq) else qq - 1

        def sel_before(t, qq):
            return (t - 2) + (0 if first_q(qq) else 1)

        def b_use(t, qq):
            return 8 * piece(t, qq) - 4 + 2 * sel_before(t, qq)

        def a_use(t, qq):
            return b_use(t, qq) + 4

        def consumed(lt):
            return (s_yv, NV, VEC_LT.index(lt)) if lt in VEC_LT else (s_qa, NA, ACT_LT.index(lt))

        ctx.enter_context(nc.allow_non_contiguous_dma(reason="vectors of a few hundred values, one per partition"))
        block = ctx.enter_context(nc.Block())

        @block.sync
        def _(sp):
            hflat = h[:, :, :, :].rearrange("p a k l -> p (a k l)")
            yflat = y[:, :, :].rearrange("p a k -> p (a k)")
            for kk in range(KD):
                sp.dma_start(c_T[:, kk, :], c[:, kk * P:(kk + 1) * P].rearrange("b p -> p b")).then_inc(s_cT, 16)
            sp.dma_start(yflat[0:NB, 3584:3584 + D], bo[None, :].to_broadcast((NB, D))).then_inc(s_cT, 16)
            sp.dma_start(hflat[:, 0:KD * 6 * D].rearrange("p (k n) -> p k n", k=KD),
                         wmod.rearrange("(k p) n -> p k n", p=P)).then_inc(s_wm, 16)
            for dst, src in (
                (w_in[:, :, :], in_proj_w.rearrange("(k p) n -> p k n", p=P)),
                (w_x[:, :, :], x_proj_w.rearrange("(k p) n -> p k n", p=P)),
                (w_dt[:, :], dt_proj_w),
                (w_p1[:, :, :], Wp1.rearrange("(k p) n -> p k n", p=P)),
                (w_p2[:, :], Wp2),
                (nw_c[:, :], norm_w.rearrange("(k p) -> p k", p=P)),
                (nb_c[:, :], norm_b.rearrange("(k p) -> p k", p=P)),
                (cw_c[:, :, :], conv_w.rearrange("(k p) n -> p k n", p=P)),
                (cb_c[:, :], conv_b.rearrange("(k p) -> p k", p=P)),
                (dtb_c[:, :], dt_proj_b.rearrange("(k p) -> p k", p=P)),
                (D_c[:, :], D_param.rearrange("(k p) -> p k", p=P)),
                (bp1_c[:, :], bp1.rearrange("(p k) -> p k", k=1)),
                (bp2_r[:, :], bp2.rearrange("(p k) -> p k", p=1)),
                (A_c[:, :, :], A_log.rearrange("(k p) n -> p k n", p=P)),
            ):
                sp.dma_start(dst, src).then_inc(s_wt, 16)
            sp.dma_start(brow_d[NB * NS:NB * NS + 1, :], x_rows[0:L // D, :].rearrange("(o a) d -> o (a d)", o=1)
                         ).then_inc(s_pad, 16)
            sp.wait_ge(s_modv, 1)
            sp.dma_start(mods_d, yflat[0:NB, 1536:1536 + NM * D]).then_inc(s_modw, 16)
            sp.wait_ge(s_modw, 16)

            def quarter(t, qq):
                first = first_q(qq)
                if has_pre(t) and first:
                    wait(sp, s_hx, NQ * t)
                    sp.dma_start(pre_row[:, :], mods_d[t:t + 1, 0:3 * D].to_broadcast((P, 3 * D))).then_inc(s_prow, 16)
                for s in range(SPQ):
                    if has_pre(t) and s == 0:
                        k = chunk(t, qq)
                        wait(sp, s_hx, k)
                        sp.dma_start(x_t[:, :, :], x_rows[ds(k * CH, CH), :].rearrange("(j p) d -> p j d", p=P)
                                     ).then_inc(s_x, 16)
                    if has_tail(t, qq, s) and first and s == 0 and t >= 2:
                        for lt in range(LT):
                            if lt in VEC_LT:
                                sp.wait_ge(s_yv, NV * (NS * (t - 1) - 1) + VEC_LT.index(lt) + 1)
                            else:
                                sp.wait_ge(s_yg, NA * (NS * (t - 1) - 1) + ACT_LT.index(lt) + 1)
                            tok = (t - 2) * L + lt * P
                            sp.dma_start(y_d[tok:tok + P, :], y[:, lt, :]).then_inc(s_ysp, 16)
                    if has_a(t) and first and s == 0:
                        m = piece(t, 0)
                        wait(sp, s_rr, m)
                        wait(sp, s_wof, t - 2)
                        wait(sp, s_h2, m)
                        sp.dma_start(post_row[:, :], mods_d[t - 2:t - 1, 2 * D:6 * D].to_broadcast((P, 4 * D))
                                     ).then_inc(s_qrow, 16)
                        sp.dma_start(post_col[:, :, :].rearrange("p c k -> p (c k)"),
                                     mods_d[t - 2, 6 * D:8 * D].rearrange("(n p) -> p n", p=P)
                                     ).then_inc(s_qrow, 16)
                        wait(sp, s_x1, m)
                        sp.dma_start(w_out[:, :, :], out_proj_w.rearrange("(k p) n -> p k n", p=P)).then_inc(s_wl, 16)
                    if has_a(t) and s == 0:
                        m, pq_ = piece(t, qq), piece_q(qq)
                        if first:
                            sp.wait_ge(s_ysp, 16 * LT * (t - 1))
                            sp.wait_ge(s_xsd, 16 * NQ * (t - 1))
                            sp.wait_ge(s_sresd, 16 * NQ * (t - 1))
                            sp.wait_ge(s_hxd, 16 * NQ * (t - 1))
                        wait(sp, s_gate, m)
                        wait(sp, s_x1, m)
                        tok = (t - 2) * L + pq_ * CH
                        sp.dma_start(y_c[:, :, :], y_d[ds(tok, CH), :].rearrange("(j p) d -> p j d", p=P)).then_inc(s_yc, 16)
                        rows = slice((t - 2) * P, (t - 1) * P)
                        sp.dma_start(yg[:, :, :], xs_d[rows, :, ds(pq_ * CH, CH)]).then_inc(s_xc, 16)
                        sp.dma_start(sres_c[:, :, :], sres_d[rows, :, ds(pq_ * CH, CH)]).then_inc(s_sc, 16)
                        sp.dma_start(hx_c[:, :, :], hx_d[ds(tok, CH), :].rearrange("(j p) d -> p j d", p=P)).then_inc(s_hc, 16)
                    if has_pre(t) and s == 1:
                        sp.wait_ge(s_hx, k + 1)
                        sp.dma_start(hx_d[ds(k * CH, CH), :].rearrange("(j p) d -> p j d", p=P), hx[:, :, :]
                                     ).then_inc(s_hxd, 16)
                    if has_b(t, qq) and s == 1:
                        sp.wait_ge(s_fin, piece(t, qq))
                        store(t, qq)
                    if has_a(t) and first and s == 1:
                        sp.dma_start(w_o[:, :, :], Wo.rearrange("(k p) n -> p k n", p=P)).then_inc(s_wo, 16)
                    if has_pre(t) and s == 2:
                        rows = slice(t * P, (t + 1) * P)
                        at = qq * CH
                        sp.wait_ge(s_bT, k + 1)
                        sp.dma_start(brow_d[t * NS:(t + 1) * NS, ds(at, CH)], b_T[:, :]).then_inc(s_bTd, 16)
                        sp.wait_ge(s_xs, k + 1)
                        sp.dma_start(xs_d[rows, :, ds(at, CH)], xs[:, :, :]).then_inc(s_xsd, 16)
                        sp.wait_ge(s_sres, 2 * k + 2)
                        sp.dma_start(sres_d[rows, :, ds(at, CH)], sres[:, :, :]).then_inc(s_sresd, 16)
                    if has_a(t) and first and s == 3:
                        sp.wait_ge(s_si, t - 1)
                        e = sp.value_load(sel_i[0:1, 0:1], min_val=0, max_val=NE - 1)
                        sp.dma_start(w_1[:, :, :], W1[ds(e, 1), :, :].rearrange("e (k p) f -> p (e k) f", p=P)).then_inc(s_ew, 16)
                        sp.dma_start(w_2[:, :, :], W2[ds(e, 1), :, :].rearrange("e (k p) f -> p (e k) f", p=P)).then_inc(s_ew, 16)
                        sp.dma_start(b1_c[:, :], b1[ds(e, 1), :].rearrange("e (k p) -> p (e k)", p=P)).then_inc(s_ew, 16)
                        sp.dma_start(b2_c[:, :], b2[ds(e, 1), :].rearrange("e (k p) -> p (e k)", p=P)).then_inc(s_ew, 16)

            def store(t, qq):
                if first_q(qq):
                    tok = (t - 3) * L + (NQ - 2) * CH
                else:
                    tok = (t - 2) * L + ((qq + (NQ - 2)) % NQ) * CH
                sp.dma_start(out_rows[ds(tok, CH), :].rearrange("(j p) d -> p j d", p=P), rr[:, :, :]).then_inc(s_out, 16)

            sections(sp, quarter, lambda: None, unrolled=(0,))
            sp.wait_ge(s_fin, NB * NQ)
            store(NB + 2, 0)
            sp.wait_ge(s_out, 16 * NB * NQ)

        @block.gpsimd
        def _(gp):
            gp.memset(ident[:, :], 0.0).then_inc(s_id0, 1)
            gp.wait_ge(s_id0, 1)
            gp.affine_select(out=ident[:, :], in_=ident[:, :], compare_op=ALU.not_equal, fill=1.0, base=0,
                             pattern=[[-1, P]], channel_multiplier=1).then_inc(s_id, 1)
            gp.memset(eps_c[:, :], EPS).then_inc(s_const, 1)
            gp.iota(iota8[:, :], pattern=[[1, NE]], base=0, channel_multiplier=0,
                    allow_small_or_imprecise_dtypes=True).then_inc(s_const, 1)

            def quarter(t, qq):
                first = first_q(qq)
                k = chunk(t, qq)
                for s in range(SPQ):
                    for p in range(LT):
                        if has_scan(t) and p % 2 == 0:
                            dt, i = p // 2, slot(t, qq, s)
                            if dt == 0:
                                if first and s == 0:
                                    gp.wait_ge(s_du, NQ * t)
                                gp.wait_ge(s_b, 16 * (i + 1))
                                wait(gp, s_hT, LT * (i - 1))
                            gp.tensor_tensor(h[:, s % 2, dt, :], du[:, (t - 1) % 2, dt, :], b_bc[:, s % 2, :],
                                             ALU.mult).then_inc(s_dbu, 1)
                        if has_tail(t, qq, s) and p in ACT_LT:
                            i, rank = slot(t, qq, s) - 1, ACT_LT.index(p)
                            start = first and s == 1
                            gp.wait_ge(s_qa, NA * i + rank + 1)
                            wait(gp, s_yg, NA * (i - 1) + rank + 1)
                            if start:
                                wait(gp, s_ysp, 16 * LT * (t - 1))
                                gp.tensor_copy(y[:, p, :], q[:, rank % 2, :]).then_inc(s_yg, 1)
                            else:
                                gp.tensor_tensor(y[:, p, :], y[:, p, :], q[:, rank % 2, :], ALU.add).then_inc(s_yg, 1)
                        if has_pre(t) and (s, p) == (0, 7):
                            gp.wait_ge(s_hm, k + 1)
                            wait(gp, s_hxd, 16 * k)
                            for j in range(JC):
                                gp.tensor_tensor(hx[:, j, :], hm[:, j, :], pre_row[:, 2 * D:3 * D], ALU.mult).then_inc(s_hxc, 1)
                            gp.wait_ge(s_hxc, JC * (k + 1))
                            gp.tensor_tensor(hx[:, :, :], hx[:, :, :], x_t[:, :, :], ALU.add).then_inc(s_hx, 1)
                        if has_pre(t) and (s, p) == (3, 4):
                            gp.wait_ge(s_lp, 2 * (k + 1))
                            dd = delta[:, t % 2, :, ds(qq * CH, CH)]
                            gp.tensor_tensor(dd, dd, lp[:, :, :], ALU.add).then_inc(s_dl, 1)
                        if has_pre(t) and (s, p) == (3, 6):
                            gp.wait_ge(s_dl, k + 1)
                            gp.tensor_tensor(du[:, t % 2, :, ds(qq * CH, CH)], delta[:, t % 2, :, ds(qq * CH, CH)],
                                             xs[:, :, :], ALU.mult).then_inc(s_du, 1)
                        if has_a(t) and first and (s, p) == (1, 0):
                            gp.wait_ge(s_qrow, 32 * (t - 1))
                            gp.wait_ge(s_wl, 16 * (t - 1))
                            for kk in range(KI):
                                gp.tensor_tensor(w_out[:, kk, :], w_out[:, kk, :], post_row[:, 0:D], ALU.mult).then_inc(s_wf, 1)
                        if has_a(t) and (s, p) == (1, 7):
                            m = piece(t, qq)
                            gp.wait_ge(s_ud, KI * (m + 1))
                            gp.wait_ge(s_sc, 16 * (m + 1))
                            gp.tensor_tensor(yg[:, :, :], yg[:, :, :], sres_c[:, :, :], ALU.mult).then_inc(s_gate, 1)
                        if has_a(t) and (s, p) == (2, 6):
                            m = piece(t, qq)
                            gp.wait_ge(s_xh, m + 1)
                            wait(gp, s_out, 16 * m)
                            for j in range(JC):
                                gp.tensor_tensor(rr[:, j, :], xh[:, j, :], post_row[:, D:2 * D], ALU.mult).then_inc(s_rrc, 1)
                            gp.wait_ge(s_rrc, (JC + 1) * m + JC)
                            gp.tensor_tensor(rr[:, :, :], rr[:, :, :], x1[:, :, :], ALU.add).then_inc(s_rrc, 1)
                            gp.wait_ge(s_rrc, (JC + 1) * (m + 1))
                            for j in range(JC):
                                last = gp.tensor_tensor(rr[:, j, :], rr[:, j, :], post_row[:, 2 * D:3 * D], ALU.add)
                            last.then_inc(s_rr, 1)
                        if has_a(t) and first and (s, p) == (3, 1):
                            gp.wait_ge(s_wo, 16 * (t - 1))
                            for kk in range(KD):
                                last = gp.tensor_tensor(w_o[:, kk, :], w_o[:, kk, :], post_row[:, 3 * D:4 * D], ALU.mult)
                            last.then_inc(s_wof, 1)

            sections(gp, quarter, lambda: None)
            gp.wait_ge(s_b, 16 * (NB * NS + 1))

        @block.scalar
        def _(act):
            act.wait_ge(s_cT, 16 * (KD + 1))
            nc.scalar.activation(c_T[:, :, :], c_T[:, :, :], ACT.Silu).then_inc(s_cs, 1)
            act.wait_ge(s_wt, 16 * 14)
            nc.scalar.activation(A_c[:, :, :], A_c[:, :, :], ACT.Exp).then_inc(s_Aexp, 1)
            act.wait_ge(s_Aexp, 1)
            nc.scalar.mul(A_c[:, :, :], A_c[:, :, :], -1.0).then_inc(s_Aexp, 1)
            act.wait_ge(s_Aexp, 2)
            act.wait_ge(s_const, 2)

            def rsqrt_guess(mv, rs, s_in, s_out_, n):
                act.wait_ge(s_in, n + 1)
                nc.scalar.activation(rs[:, 0, :], mv[:, :, 1], ACT.Ln, bias=eps_c[:, :]).then_inc(s_out_, 1)
                act.wait_ge(s_out_, 2 * n + 1)
                nc.scalar.activation(rs[:, 1, :], rs[:, 0, :], ACT.Exp, scale=-0.5).then_inc(s_out_, 1)

            def fetch_b(i, s):
                wait(act, s_dbu, KI * (i - 1))
                act.dma_start(b_bc[:, s % 2, :], brow_d[ds(i, 1), :].to_broadcast((P, L))).then_inc(s_b, 16)

            def quarter(t, qq):
                first = first_q(qq)
                k = chunk(t, qq)
                for s in range(SPQ):
                    for p in range(LT):
                        if has_scan(t) and p % 2 == 0:
                            dt, i = p // 2, slot(t, qq, s)
                            if first and s == 0 and dt == 0:
                                act.wait_ge(s_dl, NQ * t)
                                if t == 1:
                                    act.wait_ge(s_bTd, 16 * NQ)
                                    fetch_b(0, 0)
                            if dt == 3:
                                if s == SPQ - 1:
                                    act.wait_ge(s_bTd, 16 * (chunk(t, qq) + 1) if has_pre(t) else 16 * NQ * NB)
                                    if t == NB:
                                        act.wait_ge(s_pad, 16)
                                fetch_b(i + 1, s + 1)
                            wait(act, s_scan, KI * i + dt - 1)
                            nc.scalar.activation(pA[dt % 2][:, :], delta[:, (t - 1) % 2, dt, :], ACT.Exp,
                                                 scale=A_c[:, dt, ds(SPQ * qq + s, 1)]).then_inc(s_dA, 1)
                        if has_tail(t, qq, s) and p in ACT_LT:
                            i, rank = slot(t, qq, s) - 1, ACT_LT.index(p)
                            bb = (t - 2) if first and s == 0 else (t - 1)
                            n = NS - 1 if first and s == 0 else SPQ * qq + s - 1
                            if first and s == 1 and rank == 0:
                                act.wait_ge(s_C, NQ * t)
                            act.wait_ge(s_hT, LT * i + p + 1)
                            wait(act, s_yg, NA * i + rank - 1)
                            nc.scalar.activation(q[:, rank % 2, :], pH[p % 2][:, :], ACT.Copy,
                                                 scale=C_t[:, bb % 2, p, ds(n, 1)]).then_inc(s_qa, 1)
                        if has_pre(t):
                            base = PRE_USES * k
                            if (s, p) == (0, 1):
                                rsqrt_guess(mv_p, rs_p, s_pst, s_prs, 2 * k)
                            if (s, p) == (0, 3):
                                rsqrt_guess(mv_p, rs_p, s_pst, s_prs, 2 * k + 1)
                            if (s, p) == (0, 7):
                                act.wait_ge(s_pp, base + 1)
                                for kk in range(KD):
                                    last = nc.scalar.activation(hnT[:, kk, :], pp[:, kk * CH:(kk + 1) * CH], ACT.Identity,
                                                                scale=nw_c[:, kk:kk + 1], bias=nb_c[:, kk:kk + 1])
                                last.then_inc(s_ppf, 1)
                            if (s, p) in ((1, 1), (1, 3)):
                                u = (p - 1) // 2
                                act.wait_ge(s_pp, base + 2 + u)
                                if u == 0:
                                    act.wait_ge(s_conv0, k + 1)
                                    wait(act, s_du, k)
                                    wait(act, s_xsd, 16 * k)
                                for kk in (2 * u, 2 * u + 1):
                                    half = pp[:, (kk % 2) * CH:(kk % 2 + 1) * CH]
                                    nc.scalar.copy(xpre[:, kk, KC - 1:], half)
                                    last = nc.scalar.activation(xs[:, kk, :], half, ACT.Identity,
                                                                scale=cw_c[:, kk, KC - 1:KC], bias=cb_c[:, kk:kk + 1])
                                last.then_inc(s_ppf, 1)
                            if (s, p) == (2, 0):
                                act.wait_ge(s_conv, (KC - 1) * KI * (k + 1))
                                nc.scalar.activation(xs[:, :, :], xs[:, :, :], ACT.Silu).then_inc(s_xs, 1)
                            if (s, p) in ((2, 0), (2, 1)):
                                act.wait_ge(s_pp, base + 4 + p)
                                if p == 0:
                                    wait(act, s_dl, k)
                                nc.scalar.activation(sres[:, 2 * p:2 * p + 2, :],
                                                     pp[:, :].rearrange("p (a c) -> p a c", a=2), ACT.Silu).then_inc(s_sres, 1)
                            if (s, p) == (2, 3):
                                act.wait_ge(s_pp, base + 6)
                                wait(act, s_bTd, 16 * k)
                                nc.scalar.copy(dr[:, :], pp[:, 0:CH])
                                nc.scalar.copy(b_T[:, :], pp[0:NS, CH:2 * CH]).then_inc(s_bT, 1)
                            if (s, p) in ((2, 7), (3, 1)):
                                u = 0 if s == 2 else 1
                                act.wait_ge(s_pp, base + 8 + u)
                                if u == 0:
                                    act.wait_ge(s_sresd, 16 * (k + 1))
                                    if first and t >= 2:
                                        act.wait_ge(s_dA, KI * NS * (t - 1))
                                for kk in (2 * u, 2 * u + 1):
                                    half = pp[:, (kk % 2) * CH:(kk % 2 + 1) * CH]
                                    nc.scalar.activation(lp[:, kk, :], half, ACT.Abs, bias=dtb_c[:, kk:kk + 1])
                                    last = nc.scalar.activation(delta[:, t % 2, kk, ds(qq * CH, CH)], half, ACT.Relu,
                                                                bias=dtb_c[:, kk:kk + 1])
                                last.then_inc(s_ppf, 1)
                            if (s, p) == (3, 3):
                                act.wait_ge(s_ppf, PRE_FREE * k + 5)
                                nc.scalar.activation(lp[:, :, :], lp[:, :, :], ACT.Exp, scale=-1.0).then_inc(s_lp, 1)
                                act.wait_ge(s_lp, 2 * k + 1)
                                nc.scalar.activation(lp[:, :, :], lp[:, :, :], ACT.Ln, bias=1.0).then_inc(s_lp, 1)
                        if has_b(t, qq) and (s, p) == (0, 7):
                            for u in range(2):
                                act.wait_ge(s_pq, b_use(t, qq) + 1 + u)
                                if u == 0:
                                    act.wait_ge(s_ew, 64 * (t - 2 if first else t - 1))
                                    act.wait_ge(s_rr, piece(t, qq))
                                for kk in (2 * u, 2 * u + 1):
                                    last = nc.scalar.activation(g[:, kk, :], pq[:, (kk % 2) * CH:(kk % 2 + 1) * CH], ACT.Gelu,
                                                                bias=b1_c[:, kk:kk + 1])
                                last.then_inc(s_pqf, 1)
                        if has_b(t, qq) and (s, p) == (1, 1):
                            act.wait_ge(s_pq, b_use(t, qq) + 3)
                            for kk in range(KD):
                                last = nc.scalar.activation(r_T[:, kk, :], pq[:, kk * CH:(kk + 1) * CH], ACT.Identity,
                                                            bias=b2_c[:, kk:kk + 1])
                            last.then_inc(s_pqf, 1)
                        if has_a(t):
                            m = piece(t, qq)
                            if (s, p) == (2, 3):
                                rsqrt_guess(mv_a, rs_a, s_ast, s_ars, m)
                            if (s, p) == (2, 7):
                                act.wait_ge(s_pq, a_use(t, qq) + 4)
                                if first:
                                    act.wait_ge(s_qrow, 32 * (t - 1))
                                for kk in range(KD):
                                    last = nc.scalar.activation(h2T[:, kk, :], pq[:, kk * CH:(kk + 1) * CH], ACT.Identity,
                                                                scale=post_col[:, 0, kk:kk + 1], bias=post_col[:, 1, kk:kk + 1])
                                last.then_inc(s_h2, 1)
                            if first and (s, p) == (3, 0):
                                act.wait_ge(s_pq, a_use(t, qq) + 5)
                                nc.scalar.activation(nav[:, :], pq[:, 0:1], ACT.Gelu, bias=bp1_c[:, :]).then_inc(s_nav, 1)
                            if first and (s, p) == (3, 3):
                                act.wait_ge(s_schain, SEL_STEPS * (t - 2) + 3)
                                nc.scalar.activation(sel[:, 2, :], sel[:, 1, :], ACT.Exp, accum_out=sel[:, 3, 0:1]
                                                     ).then_inc(s_se, 1)

            def flush():
                t, qq = NB + 2, 0
                act.wait_ge(s_rr, NB * NQ)
                for u in range(2):
                    act.wait_ge(s_pq, b_use(t, qq) + 1 + u)
                    for kk in (2 * u, 2 * u + 1):
                        last = nc.scalar.activation(g[:, kk, :], pq[:, (kk % 2) * CH:(kk % 2 + 1) * CH], ACT.Gelu,
                                                    bias=b1_c[:, kk:kk + 1])
                    last.then_inc(s_pqf, 1)
                act.wait_ge(s_pq, b_use(t, qq) + 3)
                for kk in range(KD):
                    last = nc.scalar.activation(r_T[:, kk, :], pq[:, kk * CH:(kk + 1) * CH], ACT.Identity,
                                                bias=b2_c[:, kk:kk + 1])
                last.then_inc(s_pqf, 1)

            sections(act, quarter, flush)

        @block.vector
        def _(dve):
            yflat = y[:, :, :].rearrange("p a k -> p (a k)")
            steps = [0]
            dve.wait_ge(s_wt, 16 * 14)

            def link(ins):
                steps[0] += 1
                ins.then_inc(s_vec0, 1)
                dve.wait_ge(s_vec0, steps[0])

            def mod(i):
                return yflat[0:NB, i * D:(i + 1) * D]

            def keep(i):
                return yflat[0:NB, (6 + i) * D:(7 + i) * D]
            bo4 = yflat[0:NB, 3584:3584 + D]
            tmp = yflat[0:NB, 3840:3840 + D]
            for i in range(3):
                dve.wait_ge(s_mod, i + 1)
                link(nc.vector.tensor_copy(yflat[0:NB, i * 512:(i + 1) * 512], (pp, pq, pH[0])[i][0:NB, :]))
            dve.wait_ge(s_cT, 16 * (KD + 1))
            link(nc.vector.tensor_scalar(keep(0), mod(1), 1.0, None, ALU.add))
            link(nc.vector.tensor_copy(keep(1), mod(0)))
            for gate, dst in ((2, 2), (5, 5)):
                link(nc.vector.tensor_scalar(tmp, mod(gate), 0.0, 2.0, ALU.is_ge, ALU.mult))
                link(nc.vector.tensor_scalar(tmp, tmp, -1.0, None, ALU.add))
                link(nc.vector.scalar_tensor_tensor(keep(dst), mod(gate), -1.0, mod(gate), ALU.mult, ALU.max))
                link(nc.vector.scalar_tensor_tensor(keep(dst), keep(dst), 0.25, tmp, ALU.max, ALU.mult))
            link(nc.vector.tensor_scalar(keep(6), mod(4), 1.0, None, ALU.add))
            link(nc.vector.tensor_copy(keep(7), mod(3)))
            link(nc.vector.tensor_tensor(keep(3), keep(5), keep(6), ALU.mult))
            link(nc.vector.scalar_tensor_tensor(keep(4), bo4, 0.3, mod(3), ALU.mult, ALU.add))
            link(nc.vector.tensor_tensor(keep(4), keep(4), keep(5), ALU.mult))
            nc.vector.tensor_scalar(keep(5), keep(5), 0.3, None, ALU.mult).then_inc(s_modv, 1)

            def stats(src, st, mv, rs, s_chain, base, s_done):
                for j in range(JC):
                    last = nc.vector.bn_stats(st[:, j, :], src[:, j, :])
                last.then_inc(s_chain, 1)
                dve.wait_ge(s_chain, base + 1)
                nc.vector.memset(rs[:, 2, :], 0.0)
                for j in range(JC):
                    last = nc.vector.bn_aggr(mv[:, j, :], st[:, j, :])
                last.then_inc(s_done, 1)

            def refine(mv, rs, s_chain, base):
                nc.vector.tensor_tensor(rs[:, 2, :], rs[:, 1, :], rs[:, 1, :], ALU.mult).then_inc(s_chain, 1)
                dve.wait_ge(s_chain, base + 1)
                nc.vector.scalar_tensor_tensor(rs[:, 2, :], mv[:, :, 1], EPS, rs[:, 2, :], ALU.add, ALU.mult).then_inc(s_chain, 1)
                dve.wait_ge(s_chain, base + 2)
                nc.vector.tensor_scalar(rs[:, 2, :], rs[:, 2, :], -0.5, 1.5, ALU.mult, ALU.add).then_inc(s_chain, 1)
                dve.wait_ge(s_chain, base + 3)
                nc.vector.tensor_tensor(rs[:, 1, :], rs[:, 1, :], rs[:, 2, :], ALU.mult).then_inc(s_chain, 1)
                dve.wait_ge(s_chain, base + 4)

            PCH = 12
            ACH = 5

            def quarter(t, qq):
                first = first_q(qq)
                k = chunk(t, qq)
                for s in range(SPQ):
                    for p in range(LT):
                        if has_scan(t) and p % 2 == 0:
                            dt, i = p // 2, slot(t, qq, s)
                            dve.wait_ge(s_dA, KI * i + dt + 1)
                            dve.wait_ge(s_dbu, KI * i + dt + 1)
                            nc.vector.tensor_tensor_scan(h[:, s % 2, dt, :], pA[dt % 2][:, :], h[:, s % 2, dt, :], 0.0,
                                                         ALU.mult, ALU.add).then_inc(s_scan, 1)
                        if has_tail(t, qq, s) and p in VEC_LT:
                            i, rank = slot(t, qq, s) - 1, VEC_LT.index(p)
                            bb = (t - 2) if first and s == 0 else (t - 1)
                            n = NS - 1 if first and s == 0 else SPQ * qq + s - 1
                            scale = C_t[:, bb % 2, p, ds(n, 1)]
                            dve.wait_ge(s_hT, LT * i + p + 1)
                            wait(dve, s_yv, NV * (i - 1) + rank + 1)
                            if first and s == 1:
                                wait(dve, s_ysp, 16 * LT * (t - 1))
                                nc.vector.tensor_scalar(y[:, p, :], pH[p % 2][:, :], scale, None, ALU.mult).then_inc(s_yv, 1)
                            else:
                                nc.vector.scalar_tensor_tensor(y[:, p, :], pH[p % 2][:, :], scale, y[:, p, :],
                                                               ALU.mult, ALU.add).then_inc(s_yv, 1)
                        if has_pre(t):
                            base = PCH * k
                            if (s, p) == (0, 0):
                                dve.wait_ge(s_x, 16 * (k + 1))
                                stats(x_t, st_p, mv_p, rs_p, s_pchain, base, s_pst)
                            if (s, p) == (0, 2):
                                dve.wait_ge(s_prs, 4 * k + 2)
                                refine(mv_p, rs_p, s_pchain, base + 1)
                                if first:
                                    dve.wait_ge(s_prow, 16 * (t + 1))
                                wait(dve, s_hx, k)
                                for j in range(JC):
                                    last = nc.vector.tensor_scalar(hm[:, j, :], x_t[:, j, :], mv_p[:, j, 0:1],
                                                                   rs_p[:, 1, j:j + 1], ALU.subtract, ALU.mult)
                                last.then_inc(s_pchain, 1)
                                dve.wait_ge(s_pchain, base + 6)
                                for j in range(JC):
                                    last = nc.vector.tensor_tensor(hm[:, j, :], hm[:, j, :], pre_row[:, 0:D], ALU.mult)
                                last.then_inc(s_pchain, 1)
                                dve.wait_ge(s_pchain, base + 7)
                                for j in range(JC):
                                    last = nc.vector.tensor_tensor(hm[:, j, :], hm[:, j, :], pre_row[:, D:2 * D], ALU.add)
                                last.then_inc(s_hm, 1)
                                dve.wait_ge(s_hm, k + 1)
                                stats(hm, st_p, mv_p, rs_p, s_pchain, base + 7, s_pst)
                            if (s, p) == (0, 4):
                                dve.wait_ge(s_prs, 4 * k + 4)
                                refine(mv_p, rs_p, s_pchain, base + 8)
                                wait(dve, s_pp, PRE_USES * (k - 1) + 1)
                                for j in range(JC):
                                    last = nc.vector.tensor_scalar(hn[:, j, :], hm[:, j, :], mv_p[:, j, 0:1],
                                                                   rs_p[:, 1, j:j + 1], ALU.subtract, ALU.mult)
                                last.then_inc(s_hn, 1)
                            if (s, p) == (0, 6):
                                if first:
                                    wait(dve, s_conv, (KC - 1) * KI * k)
                                    nc.vector.memset(xpre[:, :, 0:KC - 1], 0.0).then_inc(s_conv0, 1)
                                else:
                                    wait(dve, s_conv, (KC - 1) * KI * k)
                                    nc.vector.tensor_copy(xpre[:, :, 0:KC - 1], xpre[:, :, CH:CH + KC - 1]).then_inc(s_conv0, 1)
                            if (s, p) in ((1, 4), (1, 5), (1, 6)):
                                tap = p - 4
                                for kk in range(KI):
                                    if tap == 0:
                                        dve.wait_ge(s_ppf, PRE_FREE * k + 2 + kk // 2)
                                    else:
                                        dve.wait_ge(s_conv, (KC - 1) * KI * k + KI * (tap - 1) + kk + 1)
                                    nc.vector.scalar_tensor_tensor(xs[:, kk, :], xpre[:, kk, tap:tap + CH],
                                                                   cw_c[:, kk, tap:tap + 1], xs[:, kk, :],
                                                                   ALU.mult, ALU.add).then_inc(s_conv, 1)
                            if (s, p) == (2, 6):
                                dve.wait_ge(s_pp, PRE_USES * k + 7)
                                if first and t >= 2:
                                    dve.wait_ge(s_qa, NA * NS * (t - 1))
                                nc.vector.tensor_copy(C_t[:, t % 2, ds(JC * qq, JC), :],
                                                      pp[:, 0:JC * NS].rearrange("p (j n) -> p j n", j=JC)).then_inc(s_C, 1)
                        if has_b(t, qq) and (s, p) == (1, 3):
                            dve.wait_ge(s_pq, b_use(t, qq) + 4)
                            dve.wait_ge(s_rr, piece(t, qq))
                            nc.vector.tensor_tensor(rr[:, :, :], rr[:, :, :], pq[:, :].rearrange("p (j d) -> p j d", j=JC),
                                                    ALU.add).then_inc(s_fin, 1)
                        if has_a(t):
                            m = piece(t, qq)
                            if (s, p) in ((1, 4), (1, 6)):
                                u = (p - 4) // 2
                                dve.wait_ge(s_pq, a_use(t, qq) + 1 + u)
                                dve.wait_ge(s_xc, 16 * (m + 1))
                                for kk in (2 * u, 2 * u + 1):
                                    nc.vector.scalar_tensor_tensor(yg[:, kk, :], yg[:, kk, :], D_c[:, kk:kk + 1],
                                                                   pq[:, (kk % 2) * CH:(kk % 2 + 1) * CH],
                                                                   ALU.mult, ALU.add).then_inc(s_ud, 1)
                            if (s, p) == (2, 2):
                                dve.wait_ge(s_pq, a_use(t, qq) + 3)
                                dve.wait_ge(s_hc, 16 * (m + 1))
                                wait(dve, s_rr, m)
                                nc.vector.tensor_tensor(x1[:, :, :], hx_c[:, :, :],
                                                        pq[:, :].rearrange("p (j d) -> p j d", j=JC), ALU.add).then_inc(s_x1, 1)
                                dve.wait_ge(s_x1, m + 1)
                                stats(x1, st_a, mv_a, rs_a, s_achain, ACH * m, s_ast)
                            if (s, p) == (2, 4):
                                dve.wait_ge(s_ars, 2 * m + 2)
                                refine(mv_a, rs_a, s_achain, ACH * m + 1)
                                wait(dve, s_h2, m)
                                for j in range(JC):
                                    last = nc.vector.tensor_scalar(xh[:, j, :], x1[:, j, :], mv_a[:, j, 0:1],
                                                                   rs_a[:, 1, j:j + 1], ALU.subtract, ALU.mult)
                                last.then_inc(s_xh, 1)
                            if first and (s, p) == (3, 2):
                                cbase = SEL_STEPS * (t - 2)
                                dve.wait_ge(s_pq, a_use(t, qq) + 6)
                                nc.vector.tensor_tensor(sel[:, 0, :], pq[0:1, 0:NE], bp2_r[:, :], ALU.add).then_inc(s_schain, 1)
                                dve.wait_ge(s_schain, cbase + 1)
                                nc.vector.reduce_max(sel[:, 3, 1:2], sel[:, 0, :], AX_X).then_inc(s_schain, 1)
                                dve.wait_ge(s_schain, cbase + 2)
                                nc.vector.tensor_scalar(sel[:, 1, :], sel[:, 0, :], sel[:, 3, 1:2], None, ALU.subtract
                                                        ).then_inc(s_schain, 1)
                            if first and (s, p) == (3, 4):
                                cbase = SEL_STEPS * (t - 2)
                                dve.wait_ge(s_se, t - 1)
                                nc.vector.reciprocal(sel[:, 3, 2:3], sel[:, 3, 0:1]).then_inc(s_schain, 1)
                                dve.wait_ge(s_schain, cbase + 4)
                                nc.vector.tensor_scalar(sel[:, 4, :], sel[:, 2, :], sel[:, 3, 2:3], None, ALU.mult
                                                        ).then_inc(s_schain, 1)
                                dve.wait_ge(s_schain, cbase + 5)
                                nc.vector.reduce_max(sel[:, 3, 3:4], sel[:, 4, :], AX_X).then_inc(s_schain, 1)
                                dve.wait_ge(s_schain, cbase + 6)
                                nc.vector.tensor_scalar(sel[:, 5, :], sel[:, 4, :], sel[:, 3, 3:4], None, ALU.is_ge
                                                        ).then_inc(s_schain, 1)
                                dve.wait_ge(s_schain, cbase + 7)
                                nc.vector.scalar_tensor_tensor(sel[:, 6, :], iota8[:, :], -float(NE), sel[:, 5, :],
                                                               ALU.add, ALU.mult).then_inc(s_schain, 1)
                                dve.wait_ge(s_schain, cbase + 8)
                                nc.vector.tensor_reduce(sel[:, 3, 4:5], sel[:, 6, :], AX_X, ALU.min).then_inc(s_schain, 1)
                                dve.wait_ge(s_schain, cbase + 9)
                                nc.vector.tensor_scalar(sel[:, 3, 5:6], sel[:, 3, 4:5], float(NE), None, ALU.add).then_inc(s_schain, 1)
                                dve.wait_ge(s_schain, cbase + 10)
                                nc.vector.tensor_copy(sel_i[:, :], sel[:, 3, 5:6]).then_inc(s_si, 1)

            def flush():
                t, qq = NB + 2, 0
                dve.wait_ge(s_pq, b_use(t, qq) + 4)
                dve.wait_ge(s_rr, NB * NQ)
                nc.vector.tensor_tensor(rr[:, :, :], rr[:, :, :], pq[:, :].rearrange("p (j d) -> p j d", j=JC),
                                        ALU.add).then_inc(s_fin, 1)

            sections(dve, quarter, flush)

        @block.tensor
        def _(pe):
            hflat = h[:, :, :, :].rearrange("p a k l -> p (a k l)")
            wm = hflat[:, 0:KD * 6 * D].rearrange("p (k n) -> p k n", k=KD)
            pe.wait_ge(s_cs, 1)
            pe.wait_ge(s_wm, 16)
            for i, bank in enumerate((pp, pq, pH[0])):
                for kk in range(KD):
                    last = nc.tensor.matmul(bank[0:NB, :], c_T[:, kk, :], wm[:, kk, i * 512:(i + 1) * 512],
                                            start=(kk == 0), stop=(kk == KD - 1))
                last.then_inc(s_mod, 1)
            pe.wait_ge(s_modv, 1)
            pe.wait_ge(s_id, 1)
            pe.wait_ge(s_wt, 16 * 14)

            def expert_up(t, qq, u):
                if u == 0:
                    pe.wait_ge(s_h2, piece(t, qq))
                else:
                    pe.wait_ge(s_pqf, B_FREE * (piece(t, qq) - 1) + 1)
                for kk in (2 * u, 2 * u + 1):
                    for kd in range(KD):
                        last = nc.tensor.matmul(pq[:, (kk % 2) * CH:(kk % 2 + 1) * CH], w_1[:, kd, kk * P:(kk + 1) * P],
                                                h2T[:, kd, :], start=(kd == 0), stop=(kd == KD - 1))
                last.then_inc(s_pq, 1)

            def expert_down(t, qq):
                pe.wait_ge(s_pqf, B_FREE * (piece(t, qq) - 1) + 2)
                for kd in range(KD):
                    for kk in range(F // P):
                        last = nc.tensor.matmul(pq[:, kd * CH:(kd + 1) * CH], w_2[:, kk, kd * P:(kd + 1) * P], g[:, kk, :],
                                                start=(kk == 0), stop=(kk == F // P - 1))
                last.then_inc(s_pq, 1)

            def expert_out(t, qq):
                pe.wait_ge(s_pqf, B_FREE * (piece(t, qq) - 1) + 3)
                for j in range(JC):
                    for kd in range(KD):
                        last = nc.tensor.matmul(pq[:, j * D:(j + 1) * D], r_T[:, kd, j * P:(j + 1) * P], w_o[:, kd, :],
                                                start=(kd == 0), stop=(kd == KD - 1))
                last.then_inc(s_pq, 1)

            def quarter(t, qq):
                first = first_q(qq)
                k = chunk(t, qq)
                for s in range(SPQ):
                    for p in range(LT):
                        if has_tail(t, qq, s):
                            i = slot(t, qq, s) - 1
                            if p == 0:
                                pe.wait_ge(s_scan, KI * (i + 1))
                            prev, n_, rank = consumed((p - 2) % LT)
                            wait(pe, prev, n_ * (i if p >= 2 else i - 1) + rank + 1)
                            for dt in range(KI):
                                last = nc.tensor.transpose(pH[p % 2][:, dt * P:(dt + 1) * P],
                                                           h[:, (s + 1) % 2, dt, p * P:(p + 1) * P], ident[:, :])
                            last.then_inc(s_hT, 1)
                        if has_pre(t):
                            base = PRE_USES * k
                            if (s, p) == (0, 5):
                                pe.wait_ge(s_hn, k + 1)
                                wait(pe, s_ppf, PRE_FREE * k)
                                for kk in range(KD):
                                    for j in range(JC):
                                        last = nc.tensor.transpose(pp[:, kk * CH + j * P:kk * CH + (j + 1) * P],
                                                                   hn[:, j, kk * P:(kk + 1) * P], ident[:, :])
                                last.then_inc(s_pp, 1)
                            if (s, p) in ((1, 0), (1, 2), (1, 7), (2, 1)):
                                u = {(1, 0): 0, (1, 2): 1, (1, 7): 2, (2, 1): 3}[s, p]
                                if u < 3:
                                    pe.wait_ge(s_ppf, PRE_FREE * k + 1 + u)
                                else:
                                    pe.wait_ge(s_sres, 2 * k + 1)
                                for mt in (2 * u, 2 * u + 1):
                                    for kk in range(KD):
                                        last = nc.tensor.matmul(pp[:, (mt % 2) * CH:(mt % 2 + 1) * CH],
                                                                w_in[:, kk, mt * P:(mt + 1) * P], hnT[:, kk, :],
                                                                start=(kk == 0), stop=(kk == KD - 1))
                                last.then_inc(s_pp, 1)
                            if (s, p) == (2, 2):
                                pe.wait_ge(s_xs, k + 1)
                                pe.wait_ge(s_sres, 2 * k + 2)
                                for kk in range(KI):
                                    nc.tensor.matmul(pp[:, 0:CH], w_x[:, kk, 0:R], xs[:, kk, :],
                                                     start=(kk == 0), stop=(kk == KI - 1))
                                for kk in range(KI):
                                    last = nc.tensor.matmul(pp[0:NS, CH:2 * CH], w_x[:, kk, R:R + NS], xs[:, kk, :],
                                                            start=(kk == 0), stop=(kk == KI - 1))
                                last.then_inc(s_pp, 1)
                            if (s, p) == (2, 4):
                                pe.wait_ge(s_bT, k + 1)
                                for j in range(JC):
                                    for kk in range(KI):
                                        last = nc.tensor.matmul(pp[:, j * NS:(j + 1) * NS], xs[:, kk, j * P:(j + 1) * P],
                                                                w_x[:, kk, R + NS:R + 2 * NS],
                                                                start=(kk == 0), stop=(kk == KI - 1))
                                last.then_inc(s_pp, 1)
                            if (s, p) in ((2, 7), (3, 0)):
                                u = 0 if s == 2 else 1
                                if u == 0:
                                    pe.wait_ge(s_C, k + 1)
                                else:
                                    pe.wait_ge(s_ppf, PRE_FREE * k + 4)
                                for kk in (2 * u, 2 * u + 1):
                                    last = nc.tensor.matmul(pp[:, (kk % 2) * CH:(kk % 2 + 1) * CH],
                                                            w_dt[:, kk * P:(kk + 1) * P], dr[:, :], start=True, stop=True)
                                last.then_inc(s_pp, 1)
                        if has_b(t, qq):
                            if (s, p) == (0, 5):
                                pe.wait_ge(s_ew, 64 * (t - 2 if first else t - 1))
                                expert_up(t, qq, 0)
                            if (s, p) == (0, 7):
                                expert_up(t, qq, 1)
                            if (s, p) == (1, 0):
                                expert_down(t, qq)
                            if (s, p) == (1, 2):
                                if not first:
                                    pe.wait_ge(s_wof, t - 1)
                                expert_out(t, qq)
                        if has_a(t):
                            use, m = a_use(t, qq), piece(t, qq)
                            if (s, p) in ((1, 3), (1, 5)):
                                u = (p - 3) // 2
                                if u == 0:
                                    pe.wait_ge(s_yc, 16 * (m + 1))
                                    wait(pe, s_fin, m)
                                else:
                                    pe.wait_ge(s_ud, KI * m + 2)
                                for kk in (2 * u, 2 * u + 1):
                                    for j in range(JC):
                                        last = nc.tensor.transpose(pq[:, (kk % 2) * CH + j * P:(kk % 2) * CH + (j + 1) * P],
                                                                   y_c[:, j, kk * P:(kk + 1) * P], ident[:, :])
                                last.then_inc(s_pq, 1)
                            if (s, p) == (2, 1):
                                pe.wait_ge(s_gate, m + 1)
                                pe.wait_ge(s_wf, KI * (t - 1))
                                for j in range(JC):
                                    for kk in range(KI):
                                        last = nc.tensor.matmul(pq[:, j * D:(j + 1) * D], yg[:, kk, j * P:(j + 1) * P],
                                                                w_out[:, kk, :], start=(kk == 0), stop=(kk == KI - 1))
                                last.then_inc(s_pq, 1)
                            if (s, p) == (2, 5):
                                pe.wait_ge(s_xh, m + 1)
                                for kk in range(KD):
                                    for j in range(JC):
                                        last = nc.tensor.transpose(pq[:, kk * CH + j * P:kk * CH + (j + 1) * P],
                                                                   xh[:, j, kk * P:(kk + 1) * P], ident[:, :])
                                last.then_inc(s_pq, 1)
                            if first and (s, p) == (3, 0):
                                pe.wait_ge(s_h2, m + 1)
                                for kk in range(KD):
                                    last = nc.tensor.matmul(pq[:, 0:1], w_p1[:, kk, :], h2T[:, kk, CH - 1:CH],
                                                            start=(kk == 0), stop=(kk == KD - 1))
                                last.then_inc(s_pq, 1)
                            if first and (s, p) == (3, 1):
                                pe.wait_ge(s_nav, t - 1)
                                nc.tensor.matmul(pq[0:1, 0:NE], nav[:, :], w_p2[:, :], start=True, stop=True).then_inc(s_pq, 1)

            def flush():
                t, qq = NB + 2, 0
                expert_up(t, qq, 0)
                expert_up(t, qq, 1)
                expert_down(t, qq)
                expert_out(t, qq)

            sections(pe, quarter, flush)


INPUTS = [
    "L0_attn_x", "L0_attn_norm_w", "L0_attn_norm_b", "L0_attn_in_proj_w", "L0_attn_conv_w", "L0_attn_conv_b",
    "L0_attn_x_proj_w", "L0_attn_dt_proj_w", "L0_attn_dt_proj_b", "L0_attn_A_log", "L0_attn_D_param",
    "L0_attn_out_proj_w", "L0_ffn_Wp1", "L0_ffn_bp1", "L0_ffn_Wp2", "L0_ffn_bp2", "L0_ffn_W1", "L0_ffn_b1",
    "L0_ffn_W2", "L0_ffn_b2", "L0_ffn_Wo", "L0_ffn_bo", "L0_c", "L0_wmod",
]


def kernel(**inputs):
    import numpy as np
    import concourse.bacc as bacc
    from concourse.bass_utils import run_bass_kernel_spmd

    nc = bacc.Bacc("TRN2", target_bir_lowering=False, num_devices=1)
    arrays, args = {}, []
    for name in INPUTS:
        a = np.ascontiguousarray(inputs[name])
        arrays[f"in_{name}"] = a
        args.append(nc.dram_tensor(f"in_{name}", a.shape, mybir.dt.from_np(a.dtype), kind="ExternalInput").ap())
    args.append(nc.dram_tensor("out_0", (NB, L, D), F32, kind="ExternalOutput").ap())
    build(nc, *args)
    result = run_bass_kernel_spmd(nc, [arrays], core_ids=[0])
    return result.results[0]["out_0"]
```

```python
from contextlib import ExitStack

import concourse.bass as bass
from concourse import mybir

F32 = mybir.dt.float32
I32 = mybir.dt.int32
ACT = mybir.ActivationFunctionType
ALU = mybir.AluOpType
AX_X = mybir.AxisListType.X
ds = bass.ds

P = 128
NB, L, D = 4, 1024, 256
DI, NS, R, KC = 512, 16, 128, 4
NE, F = 8, 512
EPS = 1e-5
KD, KI = D // P, DI // P
CH = 256
JC = CH // P
NQ = L // CH
SPQ = NS // NQ
LT = L // P
NM = 8
VEC_LT = [0, 2, 4, 6, 7]
ACT_LT = [1, 3, 5]
ADD_LAG = 2
NV, NA = len(VEC_LT), len(ACT_LT)
QR = 4
PRE_USES = 11
B_FREE = 3
SEL_STEPS = 10

POS = dict(
    ln1=0, ln1_rs=1, ln2=2, ln2_rs=3, hn=4, hx=5, hnT=5, hnT_out=6,
    in0=7, in0_out=8, in1=9, in1_out=10, conv0=11, conv0b=12, conv0_out=13, conv1=14, conv1b=15, conv1_out=16,
    res0=17, res0_out=18, res1=19, res1_out=20, silu_x=20, silu_g=20, xproj=21, xprojb=22, xproj_out=23,
    cproj=24, cproj_out=25, dt0=25, dt0_out=26, dt1=27, dt1_out=28, softplus=29, delta=30, du=31,
    up0=0, up0_out=1, up1=2, up1_out=3, gelu=3, down=4, downb=5, down_out=6, eout=8, eoutb=10, fin=11, w_o=12, diag=12,
    w_out=9, yT0=12, yT0_out=13, yT1=14, yT1_out=15, gate=16, oproj=18, oprojb=20, x1=21, x1_rs=22, xh=23,
    xhT=25, xhT_out=26, sel0=27, sel0_out=28, sel1=29, sel1_out=30, sel_exp=31, sel=31,
)
POS0 = dict(POS, hnT=0, hnT_out=1, in0=1, in1=2, in0_out=2, in1_out=3, ln1=1, conv0=4, conv0b=4, conv0_out=5,
            conv1=5, conv1b=5, conv1_out=6, silu_x=6, res0=6, res1=7, res0_out=8, res1_out=9, silu_g=10,
            ln1_rs=11, ln2=12, xproj=12, xprojb=12, xproj_out=13, cproj=13, cproj_out=14, hx=15, ln2_rs=15, hn=16,
            dt0=17, dt0_out=18, dt1=18, dt1_out=19, softplus=20, delta=21, du=22)
BANKS0 = 4

def build(nc, x, norm_w, norm_b, in_proj_w, conv_w, conv_b, x_proj_w, dt_proj_w, dt_proj_b, A_log, D_param,
          out_proj_w, Wp1, bp1, Wp2, bp2, W1, b1, W2, b2, Wo, bo, c, wmod, out):
    ctx = ExitStack()
    with ctx:
        def sb(name, shape, dt=F32):
            return ctx.enter_context(nc.sbuf_tensor(name, shape, dt))

        def pb_(name, shape):
            return ctx.enter_context(nc.psum_tensor(name, shape, F32))

        def sem(name):
            return ctx.enter_context(nc.semaphore(name))

        x_rows = x.rearrange("b l d -> (b l) d")
        out_rows = out.rearrange("b l d -> (b l) d")
        mods_d = nc.dram_tensor("mods_d", (NB, NM * D), F32).ap()
        brow_d = nc.dram_tensor("brow_d", (NB * NS + 1, L), F32).ap()
        hx_d = nc.dram_tensor("hx_d", (NB * L, D), F32).ap()
        y_d = nc.dram_tensor("y_d", (NB * L, DI), F32).ap()
        xs_d = nc.dram_tensor("xs_d", (NB * P, KI, L), F32).ap()
        delta_d = nc.dram_tensor("delta_d", (NB * P, KI, L), F32).ap()
        du_d = nc.dram_tensor("du_d", (NB * P, KI, L), F32).ap()
        sres_d = nc.dram_tensor("sres_d", (NB * P, KI, L), F32).ap()

        w_in = sb("w_in", [P, KD, 2 * DI])
        w_x = sb("w_x", [P, KI, R + 2 * NS])
        w_dt = sb("w_dt", [P, DI])
        w_out = sb("w_out", [P, KI, D])
        w_p1 = sb("w_p1", [P, KD, P])
        w_p2 = sb("w_p2", [P, NE])
        w_o = sb("w_o", [P, KD, D])
        w_1 = sb("w_1", [P, KD, F])
        w_2 = sb("w_2", [P, F // P, D])
        b1_c = sb("b1_c", [P, F // P])
        b2_c = sb("b2_c", [P, KD])
        nw_c = sb("nw_c", [P, KD])
        nb_c = sb("nb_c", [P, KD])
        cw_c = sb("cw_c", [P, KI, KC])
        cb_c = sb("cb_c", [P, KI])
        dtb_c = sb("dtb_c", [P, KI])
        D_c = sb("D_c", [P, KI])
        bp1_c = sb("bp1_c", [P, 1])
        bp2_r = sb("bp2_r", [1, NE])
        A_c = sb("A_c", [P, KI, NS])
        c_T = sb("c_T", [P, KD, NB])
        eps_c = sb("eps_c", [P, 1])
        ident = sb("ident", [P, P])
        iota8 = sb("iota8", [1, NE])
        pre_row = sb("pre_row", [P, 3 * D])
        post_row = sb("post_row", [P, 2 * D])
        post_col = sb("post_col", [P, 3, KD])
        bo_row = sb("bo_row", [1, D])
        ones = sb("ones", [1, P])
        diag_gb = sb("diag_gb", [P, KD, D])
        diag_w = sb("diag_w", [P, KI, KC, P])
        delta = sb("delta", [P, KI, L])
        du = sb("du", [P, KI, L])
        C_t = sb("C_t", [P, 2, LT, NS])
        b_bc = sb("b_bc", [P, 2, L])
        h = sb("h", [P, 2, KI, L])
        y = sb("y", [P, LT, DI])
        q = sb("q", [P, QR, DI])
        x_t = sb("x_t", [P, JC, D])
        hm = sb("hm", [P, JC, D])
        hn = sb("hn", [P, JC, D])
        hx = sb("hx", [P, JC, D])
        hnT = sb("hnT", [P, KD, CH])
        xpre = sb("xpre", [P, KI, CH + KC - 1])
        xs = sb("xs", [P, KI, CH])
        sres = sb("sres", [P, KI, CH])
        dr = sb("dr", [P, CH])
        b_T = sb("b_T", [NS, CH])
        delta_c = sb("delta_c", [P, KI, CH])
        du_c = sb("du_c", [P, KI, CH])
        lp = du_c
        st_p = sb("st_p", [P, JC, 6])
        mv_p = sb("mv_p", [P, JC, 2])
        rs_p = sb("rs_p", [P, 3, JC])
        y_c = sb("y_c", [P, JC, DI])
        yg = sb("yg", [P, KI, CH])
        sres_c = sb("sres_c", [P, KI, CH])
        hx_c = sb("hx_c", [P, JC, D])
        g = sb("g", [P, F // P, CH])
        xh = g[:, 0:JC, :]
        x1 = sb("x1", [P, JC, D])
        h2T = sb("h2T", [P, KD, CH])
        r_T = sb("r_T", [P, KD, CH])
        st_a = sb("st_a", [P, JC, 6])
        mv_a = sb("mv_a", [P, JC, 2])
        rs_a = sb("rs_a", [P, 3, JC])
        nav = sb("nav", [P, 1])
        sel = sb("sel", [1, 8, NE])
        sel_i = sb("sel_i", [1, 1], I32)

        pA = [pb_(f"pA{i}", [P, L]) for i in range(2)]
        pH = [pb_(f"pH{i}", [P, DI]) for i in range(2)]
        pp = pb_("pp", [P, 512])
        pq = pb_("pq", [P, 512])

        s_wt, s_cT, s_wm, s_id0, s_id = sem("s_wt"), sem("s_cT"), sem("s_wm"), sem("s_id0"), sem("s_id")
        s_cs, s_mod, s_modv, s_modw, s_Aexp, s_const = (sem("s_cs"), sem("s_mod"), sem("s_modv"), sem("s_modw"),
                                                        sem("s_Aexp"), sem("s_const"))
        s_vec0 = sem("s_vec0")
        s_pad = sem("s_pad")
        s_b, s_dbu, s_dA, s_scan, s_hT = sem("s_b"), sem("s_dbu"), sem("s_dA"), sem("s_scan"), sem("s_hT")
        s_yv, s_qa, s_yg = sem("s_yv"), sem("s_qa"), sem("s_yg")
        s_ysp = sem("s_ysp")
        s_prow, s_x, s_pst, s_prs, s_hm, s_hn, s_hx, s_hxd = (sem("s_prow"), sem("s_x"), sem("s_pst"), sem("s_prs"),
                                                              sem("s_hm"), sem("s_hn"), sem("s_hx"), sem("s_hxd"))
        s_pchain, s_hxc = sem("s_pchain"), sem("s_hxc")
        s_pp, s_ppf = sem("s_pp"), sem("s_ppf")
        s_move, s_xs, s_sres, s_xsd, s_sresd, s_bTd = (sem("s_move"), sem("s_xs"), sem("s_sres"), sem("s_xsd"),
                                                             sem("s_sresd"), sem("s_bTd"))
        s_lp, s_dl, s_du = sem("s_lp"), sem("s_dl"), sem("s_du")
        s_dld, s_dud = sem("s_dld"), sem("s_dud")
        s_dli = [sem(f"s_dli{dt}") for dt in range(KI)]
        s_dui = [sem(f"s_dui{dt}") for dt in range(KI)]
        s_dgw = sem("s_dgw")
        s_qrow, s_wl, s_wf, s_yc, s_xc, s_sc, s_hc = (sem("s_qrow"), sem("s_wl"), sem("s_wf"), sem("s_yc"),
                                                      sem("s_xc"), sem("s_sc"), sem("s_hc"))
        s_pq, s_pqf = sem("s_pq"), sem("s_pqf")
        s_ud, s_gate, s_x1, s_ast, s_ars, s_xh, s_h2, s_dg0, s_dg = (sem("s_ud"), sem("s_gate"), sem("s_x1"),
                                                                     sem("s_ast"), sem("s_ars"), sem("s_xh"),
                                                                     sem("s_h2"), sem("s_dg0"), sem("s_dg"))
        s_achain = sem("s_achain")
        s_nav, s_se, s_schain, s_si, s_ew, s_g, s_rT, s_fin, s_out = (sem("s_nav"), sem("s_se"), sem("s_schain"),
                                                                      sem("s_si"), sem("s_ew"), sem("s_g"),
                                                                      sem("s_rT"), sem("s_fin"), sem("s_out"))
        s_wo = sem("s_wo")
        s_wof = sem("s_wof")
        s_bo = sem("s_bo")

        def wait(eng, s, value):
            if not (isinstance(value, int) and value <= 0):
                eng.wait_ge(s, value)

        def first_q(qq):
            return isinstance(qq, int) and qq == 0

        def sections(eng, quarter, flush, unrolled=(0,)):
            for t in range(NB + 2):
                quarter(t, 0)
                if t in unrolled:
                    for qq in range(1, NQ):
                        quarter(t, qq)
                    continue
                with eng.Fori(1, NQ) as qq:
                    quarter(t, qq)
            flush()

        def has_pre(t):
            return t < NB

        def has_scan(t):
            return 1 <= t <= NB

        def has_a(t):
            return t >= 2

        def has_b(t, qq):
            return t >= 3 or (t == 2 and not first_q(qq))

        def has_tail(t, qq, s):
            if first_q(qq) and s == 0:
                return 2 <= t <= NB + 1
            return has_scan(t)

        def chunk(t, qq):
            return NQ * t + qq

        def slot(t, qq, s):
            return SPQ * (NQ * (t - 1) + qq) + s

        def piece(t, qq):
            return NQ * (t - 2) + qq

        def piece_q(qq):
            return NQ - 1 if first_q(qq) else qq - 1

        def sel_before(t, qq):
            return (t - 2) + (0 if first_q(qq) else 1)

        def b_use(t, qq):
            return 8 * piece(t, qq) - 4 + 2 * sel_before(t, qq)

        def a_use(t, qq):
            return b_use(t, qq) + 4

        def q_of(rank, s):
            return q[:, (NA * ((s - 1) % SPQ) + rank) % QR, :]

        def at(step, t, s, p):
            return (POS if t else POS0)[step] == s * LT + p

        def pre_bank(t, use):
            return pp if t else (pp, pq, pH[0], pH[1])[use % BANKS0]

        def pre_empty(t, k, use, needs=0):
            if t:
                return PRE_USES * k + use
            last = use - BANKS0 if use >= BANKS0 else use + 2 * BANKS0 - PRE_USES - (BANKS0 if use == BANKS0 - 1 else 0)
            return PRE_USES * k + max(last + 1, needs)

        def ln_piece(t, qq):
            return chunk(t, qq) if t else qq + 1

        def has_ln(t, qq):
            return has_pre(t) and (t > 0 or qq + 1 < NQ)

        def consumed(lt):
            return (s_yv, NV, VEC_LT.index(lt)) if lt in VEC_LT else (s_qa, NA, ACT_LT.index(lt))

        ctx.enter_context(nc.allow_non_contiguous_dma(reason="vectors of a few hundred values, one per partition"))
        block = ctx.enter_context(nc.Block())

        @block.sync
        def _(sp):
            hflat = h[:, :, :, :].rearrange("p a k l -> p (a k l)")
            yflat = y[:, :, :].rearrange("p a k -> p (a k)")
            sp.dma_start(x_t[:, :, :], x_rows[0:CH, :].rearrange("(j p) d -> p j d", p=P)).then_inc(s_x, 16)
            for kk in range(KD):
                sp.dma_start(c_T[:, kk, :], c[:, kk * P:(kk + 1) * P].rearrange("b p -> p b")).then_inc(s_cT, 16)
            sp.dma_start(yflat[0:NB, 3584:3584 + D], bo[None, :].to_broadcast((NB, D))).then_inc(s_cT, 16)
            sp.dma_start(hflat[:, 0:KD * 6 * D].rearrange("p (k n) -> p k n", k=KD),
                         wmod.rearrange("(k p) n -> p k n", p=P)).then_inc(s_wm, 16)
            for dst, src in (
                (w_in[:, :, :], in_proj_w.rearrange("(k p) n -> p k n", p=P)),
                (w_x[:, :, :], x_proj_w.rearrange("(k p) n -> p k n", p=P)),
                (w_dt[:, :], dt_proj_w),
                (w_p1[:, :, :], Wp1.rearrange("(k p) n -> p k n", p=P)),
                (w_p2[:, :], Wp2),
                (nw_c[:, :], norm_w.rearrange("(k p) -> p k", p=P)),
                (nb_c[:, :], norm_b.rearrange("(k p) -> p k", p=P)),
                (cw_c[:, :, :], conv_w.rearrange("(k p) n -> p k n", p=P)),
                (cb_c[:, :], conv_b.rearrange("(k p) -> p k", p=P)),
                (dtb_c[:, :], dt_proj_b.rearrange("(k p) -> p k", p=P)),
                (D_c[:, :], D_param.rearrange("(k p) -> p k", p=P)),
                (bp1_c[:, :], bp1.rearrange("(p k) -> p k", k=1)),
                (bp2_r[:, :], bp2.rearrange("(p k) -> p k", p=1)),
                (A_c[:, :, :], A_log.rearrange("(k p) n -> p k n", p=P)),
            ):
                sp.dma_start(dst, src).then_inc(s_wt, 16)
            sp.dma_start(brow_d[NB * NS:NB * NS + 1, :], x_rows[0:L // D, :].rearrange("(o a) d -> o (a d)", o=1)
                         ).then_inc(s_pad, 16)
            sp.wait_ge(s_modv, 1)
            sp.dma_start(mods_d, yflat[0:NB, 1536:1536 + NM * D]).then_inc(s_modw, 16)
            sp.wait_ge(s_modw, 16)

            def load_pre_row(t):
                wait(sp, s_hx, NQ * t)
                sp.dma_start(pre_row[:, :], mods_d[t:t + 1, 0:3 * D].to_broadcast((P, 3 * D))).then_inc(s_prow, 16)

            def load_x(k):
                wait(sp, s_hx, k)
                sp.dma_start(x_t[:, :, :], x_rows[ds(k * CH, CH), :].rearrange("(j p) d -> p j d", p=P)
                             ).then_inc(s_x, 16)

            def store_hx(k):
                sp.wait_ge(s_hx, k + 1)
                sp.dma_start(hx_d[ds(k * CH, CH), :].rearrange("(j p) d -> p j d", p=P), hx[:, :, :]
                             ).then_inc(s_hxd, 16)

            load_pre_row(0)
            store_hx(0)
            load_x(1)

            def quarter(t, qq):
                first = first_q(qq)
                k = chunk(t, qq)
                if has_scan(t) and first:
                    sp.wait_ge(s_dld, 16 * NQ * t)
                    sp.wait_ge(s_dud, 16 * NQ * t)
                    rows = slice((t - 1) * P, t * P)
                    for dt in range(KI):
                        done = KI * (NS * (t - 1) - 1) + dt + 1
                        wait(sp, s_dA, done)
                        sp.dma_start(delta[:, dt, :], delta_d[rows, dt, :]).then_inc(s_dli[dt], 16)
                        wait(sp, s_dbu, done)
                        sp.dma_start(du[:, dt, :], du_d[rows, dt, :]).then_inc(s_dui[dt], 16)
                if has_pre(t) and t > 0:
                    if first:
                        load_pre_row(t)
                    load_x(k)
                if has_tail(t, qq, 0) and first:
                    for lt in range(LT):
                        if lt in VEC_LT:
                            sp.wait_ge(s_yv, NV * (NS * (t - 1) - 1) + VEC_LT.index(lt) + 1)
                        else:
                            sp.wait_ge(s_yg, NA * (NS * (t - 1) - 1) + ACT_LT.index(lt) + 1)
                        tok = (t - 2) * L + lt * P
                        sp.dma_start(y_d[tok:tok + P, :], y[:, lt, :]).then_inc(s_ysp, 16)
                if has_a(t) and first:
                    m = piece(t, 0)
                    wait(sp, s_wof, t - 2)
                    wait(sp, s_h2, m)
                    wait(sp, s_dg, t - 2)
                    sp.dma_start(post_row[:, :], mods_d[t - 2:t - 1, 2 * D:4 * D].to_broadcast((P, 2 * D))
                                 ).then_inc(s_qrow, 16)
                    sp.dma_start(post_col[:, :, :].rearrange("p c k -> p (c k)"),
                                 mods_d[t - 2, 5 * D:8 * D].rearrange("(n p) -> p n", p=P)).then_inc(s_qrow, 16)
                    wait(sp, s_x1, m)
                    sp.dma_start(w_out[:, :, :], out_proj_w.rearrange("(k p) n -> p k n", p=P)).then_inc(s_wl, 16)
                if has_a(t):
                    m, pq_ = piece(t, qq), piece_q(qq)
                    if first:
                        sp.wait_ge(s_ysp, 16 * LT * (t - 1))
                        sp.wait_ge(s_xsd, 16 * NQ * (t - 1))
                        sp.wait_ge(s_sresd, 16 * NQ * (t - 1))
                        sp.wait_ge(s_hxd, 16 * NQ * (t - 1))
                    wait(sp, s_x1, m)
                    tok = (t - 2) * L + pq_ * CH
                    sp.dma_start(y_c[:, :, :], y_d[ds(tok, CH), :].rearrange("(j p) d -> p j d", p=P)).then_inc(s_yc, 16)
                    rows = slice((t - 2) * P, (t - 1) * P)
                    sp.dma_start(yg[:, :, :], xs_d[rows, :, ds(pq_ * CH, CH)]).then_inc(s_xc, 16)
                    sp.dma_start(sres_c[:, :, :], sres_d[rows, :, ds(pq_ * CH, CH)]).then_inc(s_sc, 16)
                    sp.dma_start(hx_c[:, :, :], hx_d[ds(tok, CH), :].rearrange("(j p) d -> p j d", p=P)).then_inc(s_hc, 16)
                if has_pre(t) and t > 0:
                    store_hx(k)
                if has_b(t, qq):
                    sp.wait_ge(s_fin, piece(t, qq))
                    store(t, qq)
                if has_a(t) and first:
                    sp.dma_start(w_o[:, :, :], Wo.rearrange("(k p) n -> p k n", p=P)).then_inc(s_wo, 16)
                    sp.dma_start(bo_row[:, :], mods_d[t - 2:t - 1, 4 * D:5 * D]).then_inc(s_bo, 16)
                if has_pre(t):
                    rows = slice(t * P, (t + 1) * P)
                    at_l = qq * CH
                    sp.wait_ge(s_xs, 2 * k + 2)
                    sp.dma_start(xs_d[rows, :, ds(at_l, CH)], xs[:, :, :]).then_inc(s_xsd, 16)
                    sp.dma_start(sres_d[rows, :, ds(at_l, CH)], sres[:, :, :]).then_inc(s_sresd, 16)
                    if has_ln(t, qq) and t == 0:
                        store_hx(k + 1)
                        if qq + 2 < NQ:
                            load_x(k + 2)
                    sp.wait_ge(s_ppf, PRE_USES * k + 8)
                    sp.dma_start(brow_d[t * NS:(t + 1) * NS, ds(at_l, CH)], b_T[:, :]).then_inc(s_bTd, 16)
                    sp.wait_ge(s_dl, k + 1)
                    sp.dma_start(delta_d[rows, :, ds(at_l, CH)], delta_c[:, :, :]).then_inc(s_dld, 16)
                    sp.wait_ge(s_du, k + 1)
                    sp.dma_start(du_d[rows, :, ds(at_l, CH)], du_c[:, :, :]).then_inc(s_dud, 16)
                if has_a(t) and first:
                    sp.wait_ge(s_si, t - 1)
                    e = sp.value_load(sel_i[0:1, 0:1], min_val=0, max_val=NE - 1)
                    sp.dma_start(w_1[:, :, :], W1[ds(e, 1), :, :].rearrange("e (k p) f -> p (e k) f", p=P)).then_inc(s_ew, 16)
                    sp.dma_start(w_2[:, :, :], W2[ds(e, 1), :, :].rearrange("e (k p) f -> p (e k) f", p=P)).then_inc(s_ew, 16)
                    sp.dma_start(b1_c[:, :], b1[ds(e, 1), :].rearrange("e (k p) -> p (e k)", p=P)).then_inc(s_ew, 16)
                    sp.dma_start(b2_c[:, :], b2[ds(e, 1), :].rearrange("e (k p) -> p (e k)", p=P)).then_inc(s_ew, 16)

            def store(t, qq):
                if first_q(qq):
                    tok = (t - 3) * L + (NQ - 2) * CH
                else:
                    tok = (t - 2) * L + ((qq + (NQ - 2)) % NQ) * CH
                sp.dma_start(out_rows[ds(tok, CH), :].rearrange("(j p) d -> p j d", p=P), x1[:, :, :]).then_inc(s_out, 16)

            sections(sp, quarter, lambda: None)
            sp.wait_ge(s_fin, NB * NQ)
            store(NB + 2, 0)
            sp.wait_ge(s_out, 16 * NB * NQ)

        @block.gpsimd
        def _(gp):
            gp.memset(ident[:, :], 0.0).then_inc(s_id0, 1)
            gp.wait_ge(s_id0, 1)
            gp.affine_select(out=ident[:, :], in_=ident[:, :], compare_op=ALU.not_equal, fill=1.0, base=0,
                             pattern=[[-1, P]], channel_multiplier=1).then_inc(s_id, 1)
            gp.memset(eps_c[:, :], EPS).then_inc(s_const, 1)
            gp.iota(iota8[:, :], pattern=[[1, NE]], base=0, channel_multiplier=0,
                    allow_small_or_imprecise_dtypes=True).then_inc(s_const, 1)
            gp.memset(ones[:, :], 1.0).then_inc(s_const, 1)
            gp.memset(diag_gb[:, :, :], 0.0).then_inc(s_dg0, 1)
            gp.wait_ge(s_id, 1)
            gp.wait_ge(s_wt, 16 * 14)
            for kk in range(KI):
                for tap in range(KC):
                    last = gp.tensor_scalar(diag_w[:, kk, tap, :], ident[:, :], cw_c[:, kk, tap:tap + 1], None, ALU.mult)
            last.then_inc(s_dgw, 1)

            def residual(k):
                gp.wait_ge(s_hm, k + 1)
                wait(gp, s_hxd, 16 * k)
                for j in range(JC):
                    last = gp.tensor_tensor(hx[:, j, :], hm[:, j, :], pre_row[:, 2 * D:3 * D], ALU.mult)
                last.then_inc(s_hxc, 1)
                gp.wait_ge(s_hxc, k + 1)
                gp.tensor_tensor(hx[:, :, :], hx[:, :, :], x_t[:, :, :], ALU.add).then_inc(s_hx, 1)

            def quarter(t, qq):
                first = first_q(qq)
                k = chunk(t, qq)
                for s in range(SPQ):
                    for p in range(LT):
                        if has_scan(t) and p % 2 == 0:
                            dt, i = p // 2, slot(t, qq, s)
                            if first and s == 0:
                                gp.wait_ge(s_dui[dt], 16 * t)
                            if dt == 0:
                                gp.wait_ge(s_b, 16 * (i + 1))
                                wait(gp, s_hT, LT * (i - 1))
                            gp.tensor_tensor(h[:, s % 2, dt, :], du[:, dt, :], b_bc[:, s % 2, :],
                                             ALU.mult).then_inc(s_dbu, 1)
                        if has_tail(t, qq, s) and p - ADD_LAG in ACT_LT:
                            lt = p - ADD_LAG
                            i, rank = slot(t, qq, s) - 1, ACT_LT.index(lt)
                            gp.wait_ge(s_qa, NA * i + rank + 1)
                            wait(gp, s_yg, NA * (i - 1) + rank + 1)
                            if first and s == 1:
                                wait(gp, s_ysp, 16 * LT * (t - 1))
                                gp.tensor_copy(y[:, lt, :], q_of(rank, s)).then_inc(s_yg, 1)
                            else:
                                gp.tensor_tensor(y[:, lt, :], y[:, lt, :], q_of(rank, s), ALU.add).then_inc(s_yg, 1)
                        if has_ln(t, qq) and at("hx", t, s, p):
                            residual(ln_piece(t, qq))
                        if has_pre(t) and at("delta", t, s, p):
                            gp.wait_ge(s_lp, 2 * (k + 1))
                            gp.tensor_tensor(delta_c[:, :, :], delta_c[:, :, :], lp[:, :, :], ALU.add).then_inc(s_dl, 1)
                        if has_pre(t) and at("du", t, s, p):
                            gp.wait_ge(s_dl, k + 1)
                            gp.tensor_tensor(du_c[:, :, :], delta_c[:, :, :], xs[:, :, :], ALU.mult).then_inc(s_du, 1)
                        if has_a(t) and first and at("w_out", t, s, p):
                            gp.wait_ge(s_qrow, 32 * (t - 1))
                            gp.wait_ge(s_wl, 16 * (t - 1))
                            for kk in range(KI):
                                last = gp.tensor_tensor(w_out[:, kk, :], w_out[:, kk, :], post_row[:, 0:D], ALU.mult)
                            last.then_inc(s_wf, 1)
                        if has_a(t) and at("gate", t, s, p):
                            m = piece(t, qq)
                            gp.wait_ge(s_ud, KI * (m + 1))
                            gp.wait_ge(s_sc, 16 * (m + 1))
                            gp.tensor_tensor(yg[:, :, :], yg[:, :, :], sres_c[:, :, :], ALU.mult).then_inc(s_gate, 1)
                        if has_a(t) and first and at("w_o", t, s, p):
                            gp.wait_ge(s_wo, 16 * (t - 1))
                            for kk in range(KD):
                                last = gp.tensor_tensor(w_o[:, kk, :], w_o[:, kk, :], post_row[:, D:2 * D], ALU.mult)
                            last.then_inc(s_wof, 1)

            residual(0)
            sections(gp, quarter, lambda: None)
            gp.wait_ge(s_b, 16 * (NB * NS + 1))

        @block.scalar
        def _(act):
            act.wait_ge(s_cT, 16 * (KD + 1))
            nc.scalar.activation(c_T[:, :, :], c_T[:, :, :], ACT.Silu).then_inc(s_cs, 1)
            act.wait_ge(s_wt, 16 * 14)
            nc.scalar.activation(A_c[:, :, :], A_c[:, :, :], ACT.Exp).then_inc(s_Aexp, 1)
            act.wait_ge(s_Aexp, 1)
            nc.scalar.mul(A_c[:, :, :], A_c[:, :, :], -1.0).then_inc(s_Aexp, 1)
            act.wait_ge(s_Aexp, 2)
            act.wait_ge(s_const, 2)

            def exp_and_ln():
                nc.scalar.preload_act_table_set("natural_log_exp_and_others")

            def rsqrt_guess(mv, rs, s_in, s_out_, n):
                act.wait_ge(s_in, n + 1)
                nc.scalar.activation(rs[:, 0, :], mv[:, :, 1], ACT.Ln, bias=eps_c[:, :]).then_inc(s_out_, 1)
                act.wait_ge(s_out_, 2 * n + 1)
                nc.scalar.activation(rs[:, 1, :], rs[:, 0, :], ACT.Exp, scale=-0.5).then_inc(s_out_, 1)

            def fetch_b(i, s):
                wait(act, s_dbu, KI * (i - 1))
                act.dma_start(b_bc[:, s % 2, :], brow_d[ds(i, 1), :].to_broadcast((P, L))).then_inc(s_b, 16)

            def hidden(t, qq, u):
                act.wait_ge(s_pq, b_use(t, qq) + 1 + u)
                for kk in (2 * u, 2 * u + 1):
                    last = nc.scalar.activation(g[:, kk, :], pq[:, (kk % 2) * CH:(kk % 2 + 1) * CH], ACT.Identity,
                                                bias=b1_c[:, kk:kk + 1])
                last.then_inc(s_pqf, 1)

            def gelu(t, qq):
                act.wait_ge(s_pqf, B_FREE * (piece(t, qq) - 1) + 2)
                nc.scalar.activation(g[:, :, :], g[:, :, :], ACT.Gelu).then_inc(s_g, 1)

            def down_out(t, qq):
                act.wait_ge(s_pq, b_use(t, qq) + 3)
                for kk in range(KD):
                    last = nc.scalar.activation(r_T[:, kk, :], pq[:, kk * CH:(kk + 1) * CH], ACT.Identity,
                                                bias=b2_c[:, kk:kk + 1])
                last.then_inc(s_pqf, 1)

            def quarter(t, qq):
                first = first_q(qq)
                k = chunk(t, qq)
                exp_and_ln()
                for s in range(SPQ):
                    for p in range(LT):
                        if has_scan(t) and p % 2 == 0:
                            dt, i = p // 2, slot(t, qq, s)
                            if first and s == 0:
                                if t == 1 and dt == 0:
                                    act.wait_ge(s_bTd, 16 * NQ)
                                    fetch_b(0, 0)
                                act.wait_ge(s_dli[dt], 16 * t)
                            wait(act, s_scan, KI * i + dt - 1)
                            nc.scalar.activation(pA[dt % 2][:, :], delta[:, dt, :], ACT.Exp,
                                                 scale=A_c[:, dt, ds(SPQ * qq + s, 1)]).then_inc(s_dA, 1)
                            if dt == 3:
                                if s == SPQ - 1:
                                    act.wait_ge(s_bTd, 16 * (chunk(t, qq) + 1) if has_pre(t) else 16 * NQ * NB)
                                    if t == NB:
                                        act.wait_ge(s_pad, 16)
                                fetch_b(i + 1, s + 1)
                        if has_tail(t, qq, s) and p in ACT_LT:
                            i, rank = slot(t, qq, s) - 1, ACT_LT.index(p)
                            bb = (t - 2) if first and s == 0 else (t - 1)
                            n = NS - 1 if first and s == 0 else SPQ * qq + s - 1
                            if first and s == 1 and rank == 0:
                                act.wait_ge(s_ppf, PRE_USES * NQ * t - 2)
                            act.wait_ge(s_hT, LT * i + p + 1)
                            wait(act, s_yg, NA * i + rank + 1 - QR)
                            nc.scalar.activation(q_of(rank, s), pH[p % 2][:, :], ACT.Copy,
                                                 scale=C_t[:, bb % 2, p, ds(n, 1)]).then_inc(s_qa, 1)
                        if has_pre(t):
                            base = PRE_USES * k
                            if has_ln(t, qq) and at("ln1_rs", t, s, p):
                                rsqrt_guess(mv_p, rs_p, s_pst, s_prs, 2 * ln_piece(t, qq))
                            if has_ln(t, qq) and at("ln2_rs", t, s, p):
                                rsqrt_guess(mv_p, rs_p, s_pst, s_prs, 2 * ln_piece(t, qq) + 1)
                            if at("hnT_out", t, s, p):
                                act.wait_ge(s_pp, base + 1)
                                for kk in range(KD):
                                    last = nc.scalar.activation(hnT[:, kk, :], pre_bank(t, 0)[:, kk * CH:(kk + 1) * CH], ACT.Identity,
                                                                scale=nw_c[:, kk:kk + 1], bias=nb_c[:, kk:kk + 1])
                                last.then_inc(s_ppf, 1)
                            for u in range(2):
                                if at(f"in{u}_out", t, s, p):
                                    act.wait_ge(s_pp, base + 2 + u)
                                    if u == 0:
                                        act.wait_ge(s_move, k + 1)
                                    nc.scalar.copy(xpre[:, 2 * u:2 * u + 2, KC - 1:],
                                                   pre_bank(t, 1 + u)[:, :].rearrange("p (a c) -> p a c", a=2)).then_inc(s_ppf, 1)
                                if at(f"conv{u}_out", t, s, p):
                                    act.wait_ge(s_pp, base + 4 + u)
                                    if u == 0:
                                        wait(act, s_du, k)
                                        wait(act, s_xsd, 16 * k)
                                    for kk in (2 * u, 2 * u + 1):
                                        last = nc.scalar.activation(xs[:, kk, :],
                                                                    pre_bank(t, 3 + u)[:, (kk % 2) * CH:(kk % 2 + 1) * CH],
                                                                    ACT.Identity, bias=cb_c[:, kk:kk + 1])
                                    last.then_inc(s_ppf, 1)
                                if at(f"res{u}_out", t, s, p):
                                    act.wait_ge(s_pp, base + 6 + u)
                                    if u == 0:
                                        wait(act, s_sresd, 16 * k)
                                    nc.scalar.copy(sres[:, 2 * u:2 * u + 2, :],
                                                   pre_bank(t, 5 + u)[:, :].rearrange("p (a c) -> p a c", a=2)).then_inc(s_ppf, 1)
                            if at("silu_x", t, s, p):
                                act.wait_ge(s_ppf, base + 5)
                                nc.scalar.activation(xs[:, :, :], xs[:, :, :], ACT.Silu).then_inc(s_xs, 1)
                            if at("silu_g", t, s, p):
                                act.wait_ge(s_ppf, base + 7)
                                nc.scalar.activation(sres[:, :, :], sres[:, :, :], ACT.Silu).then_inc(s_xs, 1)
                                exp_and_ln()
                            if at("xproj_out", t, s, p):
                                act.wait_ge(s_pp, base + 8)
                                wait(act, s_bTd, 16 * k)
                                nc.scalar.copy(dr[:, :], pre_bank(t, 7)[:, 0:CH])
                                nc.scalar.copy(b_T[:, :], pre_bank(t, 7)[0:NS, CH:2 * CH]).then_inc(s_ppf, 1)
                            if at("cproj_out", t, s, p):
                                act.wait_ge(s_pp, base + 9)
                                if first and t >= 2:
                                    act.wait_ge(s_yv, NV * NS * (t - 1))
                                nc.scalar.copy(C_t[:, t % 2, ds(JC * qq, JC), :],
                                               pre_bank(t, 8)[:, 0:JC * NS].rearrange("p (j n) -> p j n", j=JC)
                                               ).then_inc(s_ppf, 1)
                            for u in range(2):
                                if at(f"dt{u}_out", t, s, p):
                                    act.wait_ge(s_pp, base + 10 + u)
                                    if u == 0:
                                        wait(act, s_dud, 16 * k)
                                        wait(act, s_dld, 16 * k)
                                    for kk in (2 * u, 2 * u + 1):
                                        half = pre_bank(t, 9 + u)[:, (kk % 2) * CH:(kk % 2 + 1) * CH]
                                        nc.scalar.activation(lp[:, kk, :], half, ACT.Abs, bias=dtb_c[:, kk:kk + 1])
                                        last = nc.scalar.activation(delta_c[:, kk, :], half, ACT.Relu,
                                                                    bias=dtb_c[:, kk:kk + 1])
                                    last.then_inc(s_ppf, 1)
                            if at("softplus", t, s, p):
                                act.wait_ge(s_ppf, base + PRE_USES)
                                nc.scalar.activation(lp[:, :, :], lp[:, :, :], ACT.Exp, scale=-1.0).then_inc(s_lp, 1)
                                act.wait_ge(s_lp, 2 * k + 1)
                                nc.scalar.activation(lp[:, :, :], lp[:, :, :], ACT.Ln, bias=1.0).then_inc(s_lp, 1)
                        if has_b(t, qq):
                            if at("up0_out", t, s, p):
                                act.wait_ge(s_ew, 64 * (t - 2 if first else t - 1))
                                hidden(t, qq, 0)
                            if at("up1_out", t, s, p):
                                hidden(t, qq, 1)
                            if at("gelu", t, s, p):
                                gelu(t, qq)
                                exp_and_ln()
                            if at("down_out", t, s, p):
                                down_out(t, qq)
                        if has_a(t):
                            m = piece(t, qq)
                            if first and at("diag", t, s, p):
                                act.wait_ge(s_qrow, 32 * (t - 1))
                                act.wait_ge(s_dg0, 1)
                                act.wait_ge(s_fin, m)
                                for kk in range(KD):
                                    last = nc.scalar.activation(diag_gb[:, kk, kk * P:(kk + 1) * P], ident[:, :], ACT.Copy,
                                                                scale=post_col[:, 2, kk:kk + 1])
                                last.then_inc(s_dg, 1)
                            if at("x1_rs", t, s, p):
                                rsqrt_guess(mv_a, rs_a, s_ast, s_ars, m)
                            if at("xhT_out", t, s, p):
                                act.wait_ge(s_pq, a_use(t, qq) + 4)
                                for kk in range(KD):
                                    last = nc.scalar.activation(h2T[:, kk, :], pq[:, kk * CH:(kk + 1) * CH], ACT.Identity,
                                                                scale=post_col[:, 0, kk:kk + 1], bias=post_col[:, 1, kk:kk + 1])
                                last.then_inc(s_h2, 1)
                            if first and at("sel0_out", t, s, p):
                                act.wait_ge(s_pq, a_use(t, qq) + 5)
                                nc.scalar.activation(nav[:, :], pq[:, 0:1], ACT.Gelu, bias=bp1_c[:, :]).then_inc(s_nav, 1)
                                exp_and_ln()
                            if first and at("sel_exp", t, s, p):
                                act.wait_ge(s_schain, SEL_STEPS * (t - 2) + 3)
                                nc.scalar.activation(sel[:, 2, :], sel[:, 1, :], ACT.Exp, accum_out=sel[:, 3, 0:1]
                                                     ).then_inc(s_se, 1)

            def flush():
                t, qq = NB + 2, 0
                hidden(t, qq, 0)
                hidden(t, qq, 1)
                gelu(t, qq)
                down_out(t, qq)

            exp_and_ln()
            rsqrt_guess(mv_p, rs_p, s_pst, s_prs, 0)
            rsqrt_guess(mv_p, rs_p, s_pst, s_prs, 1)
            sections(act, quarter, flush)

        @block.vector
        def _(dve):
            yflat = y[:, :, :].rearrange("p a k -> p (a k)")
            steps = [0]
            dve.wait_ge(s_wt, 16 * 14)

            def link(ins):
                steps[0] += 1
                ins.then_inc(s_vec0, 1)
                dve.wait_ge(s_vec0, steps[0])

            def mod(i):
                return yflat[0:NB, i * D:(i + 1) * D]

            def keep(i):
                return yflat[0:NB, (6 + i) * D:(7 + i) * D]
            bo4 = yflat[0:NB, 3584:3584 + D]
            tmp = yflat[0:NB, 3840:3840 + D]
            for i in range(3):
                dve.wait_ge(s_mod, i + 1)
                link(nc.vector.tensor_copy(yflat[0:NB, i * 512:(i + 1) * 512], (pp, pq, pH[0])[i][0:NB, :]))
            dve.wait_ge(s_cT, 16 * (KD + 1))
            link(nc.vector.tensor_scalar(keep(0), mod(1), 1.0, None, ALU.add))
            link(nc.vector.tensor_copy(keep(1), mod(0)))
            for gate, dst in ((2, 2), (5, 7)):
                link(nc.vector.tensor_scalar(tmp, mod(gate), 0.0, 2.0, ALU.is_ge, ALU.mult))
                link(nc.vector.tensor_scalar(tmp, tmp, -1.0, None, ALU.add))
                link(nc.vector.scalar_tensor_tensor(keep(dst), mod(gate), -1.0, mod(gate), ALU.mult, ALU.max))
                link(nc.vector.scalar_tensor_tensor(keep(dst), keep(dst), 0.25, tmp, ALU.max, ALU.mult))
            link(nc.vector.tensor_scalar(keep(5), mod(4), 1.0, None, ALU.add))
            link(nc.vector.tensor_copy(keep(6), mod(3)))
            link(nc.vector.tensor_scalar(keep(3), keep(7), 0.3, None, ALU.mult))
            nc.vector.tensor_tensor(keep(4), keep(3), bo4, ALU.mult).then_inc(s_modv, 1)

            def stats(src, st, mv, rs, s_chain, base, s_done):
                for j in range(JC):
                    last = nc.vector.bn_stats(st[:, j, :], src[:, j, :])
                last.then_inc(s_chain, 1)
                dve.wait_ge(s_chain, base + 1)
                nc.vector.memset(rs[:, 2, :], 0.0)
                for j in range(JC):
                    last = nc.vector.bn_aggr(mv[:, j, :], st[:, j, :])
                last.then_inc(s_done, 1)

            def refine(mv, rs, s_chain, base):
                nc.vector.tensor_tensor(rs[:, 2, :], rs[:, 1, :], rs[:, 1, :], ALU.mult).then_inc(s_chain, 1)
                dve.wait_ge(s_chain, base + 1)
                nc.vector.scalar_tensor_tensor(rs[:, 2, :], mv[:, :, 1], EPS, rs[:, 2, :], ALU.add, ALU.mult).then_inc(s_chain, 1)
                dve.wait_ge(s_chain, base + 2)
                nc.vector.tensor_scalar(rs[:, 2, :], rs[:, 2, :], -0.5, 1.5, ALU.mult, ALU.add).then_inc(s_chain, 1)
                dve.wait_ge(s_chain, base + 3)
                nc.vector.tensor_tensor(rs[:, 1, :], rs[:, 1, :], rs[:, 2, :], ALU.mult).then_inc(s_chain, 1)
                dve.wait_ge(s_chain, base + 4)

            def result(t, qq):
                dve.wait_ge(s_pq, b_use(t, qq) + 4)
                nc.vector.tensor_tensor(x1[:, :, :], x1[:, :, :], pq[:, :].rearrange("p (j d) -> p j d", j=JC),
                                        ALU.add).then_inc(s_fin, 1)

            PCH = 12
            ACH = 5

            def ln1(k, t, first):
                dve.wait_ge(s_x, 16 * (k + 1))
                stats(x_t, st_p, mv_p, rs_p, s_pchain, PCH * k, s_pst)

            def ln2(k, t, first):
                base = PCH * k
                dve.wait_ge(s_prs, 4 * k + 2)
                refine(mv_p, rs_p, s_pchain, base + 1)
                if first:
                    dve.wait_ge(s_prow, 16 * (t + 1))
                wait(dve, s_hx, k)
                for j in range(JC):
                    last = nc.vector.tensor_scalar(hm[:, j, :], x_t[:, j, :], mv_p[:, j, 0:1],
                                                   rs_p[:, 1, j:j + 1], ALU.subtract, ALU.mult)
                last.then_inc(s_pchain, 1)
                dve.wait_ge(s_pchain, base + 6)
                for j in range(JC):
                    last = nc.vector.tensor_tensor(hm[:, j, :], hm[:, j, :], pre_row[:, 0:D], ALU.mult)
                last.then_inc(s_pchain, 1)
                dve.wait_ge(s_pchain, base + 7)
                for j in range(JC):
                    last = nc.vector.tensor_tensor(hm[:, j, :], hm[:, j, :], pre_row[:, D:2 * D], ALU.add)
                last.then_inc(s_hm, 1)
                dve.wait_ge(s_hm, k + 1)
                stats(hm, st_p, mv_p, rs_p, s_pchain, base + 7, s_pst)

            def second_ln(k, t, first):
                dve.wait_ge(s_prs, 4 * k + 4)
                refine(mv_p, rs_p, s_pchain, PCH * k + 8)
                wait(dve, s_pp, PRE_USES * (k - 1) + 1)
                for j in range(JC):
                    last = nc.vector.tensor_scalar(hn[:, j, :], hm[:, j, :], mv_p[:, j, 0:1],
                                                   rs_p[:, 1, j:j + 1], ALU.subtract, ALU.mult)
                last.then_inc(s_hn, 1)
                wait(dve, s_pp, PRE_USES * (k - 1) + 5)
                if first:
                    nc.vector.memset(xpre[:, :, 0:KC - 1], 0.0).then_inc(s_move, 1)
                else:
                    nc.vector.tensor_copy(xpre[:, :, 0:KC - 1], xpre[:, :, CH:CH + KC - 1]).then_inc(s_move, 1)

            def quarter(t, qq):
                first = first_q(qq)
                k = chunk(t, qq)
                for s in range(SPQ):
                    for p in range(LT):
                        if has_scan(t) and p % 2 == 0:
                            dt, i = p // 2, slot(t, qq, s)
                            dve.wait_ge(s_dA, KI * i + dt + 1)
                            dve.wait_ge(s_dbu, KI * i + dt + 1)
                            nc.vector.tensor_tensor_scan(h[:, s % 2, dt, :], pA[dt % 2][:, :], h[:, s % 2, dt, :], 0.0,
                                                         ALU.mult, ALU.add).then_inc(s_scan, 1)
                        if has_tail(t, qq, s) and p in VEC_LT:
                            i, rank = slot(t, qq, s) - 1, VEC_LT.index(p)
                            bb = (t - 2) if first and s == 0 else (t - 1)
                            n = NS - 1 if first and s == 0 else SPQ * qq + s - 1
                            scale = C_t[:, bb % 2, p, ds(n, 1)]
                            if first and s == 1 and rank == 0:
                                dve.wait_ge(s_ppf, PRE_USES * NQ * t - 2)
                            dve.wait_ge(s_hT, LT * i + p + 1)
                            wait(dve, s_yv, NV * (i - 1) + rank + 1)
                            if first and s == 1:
                                wait(dve, s_ysp, 16 * LT * (t - 1))
                                nc.vector.tensor_scalar(y[:, p, :], pH[p % 2][:, :], scale, None, ALU.mult).then_inc(s_yv, 1)
                            else:
                                nc.vector.scalar_tensor_tensor(y[:, p, :], pH[p % 2][:, :], scale, y[:, p, :],
                                                               ALU.mult, ALU.add).then_inc(s_yv, 1)
                        if has_ln(t, qq):
                            for step, run in (("ln1", ln1), ("ln2", ln2), ("hn", second_ln)):
                                if at(step, t, s, p):
                                    run(ln_piece(t, qq), t, first and t > 0)
                        if has_b(t, qq) and at("fin", t, s, p):
                            result(t, qq)
                        if has_a(t):
                            m = piece(t, qq)
                            for u in range(2):
                                if at(f"yT{u}_out", t, s, p):
                                    dve.wait_ge(s_pq, a_use(t, qq) + 1 + u)
                                    dve.wait_ge(s_xc, 16 * (m + 1))
                                    for kk in (2 * u, 2 * u + 1):
                                        nc.vector.scalar_tensor_tensor(yg[:, kk, :], yg[:, kk, :], D_c[:, kk:kk + 1],
                                                                       pq[:, (kk % 2) * CH:(kk % 2 + 1) * CH],
                                                                       ALU.mult, ALU.add).then_inc(s_ud, 1)
                            if at("x1", t, s, p):
                                dve.wait_ge(s_pq, a_use(t, qq) + 3)
                                dve.wait_ge(s_hc, 16 * (m + 1))
                                wait(dve, s_out, 16 * m)
                                nc.vector.tensor_tensor(x1[:, :, :], hx_c[:, :, :],
                                                        pq[:, :].rearrange("p (j d) -> p j d", j=JC), ALU.add).then_inc(s_x1, 1)
                                dve.wait_ge(s_x1, m + 1)
                                stats(x1, st_a, mv_a, rs_a, s_achain, ACH * m, s_ast)
                            if at("xh", t, s, p):
                                dve.wait_ge(s_ars, 2 * m + 2)
                                refine(mv_a, rs_a, s_achain, ACH * m + 1)
                                for j in range(JC):
                                    last = nc.vector.tensor_scalar(xh[:, j, :], x1[:, j, :], mv_a[:, j, 0:1],
                                                                   rs_a[:, 1, j:j + 1], ALU.subtract, ALU.mult)
                                last.then_inc(s_xh, 1)
                            if first and at("sel1_out", t, s, p):
                                cbase = SEL_STEPS * (t - 2)
                                dve.wait_ge(s_pq, a_use(t, qq) + 6)
                                nc.vector.tensor_tensor(sel[:, 0, :], pq[0:1, 0:NE], bp2_r[:, :], ALU.add).then_inc(s_schain, 1)
                                dve.wait_ge(s_schain, cbase + 1)
                                nc.vector.reduce_max(sel[:, 3, 1:2], sel[:, 0, :], AX_X).then_inc(s_schain, 1)
                                dve.wait_ge(s_schain, cbase + 2)
                                nc.vector.tensor_scalar(sel[:, 1, :], sel[:, 0, :], sel[:, 3, 1:2], None, ALU.subtract
                                                        ).then_inc(s_schain, 1)
                            if first and at("sel", t, s, p):
                                cbase = SEL_STEPS * (t - 2)
                                dve.wait_ge(s_se, t - 1)
                                nc.vector.reciprocal(sel[:, 3, 2:3], sel[:, 3, 0:1]).then_inc(s_schain, 1)
                                dve.wait_ge(s_schain, cbase + 4)
                                nc.vector.tensor_scalar(sel[:, 4, :], sel[:, 2, :], sel[:, 3, 2:3], None, ALU.mult
                                                        ).then_inc(s_schain, 1)
                                dve.wait_ge(s_schain, cbase + 5)
                                nc.vector.reduce_max(sel[:, 3, 3:4], sel[:, 4, :], AX_X).then_inc(s_schain, 1)
                                dve.wait_ge(s_schain, cbase + 6)
                                nc.vector.tensor_scalar(sel[:, 5, :], sel[:, 4, :], sel[:, 3, 3:4], None, ALU.is_ge
                                                        ).then_inc(s_schain, 1)
                                dve.wait_ge(s_schain, cbase + 7)
                                nc.vector.scalar_tensor_tensor(sel[:, 6, :], iota8[:, :], -float(NE), sel[:, 5, :],
                                                               ALU.add, ALU.mult).then_inc(s_schain, 1)
                                dve.wait_ge(s_schain, cbase + 8)
                                nc.vector.tensor_reduce(sel[:, 3, 4:5], sel[:, 6, :], AX_X, ALU.min).then_inc(s_schain, 1)
                                dve.wait_ge(s_schain, cbase + 9)
                                nc.vector.tensor_scalar(sel[:, 3, 5:6], sel[:, 3, 4:5], float(NE), None, ALU.add).then_inc(s_schain, 1)
                                dve.wait_ge(s_schain, cbase + 10)
                                nc.vector.tensor_copy(sel_i[:, :], sel[:, 3, 5:6]).then_inc(s_si, 1)

            ln1(0, 0, True)
            ln2(0, 0, True)
            second_ln(0, 0, True)
            sections(dve, quarter, lambda: result(NB + 2, 0))

        @block.tensor
        def _(pe):
            hflat = h[:, :, :, :].rearrange("p a k l -> p (a k l)")
            wm = hflat[:, 0:KD * 6 * D].rearrange("p (k n) -> p k n", k=KD)
            pe.wait_ge(s_cs, 1)
            pe.wait_ge(s_wm, 16)
            for i, bank in enumerate((pp, pq, pH[0])):
                for kk in range(KD):
                    last = nc.tensor.matmul(bank[0:NB, :], c_T[:, kk, :], wm[:, kk, i * 512:(i + 1) * 512],
                                            start=(kk == 0), stop=(kk == KD - 1))
                last.then_inc(s_mod, 1)
            pe.wait_ge(s_modv, 1)
            pe.wait_ge(s_id, 1)
            pe.wait_ge(s_wt, 16 * 14)
            pe.wait_ge(s_dgw, 1)
            pe.wait_ge(s_const, 3)

            def expert_up(t, qq, u):
                if u == 0:
                    pe.wait_ge(s_h2, piece(t, qq))
                else:
                    pe.wait_ge(s_pqf, B_FREE * (piece(t, qq) - 1) + 1)
                for kk in (2 * u, 2 * u + 1):
                    for kd in range(KD):
                        last = nc.tensor.matmul(pq[:, (kk % 2) * CH:(kk % 2 + 1) * CH], w_1[:, kd, kk * P:(kk + 1) * P],
                                                h2T[:, kd, :], start=(kd == 0), stop=(kd == KD - 1))
                last.then_inc(s_pq, 1)

            def expert_down(t, qq, kd):
                if kd == 0:
                    pe.wait_ge(s_g, piece(t, qq))
                for kk in range(F // P):
                    last = nc.tensor.matmul(pq[:, kd * CH:(kd + 1) * CH], w_2[:, kk, kd * P:(kd + 1) * P], g[:, kk, :],
                                            start=(kk == 0), stop=(kk == F // P - 1))
                if kd == KD - 1:
                    last.then_inc(s_pq, 1)

            def expert_out(t, qq, j):
                if j == 0:
                    pe.wait_ge(s_pqf, B_FREE * (piece(t, qq) - 1) + 3)
                into, tok = pq[:, j * D:(j + 1) * D], slice(j * P, (j + 1) * P)
                for kd in range(KD):
                    nc.tensor.matmul(into, r_T[:, kd, tok], w_o[:, kd, :], start=(kd == 0), stop=False)
                for kd in range(KD):
                    nc.tensor.matmul(into, h2T[:, kd, tok], diag_gb[:, kd, :], start=False, stop=False)
                last = nc.tensor.matmul(into, ones[:, :], bo_row[:, :], start=False, stop=True)
                if j == JC - 1:
                    last.then_inc(s_pq, 1)

            def h_transposed(t, qq, s, lt):
                i = slot(t, qq, s) - 1
                if lt == 0:
                    pe.wait_ge(s_scan, KI * (i + 1))
                prev, n_, rank = consumed((lt - 2) % LT)
                wait(pe, prev, n_ * (i if lt >= 2 else i - 1) + rank + 1)
                for dt in range(KI):
                    last = nc.tensor.transpose(pH[lt % 2][:, dt * P:(dt + 1) * P],
                                               h[:, (s + 1) % 2, dt, lt * P:(lt + 1) * P], ident[:, :])
                last.then_inc(s_hT, 1)

            def quarter(t, qq):
                first = first_q(qq)
                k = chunk(t, qq)
                for s in range(SPQ):
                    for p in range(LT):
                        if has_tail(t, qq, s):
                            if p == 0:
                                h_transposed(t, qq, s, 0)
                            if p + 1 < LT:
                                h_transposed(t, qq, s, p + 1)
                        if has_pre(t):
                            def fill(use, needs=0):
                                wait(pe, s_ppf, pre_empty(t, k, use, needs))
                                return pre_bank(t, use)

                            if at("hnT", t, s, p):
                                pe.wait_ge(s_hn, k + 1)
                                bank = fill(0)
                                for kk in range(KD):
                                    for j in range(JC):
                                        last = nc.tensor.transpose(bank[:, kk * CH + j * P:kk * CH + (j + 1) * P],
                                                                   hn[:, j, kk * P:(kk + 1) * P], ident[:, :])
                                last.then_inc(s_pp, 1)
                            for u in range(2):
                                if at(f"in{u}", t, s, p) or at(f"res{u}", t, s, p):
                                    gate = at(f"res{u}", t, s, p)
                                    bank = fill((5 if gate else 1) + u, 1)
                                    for half in range(2):
                                        col = (DI if gate else 0) + (2 * u + half) * P
                                        for kk in range(KD):
                                            last = nc.tensor.matmul(bank[:, half * CH:(half + 1) * CH], w_in[:, kk, col:col + P],
                                                                    hnT[:, kk, :], start=(kk == 0), stop=(kk == KD - 1))
                                    last.then_inc(s_pp, 1)
                                for half, step in enumerate((f"conv{u}", f"conv{u}b")):
                                    if at(step, t, s, p):
                                        kk = 2 * u + half
                                        bank = fill(3 + u, 2 + u) if half == 0 else pre_bank(t, 3 + u)
                                        for tap in range(KC):
                                            last = nc.tensor.matmul(bank[:, half * CH:(half + 1) * CH], diag_w[:, kk, tap, :],
                                                                    xpre[:, kk, tap:tap + CH],
                                                                    start=(tap == 0), stop=(tap == KC - 1))
                                        if half:
                                            last.then_inc(s_pp, 1)
                            if at("xproj", t, s, p):
                                bank = fill(7)
                                pe.wait_ge(s_xs, 2 * k + 1)
                                for kk in range(KI):
                                    nc.tensor.matmul(bank[:, 0:CH], w_x[:, kk, 0:R], xs[:, kk, :],
                                                     start=(kk == 0), stop=(kk == KI - 1))
                            if at("xprojb", t, s, p):
                                bank = pre_bank(t, 7)
                                for kk in range(KI):
                                    last = nc.tensor.matmul(bank[0:NS, CH:2 * CH], w_x[:, kk, R:R + NS], xs[:, kk, :],
                                                            start=(kk == 0), stop=(kk == KI - 1))
                                last.then_inc(s_pp, 1)
                            if at("cproj", t, s, p):
                                bank = fill(8)
                                for j in range(JC):
                                    for kk in range(KI):
                                        last = nc.tensor.matmul(bank[:, j * NS:(j + 1) * NS], xs[:, kk, j * P:(j + 1) * P],
                                                                w_x[:, kk, R + NS:R + 2 * NS],
                                                                start=(kk == 0), stop=(kk == KI - 1))
                                last.then_inc(s_pp, 1)
                            for u in range(2):
                                if at(f"dt{u}", t, s, p):
                                    bank = fill(9 + u, 8)
                                    for kk in (2 * u, 2 * u + 1):
                                        last = nc.tensor.matmul(bank[:, (kk % 2) * CH:(kk % 2 + 1) * CH],
                                                                w_dt[:, kk * P:(kk + 1) * P], dr[:, :], start=True, stop=True)
                                    last.then_inc(s_pp, 1)
                        if has_b(t, qq):
                            if at("up0", t, s, p):
                                pe.wait_ge(s_ew, 64 * (t - 2 if first else t - 1))
                                expert_up(t, qq, 0)
                            if at("up1", t, s, p):
                                expert_up(t, qq, 1)
                            if at("down", t, s, p):
                                expert_down(t, qq, 0)
                            if at("downb", t, s, p):
                                expert_down(t, qq, 1)
                            if at("eout", t, s, p):
                                if not first:
                                    pe.wait_ge(s_wof, t - 1)
                                    pe.wait_ge(s_dg, t - 1)
                                    pe.wait_ge(s_bo, 16 * (t - 1))
                                expert_out(t, qq, 0)
                            if at("eoutb", t, s, p):
                                expert_out(t, qq, 1)
                        if has_a(t):
                            m = piece(t, qq)
                            for u in range(2):
                                if at(f"yT{u}", t, s, p):
                                    if u == 0:
                                        pe.wait_ge(s_yc, 16 * (m + 1))
                                        wait(pe, s_fin, m)
                                    else:
                                        pe.wait_ge(s_ud, KI * m + 2)
                                    for kk in (2 * u, 2 * u + 1):
                                        for j in range(JC):
                                            last = nc.tensor.transpose(
                                                pq[:, (kk % 2) * CH + j * P:(kk % 2) * CH + (j + 1) * P],
                                                y_c[:, j, kk * P:(kk + 1) * P], ident[:, :])
                                    last.then_inc(s_pq, 1)
                            for j, step in enumerate(("oproj", "oprojb")):
                                if at(step, t, s, p):
                                    if j == 0:
                                        pe.wait_ge(s_gate, m + 1)
                                        pe.wait_ge(s_wf, t - 1)
                                    for kk in range(KI):
                                        last = nc.tensor.matmul(pq[:, j * D:(j + 1) * D], yg[:, kk, j * P:(j + 1) * P],
                                                                w_out[:, kk, :], start=(kk == 0), stop=(kk == KI - 1))
                                    if j == JC - 1:
                                        last.then_inc(s_pq, 1)
                            if at("xhT", t, s, p):
                                pe.wait_ge(s_xh, m + 1)
                                for kk in range(KD):
                                    for j in range(JC):
                                        last = nc.tensor.transpose(pq[:, kk * CH + j * P:kk * CH + (j + 1) * P],
                                                                   xh[:, j, kk * P:(kk + 1) * P], ident[:, :])
                                last.then_inc(s_pq, 1)
                            if first and at("sel0", t, s, p):
                                pe.wait_ge(s_h2, m + 1)
                                for kk in range(KD):
                                    last = nc.tensor.matmul(pq[:, 0:1], w_p1[:, kk, :], h2T[:, kk, CH - 1:CH],
                                                            start=(kk == 0), stop=(kk == KD - 1))
                                last.then_inc(s_pq, 1)
                            if first and at("sel1", t, s, p):
                                pe.wait_ge(s_nav, t - 1)
                                nc.tensor.matmul(pq[0:1, 0:NE], nav[:, :], w_p2[:, :], start=True, stop=True).then_inc(s_pq, 1)

            def flush():
                t, qq = NB + 2, 0
                expert_up(t, qq, 0)
                expert_up(t, qq, 1)
                for half in range(2):
                    expert_down(t, qq, half)
                for half in range(2):
                    expert_out(t, qq, half)

            sections(pe, quarter, flush)


INPUTS = [
    "L0_attn_x", "L0_attn_norm_w", "L0_attn_norm_b", "L0_attn_in_proj_w", "L0_attn_conv_w", "L0_attn_conv_b",
    "L0_attn_x_proj_w", "L0_attn_dt_proj_w", "L0_attn_dt_proj_b", "L0_attn_A_log", "L0_attn_D_param",
    "L0_attn_out_proj_w", "L0_ffn_Wp1", "L0_ffn_bp1", "L0_ffn_Wp2", "L0_ffn_bp2", "L0_ffn_W1", "L0_ffn_b1",
    "L0_ffn_W2", "L0_ffn_b2", "L0_ffn_Wo", "L0_ffn_bo", "L0_c", "L0_wmod",
]


def kernel(**inputs):
    import numpy as np
    import concourse.bacc as bacc
    from concourse.bass_utils import run_bass_kernel_spmd

    nc = bacc.Bacc("TRN2", target_bir_lowering=False, num_devices=1)
    arrays, args = {}, []
    for name in INPUTS:
        a = np.ascontiguousarray(inputs[name])
        arrays[f"in_{name}"] = a
        args.append(nc.dram_tensor(f"in_{name}", a.shape, mybir.dt.from_np(a.dtype), kind="ExternalInput").ap())
    args.append(nc.dram_tensor("out_0", (NB, L, D), F32, kind="ExternalOutput").ap())
    build(nc, *args)
    result = run_bass_kernel_spmd(nc, [arrays], core_ids=[0])
    return result.results[0]["out_0"]
```

```python
from contextlib import ExitStack

import concourse.bass as bass
from concourse import mybir

F32 = mybir.dt.float32
I32 = mybir.dt.int32
ACT = mybir.ActivationFunctionType
ALU = mybir.AluOpType
AX_X = mybir.AxisListType.X
ds = bass.ds

P = 128
NB, L, D = 4, 1024, 256
DI, NS, R, KC = 512, 16, 128, 4
NE, F = 8, 512
EPS = 1e-5
KD, KI = D // P, DI // P
CH = 256
JC = CH // P
NQ = L // CH
SPQ = NS // NQ
LT = L // P
NM = 8
VEC_LT = [0, 2, 3, 4, 6, 7]
ACT_LT = [1, 5]
ADD_LAG = 2
DU_B_POS = [0, 1, 3, 5]
EXP_POS = [0, 2, 4, 6]
SCAN_POS = [1, 3, 5, 7]
TURN_POS = [0, 0, 1, 2, 3, 4, 5, 6]
ADD_POS = [0, 1, 2, 3, 4, 5, 6, 7]
NV, NA = len(VEC_LT), len(ACT_LT)
QR = 4
PRE_USES = 11
B_FREE = 3
SEL_STEPS = 10

POS = dict(
    ln1=0, ln1_rs=0, ln2=0, ln2_rs=3, hn=4, hx=6, hnT=5, hnT_out=6,
    in0=6, in0_out=8, in1=10, in1_out=11, conv0=11, conv0b=12, conv0_out=14, conv1=14, conv1b=15, conv1_out=16,
    res0=16, res0_out=17, res1=17, res1_out=19, silu_x=20, silu_g=20, xproj=21, xprojb=22, xproj_out=23,
    cproj=24, cproj_out=25, dt0=25, dt0_out=26, dt1=27, dt1_out=28, softplus=29, delta=31, du=31,
    up0=0, up0_out=1, up1=2, up1_out=2, gelu=2, down=4, downb=5, down_out=6, eout=8, eoutb=10, fin=12, w_o=13, diag=13,
    w_out=9, yT0=13, yT0_out=13, yT1=14, yT1_out=15, gate=16, oproj=18, oprojb=20, x1=21, x1_rs=23, xh=27,
    xhT=28, xhT_out=30, sel0=30, sel0_out=30, sel1=31, sel1_out=31, sel_exp=31, sel=31,
)
FIRST = dict(POS, conv1_out=15, res0_out=16, up0=1, down=3, fin=11, w_o=12, diag=12, yT0=12,
             yT0_out=12, yT1=13, yT1_out=14, x1_rs=22, xh=24)
POS0 = dict(POS, in0=1, in1=2, in0_out=2, in1_out=3, ln1=1, conv0=4, conv0b=4, ln1_rs=4, ln2=4, conv0_out=5,
            conv1=5, conv1b=5, conv1_out=6, ln2_rs=7, silu_x=7, res0=6, res1=7, hx=7, hn=8, res0_out=8, res1_out=9,
            silu_g=10, xproj=12, xprojb=12, xproj_out=13, cproj=13, cproj_out=14,
            dt0=17, dt0_out=18, dt1=18, dt1_out=19, hnT=19, hnT_out=19, softplus=20, delta=21, du=22)
PRE_BANKS = {0: 4, 1: 2}

B_STEPS = ("up0", "up0_out", "up1", "up1_out", "gelu", "down", "downb", "down_out", "eout", "eoutb", "fin")
A_STEPS = ("w_out", "yT0", "yT0_out", "yT1", "yT1_out", "gate", "oproj", "oprojb", "x1", "x1_rs", "xh", "xhT", "xhT_out")
FIRST_STEPS = ("w_o", "diag", "sel0", "sel0_out", "sel1", "sel1_out", "sel_exp", "sel")


def last_order():
    def steps(names, r):
        return [(name, r) for name in names.split()]
    y_in, up = "yT0 yT1 yT0_out yT1_out gate", "up0 up0_out up1 up1_out"
    order = steps("w_out " + y_in, 0) + steps(y_in, 1) + steps(up + " gelu oproj oprojb tables x1 down x1_rs downb xh"
                                                               " down_out xhT xhT_out", 0)
    order += steps("yT0 yT1", 2) + steps("sel0 sel0_out", 0) + steps("yT0_out yT1_out gate", 2)
    order += steps("oproj oprojb", 1) + steps("sel1 sel1_out sel_exp", 0) + steps("x1", 1)
    order += steps("sel eout eoutb fin w_o diag", 0) + steps("x1_rs xh xhT xhT_out", 1)
    order += steps("oproj oprojb", 2) + steps("yT0 yT1", 3) + steps("x1 x1_rs", 2) + steps("yT0_out yT1_out gate", 3)
    order += steps("xh", 2) + steps(up, 1) + steps("xhT xhT_out", 2) + steps("oproj oprojb x1", 3) + steps("gelu", 1)
    order += steps("tables x1_rs xh", 3) + steps("down downb down_out", 1) + steps(up, 2) + steps("xhT xhT_out", 3)
    order += steps("gelu", 2) + steps("eout eoutb fin", 1)
    for b in range(2, NQ + 1):
        if b < NQ:
            order += steps(up + " gelu", b + 1)
        order += steps("down downb down_out eout eoutb fin", b)
    return order


WEIGHTS = 13
LAST = NB + 1
ORDER = last_order()


def build(nc, x, norm_w, norm_b, in_proj_w, conv_w, conv_b, x_proj_w, dt_proj_w, dt_proj_b, A_log, D_param,
          out_proj_w, Wp1, bp1, Wp2, bp2, W1, b1, W2, b2, Wo, bo, c, wmod, out):
    ctx = ExitStack()
    with ctx:
        def sb(name, shape, dt=F32):
            return ctx.enter_context(nc.sbuf_tensor(name, shape, dt))

        def pb_(name, shape):
            return ctx.enter_context(nc.psum_tensor(name, shape, F32))

        def sem(name):
            return ctx.enter_context(nc.semaphore(name))

        x_rows = x.rearrange("b l d -> (b l) d")
        out_rows = out.rearrange("b l d -> (b l) d")
        mods_d = nc.dram_tensor("mods_d", (NB, NM * D), F32).ap()
        brow_d = nc.dram_tensor("brow_d", (NB * NS + 1, L), F32).ap()
        hx_d = nc.dram_tensor("hx_d", (NB * L, D), F32).ap()
        y_d = nc.dram_tensor("y_d", (NB * L, DI), F32).ap()
        xs_d = nc.dram_tensor("xs_d", (NB * P, KI, L), F32).ap()
        delta_d = nc.dram_tensor("delta_d", (NB * P, KI, L), F32).ap()
        du_d = nc.dram_tensor("du_d", (NB * P, KI, L), F32).ap()
        sres_d = nc.dram_tensor("sres_d", (NB * P, KI, L), F32).ap()

        w_in = sb("w_in", [P, KD, 2 * DI])
        w_x = sb("w_x", [P, KI, R + 2 * NS])
        w_dt = sb("w_dt", [P, DI])
        w_out = sb("w_out", [P, KI, D])
        w_p1 = sb("w_p1", [P, KD, P])
        w_p2 = sb("w_p2", [P, NE])
        w_o = sb("w_o", [P, KD, D])
        w_1 = sb("w_1", [P, KD, F])
        w_2 = sb("w_2", [P, F // P, D])
        b1_c = sb("b1_c", [P, F // P])
        b2_c = sb("b2_c", [P, KD])
        nw_c = sb("nw_c", [P, KD])
        nb_c = sb("nb_c", [P, KD])
        cw_c = sb("cw_c", [P, KI, KC])
        cb_c = sb("cb_c", [P, KI])
        dtb_c = sb("dtb_c", [P, KI])
        D_c = sb("D_c", [P, KI])
        bp1_c = sb("bp1_c", [P, 1])
        bp2_r = sb("bp2_r", [1, NE])
        A_c = sb("A_c", [P, KI, NS])
        c_T = sb("c_T", [P, KD, NB])
        eps_c = sb("eps_c", [P, 1])
        ident = sb("ident", [P, P])
        iota8 = sb("iota8", [1, NE])
        pre_row = sb("pre_row", [P, 3 * D])
        post_row = sb("post_row", [P, 2 * D])
        post_col = sb("post_col", [P, 3, KD])
        bo_row = sb("bo_row", [1, D])
        ones = sb("ones", [1, P])
        diag_gb = sb("diag_gb", [P, KD, D])
        diag_w = sb("diag_w", [P, KI, KC, P])
        delta = sb("delta", [P, KI, L])
        du = sb("du", [P, KI, L])
        C_t = sb("C_t", [P, 2, LT, NS])
        b_bc = sb("b_bc", [P, 2, L])
        h = sb("h", [P, 2, KI, L])
        y = sb("y", [P, LT, DI])
        q = sb("q", [P, QR, DI])
        x_t = sb("x_t", [P, JC, D])
        hm = sb("hm", [P, JC, D])
        hn = sb("hn", [P, JC, D])
        hx = sb("hx", [P, JC, D])
        hnT = sb("hnT", [P, KD, CH])
        xpre = sb("xpre", [P, KI, CH + KC - 1])
        xs = sb("xs", [P, KI, CH])
        sres = sb("sres", [P, KI, CH])
        dr = sb("dr", [P, CH])
        b_T = sb("b_T", [NS, CH])
        delta_c = sb("delta_c", [P, KI, CH])
        du_c = sb("du_c", [P, KI, CH])
        st_p = sb("st_p", [P, JC, 6])
        mv_p = sb("mv_p", [P, JC, 2])
        rs_p = sb("rs_p", [P, 3, JC])
        y_c = sb("y_c", [P, JC, DI])
        yg = sb("yg", [P, KI, CH])
        sres_c = sb("sres_c", [P, KI, CH])
        hx_c = sb("hx_c", [P, JC, D])
        g = sb("g", [P, F // P, CH])
        x1 = sb("x1", [P, JC, D])
        h2T = sb("h2T", [P, KD, CH])
        r_T = sb("r_T", [P, KD, CH])
        st_a = sb("st_a", [P, JC, 6])
        mv_a = sb("mv_a", [P, JC, 2])
        rs_a = sb("rs_a", [P, 3, JC])
        nav = sb("nav", [P, 1])
        sel = sb("sel", [1, 8, NE])
        sel_i = sb("sel_i", [1, 1], I32)

        pA = [pb_(f"pA{i}", [P, L]) for i in range(2)]
        pH = [pb_(f"pH{i}", [P, DI]) for i in range(2)]
        pp = pb_("pp", [P, 512])
        pq = pb_("pq", [P, 512])

        s_cw, s_wm2, s_m0, s_prow0 = sem("s_cw"), sem("s_wm2"), sem("s_m0"), sem("s_prow0")
        s_wt, s_cT, s_wm, s_id0, s_id = sem("s_wt"), sem("s_cT"), sem("s_wm"), sem("s_id0"), sem("s_id")
        s_cs, s_mod, s_modv, s_modw, s_Aexp, s_const = (sem("s_cs"), sem("s_mod"), sem("s_modv"), sem("s_modw"),
                                                        sem("s_Aexp"), sem("s_const"))
        s_vec0 = sem("s_vec0")
        s_pad = sem("s_pad")
        s_b, s_dbu, s_dA, s_scan, s_hT = sem("s_b"), sem("s_dbu"), sem("s_dA"), sem("s_scan"), sem("s_hT")
        s_yv, s_qa, s_yg = sem("s_yv"), sem("s_qa"), sem("s_yg")
        s_ysp = sem("s_ysp")
        s_prow, s_x, s_pst, s_prs, s_hm, s_hn, s_hx, s_hxd = (sem("s_prow"), sem("s_x"), sem("s_pst"), sem("s_prs"),
                                                              sem("s_hm"), sem("s_hn"), sem("s_hx"), sem("s_hxd"))
        s_pchain, s_hxc = sem("s_pchain"), sem("s_hxc")
        s_pp, s_ppf = sem("s_pp"), sem("s_ppf")
        s_move, s_xs, s_sres, s_xsd, s_sresd, s_bTd = (sem("s_move"), sem("s_xs"), sem("s_sres"), sem("s_xsd"),
                                                             sem("s_sresd"), sem("s_bTd"))
        s_lp, s_dl, s_du = sem("s_lp"), sem("s_dl"), sem("s_du")
        s_dld, s_dud = sem("s_dld"), sem("s_dud")
        s_dli = [sem(f"s_dli{dt}") for dt in range(KI)]
        s_dui = [sem(f"s_dui{dt}") for dt in range(KI)]
        s_dgw = sem("s_dgw")
        s_qrow, s_wl, s_wf, s_yc, s_xc, s_sc, s_hc = (sem("s_qrow"), sem("s_wl"), sem("s_wf"), sem("s_yc"),
                                                      sem("s_xc"), sem("s_sc"), sem("s_hc"))
        s_pq, s_pqf = sem("s_pq"), sem("s_pqf")
        s_ud, s_gate, s_x1, s_ast, s_ars, s_xh, s_h2, s_dg0, s_dg = (sem("s_ud"), sem("s_gate"), sem("s_x1"),
                                                                     sem("s_ast"), sem("s_ars"), sem("s_xh"),
                                                                     sem("s_h2"), sem("s_dg0"), sem("s_dg"))
        s_achain = sem("s_achain")
        s_nav, s_se, s_schain, s_si, s_ew, s_g, s_rT, s_fin, s_out = (sem("s_nav"), sem("s_se"), sem("s_schain"),
                                                                      sem("s_si"), sem("s_ew"), sem("s_g"),
                                                                      sem("s_rT"), sem("s_fin"), sem("s_out"))
        s_wo = sem("s_wo")
        s_wof = sem("s_wof")
        s_bo = sem("s_bo")

        def wait(eng, s, value):
            if not (isinstance(value, int) and value <= 0):
                eng.wait_ge(s, value)

        def first_q(qq):
            return isinstance(qq, int) and qq == 0

        def sections(eng, quarter, ab):
            for qq in range(NQ):
                quarter(0, qq)
            for t in range(1, LAST):
                quarter(t, 0)
                with eng.Fori(1, NQ) as qq:
                    quarter(t, qq)
            quarter(LAST, 0)
            for step, qq in ORDER:
                ab(step, LAST, qq)

        def has_pre(t):
            return t < NB

        def has_scan(t):
            return 1 <= t <= NB

        def has_a(t):
            return t >= 2

        def has_b(t, qq):
            return t >= 3 or (t == 2 and not first_q(qq))

        def has_tail(t, qq, s):
            if first_q(qq) and s == 0:
                return 2 <= t <= LAST
            return has_scan(t)

        def chunk(t, qq):
            return NQ * t + qq

        def slot(t, qq, s):
            return SPQ * (NQ * (t - 1) + qq) + s

        def piece(t, qq):
            return NQ * (t - 2) + qq

        def piece_q(qq):
            return NQ - 1 if first_q(qq) else qq - 1

        def sel_before(t, qq):
            return (t - 2) + (0 if first_q(qq) else 1)

        def b_use(t, qq):
            return 8 * piece(t, qq) - 4 + 2 * sel_before(t, qq)

        def a_use(t, qq):
            return b_use(t, qq) + 4

        def q_of(rank, s):
            return q[:, (NA * ((s - 1) % SPQ) + rank) % QR, :]

        def piece_delta(t, qq):
            if t == 0:
                return delta[:, :, qq * CH:(qq + 1) * CH], du[:, :, qq * CH:(qq + 1) * CH]
            return delta_c[:, :, :], du_c[:, :, :]

        hf = h[:, 1, :, :].rearrange("p k l -> p (k l)")
        xf = delta[:, :, :].rearrange("p k l -> p (k l)")

        def place(flat, i, a):
            return flat[:, i * JC * D:(i + 1) * JC * D].rearrange("p (a c) -> p a c", a=a)

        class Work:
            def __init__(self, t, qq):
                if t < LAST:
                    self.y, self.yg, self.sres, self.hx = y_c, yg, sres_c, hx_c
                    self.x1, self.xh, self.h2T, self.r_T, self.g = x1, g[:, 0:JC, :], h2T, r_T, g
                    return
                pq_ = piece_q(qq)
                self.y = y[:, pq_ * JC:(pq_ + 1) * JC, :]
                self.yg = h[:, 0, :, pq_ * CH:(pq_ + 1) * CH]
                self.sres = du[:, :, pq_ * CH:(pq_ + 1) * CH]
                self.hx = place(xf, pq_, JC)
                self.x1 = place(xf, NQ + qq, JC)
                self.h2T, self.xh = place(hf, qq, KD), place(hf, NQ + qq, JC)
                self.r_T = (x_t, hm, hn, hx)[qq]
                self.g = (xs, sres, delta_c, du_c)[qq]

        def a_work(t, qq):
            return Work(t, qq) if t < LAST or qq < NQ else None

        def b_work(t, qq):
            return Work(LAST, qq - 1) if t == LAST and not first_q(qq) else Work(0, 0)

        def ab_bank(t, step):
            if t < NB:
                return pq
            if t == NB:
                return dict(up0=pp, up1=pq, down=pp, eout=pq, yT0=pp, yT1=pq, oproj=pp, xhT=pq, sel0=pp, sel1=pq)[step]
            return dict(up0=pA[1][:, 0:512], up1=pA[1][:, 512:1024], down=pq, eout=pH[0], yT0=pA[0][:, 0:512],
                        yT1=pA[0][:, 512:1024], oproj=pp, xhT=pH[1], sel0=pq, sel1=pq)[step]

        def ab_steps(t, qq, s, p):
            names = B_STEPS if has_b(t, qq) else ()
            if has_a(t):
                names += A_STEPS[0 if first_q(qq) else 1:] + (FIRST_STEPS if first_q(qq) else ())
            return [step for step in names if at(step, t, qq, s, p)]

        def filled(step, t, qq):
            if t < LAST:
                names = ("up0", "up1", "down", "eout", "yT0", "yT1", "oproj", "xhT", "sel0", "sel1")
                return b_use(t, qq) + 1 + names.index(step)
            fills = [o for o in ORDER if o[0] in ("up0", "up1", "downb", "eoutb", "yT0", "yT1", "oprojb", "xhT", "sel0", "sel1")]
            last = step + "b" if step in ("down", "eout", "oproj") else step
            return b_use(LAST, 0) + 1 + fills.index((last, qq))

        def b_emptied(step, t, qq):
            if t < LAST:
                return B_FREE * (piece(t, qq) - 1) + 1 + ("up0", "up1", "down").index(step)
            outs = [o for o in ORDER if o[0] in ("up0_out", "up1_out", "down_out")]
            return B_FREE * (piece(LAST, 0) - 1) + 1 + outs.index((step + "_out", qq))

        def loaded(t, m):
            return 16 * (piece(LAST, 0) + 1 if t == LAST else m + 1)

        def at(step, t, qq, s, p):
            return (POS0 if t == 0 else FIRST if first_q(qq) else POS)[step] == s * LT + p

        def mod_bank(i):
            return pA[i // 2][:, (i % 2) * 512:(i % 2 + 1) * 512]

        def pre_bank(t, use):
            return (pp, pq, pH[0], pH[1])[use % PRE_BANKS.get(t, 1)]

        def pre_empty(t, k, use, needs=-PRE_USES):
            banks = PRE_BANKS.get(t, 1)
            last = use - banks
            if last < 0:
                last = max(u for u in range(PRE_USES) if u % banks == use % banks) - PRE_USES
            return PRE_USES * k + max(last + 1, needs)

        def ln_piece(t, qq):
            return chunk(t, qq) if t else qq + 1

        def has_ln(t, qq):
            return has_pre(t) and (t > 0 or qq + 1 < NQ)

        def added(i, n, batch, rank):
            if isinstance(n, int) and n < 0:
                n, batch = n + NS, batch - 1
            if isinstance(n, int) and n == 0:
                return NA * (i - batch)
            return NA * (i - batch - 1) + rank + 1

        def channels_at(t, where, p):
            return [dt for dt in range(KI) if where[dt] == p] if has_scan(t) else []

        def tiles_at(t, qq, s, p, tiles):
            return [lt for lt in tiles if ADD_POS[lt] == p] if has_tail(t, qq, s) else []

        def consumed(lt):
            return (s_yv, NV, VEC_LT.index(lt)) if lt in VEC_LT else (s_qa, NA, ACT_LT.index(lt))

        ctx.enter_context(nc.allow_non_contiguous_dma(reason="vectors of a few hundred values, one per partition"))
        block = ctx.enter_context(nc.Block())

        @block.sync
        def _(sp):
            hflat = h[:, :, :, :].rearrange("p a k l -> p (a k l)")
            yflat = y[:, :, :].rearrange("p a k -> p (a k)")
            sp.dma_start(x_t[:, :, :], x_rows[0:CH, :].rearrange("(j p) d -> p j d", p=P)).then_inc(s_x, 16)
            for kk in range(KD):
                sp.dma_start(c_T[:, kk, :], c[:, kk * P:(kk + 1) * P].rearrange("b p -> p b")).then_inc(s_cT, 16)
            wm = hflat[:, 0:KD * 6 * D].rearrange("p (k n) -> p k n", k=KD)
            wm_src = wmod.rearrange("(k p) n -> p k n", p=P)
            sp.dma_start(wm[:, :, 0:2 * D], wm_src[:, :, 0:2 * D]).then_inc(s_wm, 16)
            sp.dma_start(cw_c[:, :, :], conv_w.rearrange("(k p) n -> p k n", p=P)).then_inc(s_cw, 16)
            for dst, src in (
                (w_in[:, :, :], in_proj_w.rearrange("(k p) n -> p k n", p=P)),
                (w_x[:, :, :], x_proj_w.rearrange("(k p) n -> p k n", p=P)),
                (w_dt[:, :], dt_proj_w),
                (w_p1[:, :, :], Wp1.rearrange("(k p) n -> p k n", p=P)),
                (w_p2[:, :], Wp2),
                (nw_c[:, :], norm_w.rearrange("(k p) -> p k", p=P)),
                (nb_c[:, :], norm_b.rearrange("(k p) -> p k", p=P)),
                (cb_c[:, :], conv_b.rearrange("(k p) -> p k", p=P)),
                (dtb_c[:, :], dt_proj_b.rearrange("(k p) -> p k", p=P)),
                (D_c[:, :], D_param.rearrange("(k p) -> p k", p=P)),
                (bp1_c[:, :], bp1.rearrange("(p k) -> p k", k=1)),
                (bp2_r[:, :], bp2.rearrange("(p k) -> p k", p=1)),
                (A_c[:, :, :], A_log.rearrange("(k p) n -> p k n", p=P)),
            ):
                sp.dma_start(dst, src).then_inc(s_wt, 16)
            sp.dma_start(wm[:, :, 2 * D:], wm_src[:, :, 2 * D:]).then_inc(s_wm2, 16)
            sp.dma_start(yflat[0:NB, 3584:3584 + D], bo[None, :].to_broadcast((NB, D))).then_inc(s_wm2, 16)
            sp.dma_start(brow_d[NB * NS:NB * NS + 1, :], x_rows[0:L // D, :].rearrange("(o a) d -> o (a d)", o=1)
                         ).then_inc(s_pad, 16)
            sp.wait_ge(s_modv, 1)
            sp.dma_start(mods_d, yflat[0:NB, 1536:1536 + NM * D]).then_inc(s_modw, 16)
            sp.wait_ge(s_modw, 16)

            def load_pre_row(t):
                wait(sp, s_hx, NQ * t)
                have = 0 if t else 2 * D
                sp.dma_start(pre_row[:, have:3 * D], mods_d[t:t + 1, have:3 * D].to_broadcast((P, 3 * D - have))
                             ).then_inc(s_prow, 16)

            def load_x(t, qq, k):
                tok = k * CH
                if t == NB - 1:
                    tok = (NB - 1) * L + (0 if first_q(qq + 1) else (qq + 1) % NQ) * CH
                sp.dma_start(x_t[:, :, :], x_rows[ds(tok, CH), :].rearrange("(j p) d -> p j d", p=P)).then_inc(s_x, 16)

            def store_hx(k):
                sp.wait_ge(s_hx, k + 1)
                sp.dma_start(hx_d[ds(k * CH, CH), :].rearrange("(j p) d -> p j d", p=P), hx[:, :, :]
                             ).then_inc(s_hxd, 16)

            load_pre_row(0)
            store_hx(0)
            load_x(0, 0, 1)

            def quarter(t, qq):
                first = first_q(qq)
                k = chunk(t, qq)
                if has_scan(t) and first and t > 1:
                    rows, last = slice((t - 1) * P, t * P), (NQ - 1) * CH
                    sp.wait_ge(s_dld, 16 * (NQ - 1) * (t - 1))
                    sp.wait_ge(s_dud, 16 * (NQ - 1) * (t - 1))
                    for dt in range(KI):
                        done = KI * (NS * (t - 1) - 1) + dt + 1
                        sp.wait_ge(s_dA, done)
                        sp.dma_start(delta[:, dt, 0:last], delta_d[rows, dt, 0:last]).then_inc(s_dli[dt], 16)
                        sp.wait_ge(s_dbu, done)
                        sp.dma_start(du[:, dt, 0:last], du_d[rows, dt, 0:last]).then_inc(s_dui[dt], 16)
                    sp.wait_ge(s_dl, k)
                    for dt in range(KI):
                        sp.dma_start(delta[:, dt, last:], delta_c[:, dt, :]).then_inc(s_dli[dt], 16)
                    sp.wait_ge(s_du, k)
                    for dt in range(KI):
                        sp.dma_start(du[:, dt, last:], du_c[:, dt, :]).then_inc(s_dui[dt], 16)
                if has_pre(t) and t > 0 and not first:
                    rows, at_l = slice(t * P, (t + 1) * P), (qq - 1) * CH
                    sp.wait_ge(s_dl, k)
                    sp.dma_start(delta_d[rows, :, ds(at_l, CH)], delta_c[:, :, :]).then_inc(s_dld, 16)
                    sp.wait_ge(s_du, k)
                    sp.dma_start(du_d[rows, :, ds(at_l, CH)], du_c[:, :, :]).then_inc(s_dud, 16)
                if has_pre(t) and t > 0 and first:
                    load_pre_row(t)
                if has_tail(t, qq, 0) and first and t < LAST:
                    for lt in range(LT):
                        if lt in VEC_LT:
                            sp.wait_ge(s_yv, NV * (NS * (t - 1) - 1) + VEC_LT.index(lt) + 1)
                        else:
                            sp.wait_ge(s_yg, NA * ((NS - 1) * (t - 1) - 1) + ACT_LT.index(lt) + 1)
                        tok = (t - 2) * L + lt * P
                        sp.dma_start(y_d[tok:tok + P, :], y[:, lt, :]).then_inc(s_ysp, 16)
                if has_a(t) and first:
                    m = piece(t, 0)
                    wait(sp, s_wof, t - 2)
                    wait(sp, s_h2, m)
                    wait(sp, s_dg, t - 2)
                    sp.dma_start(post_row[:, :], mods_d[t - 2:t - 1, 2 * D:4 * D].to_broadcast((P, 2 * D))
                                 ).then_inc(s_qrow, 16)
                    sp.dma_start(post_col[:, :, :].rearrange("p c k -> p (c k)"),
                                 mods_d[t - 2, 5 * D:8 * D].rearrange("(n p) -> p n", p=P)).then_inc(s_qrow, 16)
                    wait(sp, s_x1, m)
                    sp.dma_start(w_out[:, :, :], out_proj_w.rearrange("(k p) n -> p k n", p=P)).then_inc(s_wl, 16)
                if t == LAST:
                    rows = slice((NB - 1) * P, NB * P)
                    sp.wait_ge(s_xsd, 16 * NQ * NB)
                    sp.wait_ge(s_sresd, 16 * NQ * NB)
                    sp.wait_ge(s_hxd, 16 * NQ * NB)
                    sp.wait_ge(s_hT, LT * (NB * NS - 1))
                    sp.dma_start(h[:, 0, :, :], xs_d[rows, :, :]).then_inc(s_xc, 16)
                    sp.wait_ge(s_dbu, KI * NB * NS)
                    sp.dma_start(du[:, :, :], sres_d[rows, :, :]).then_inc(s_sc, 16)
                    sp.wait_ge(s_dA, KI * NB * NS)
                    sp.dma_start(xf[:, 0:LT * D].rearrange("p (j d) -> p j d", j=LT),
                                 hx_d[(NB - 1) * L:NB * L, :].rearrange("(j p) d -> p j d", p=P)).then_inc(s_hc, 16)
                elif has_a(t):
                    m, pq_ = piece(t, qq), piece_q(qq)
                    if first:
                        sp.wait_ge(s_ysp, 16 * LT * (t - 1))
                        sp.wait_ge(s_xsd, 16 * NQ * (t - 1))
                        sp.wait_ge(s_sresd, 16 * NQ * (t - 1))
                        sp.wait_ge(s_hxd, 16 * NQ * (t - 1))
                    wait(sp, s_x1, m)
                    tok = (t - 2) * L + pq_ * CH
                    sp.dma_start(y_c[:, :, :], y_d[ds(tok, CH), :].rearrange("(j p) d -> p j d", p=P)).then_inc(s_yc, 16)
                    rows = slice((t - 2) * P, (t - 1) * P)
                    sp.dma_start(yg[:, :, :], xs_d[rows, :, ds(pq_ * CH, CH)]).then_inc(s_xc, 16)
                    sp.dma_start(sres_c[:, :, :], sres_d[rows, :, ds(pq_ * CH, CH)]).then_inc(s_sc, 16)
                    sp.dma_start(hx_c[:, :, :], hx_d[ds(tok, CH), :].rearrange("(j p) d -> p j d", p=P)).then_inc(s_hc, 16)
                if has_pre(t) and t > 0:
                    store_hx(k)
                    load_x(t, qq, k + 1)
                if t == LAST:
                    load_expert(t)
                if has_b(t, qq):
                    store(t, qq)
                if has_a(t) and first:
                    sp.dma_start(w_o[:, :, :], Wo.rearrange("(k p) n -> p k n", p=P)).then_inc(s_wo, 16)
                    sp.dma_start(bo_row[:, :], mods_d[t - 2:t - 1, 4 * D:5 * D]).then_inc(s_bo, 16)
                if has_pre(t):
                    rows = slice(t * P, (t + 1) * P)
                    at_l = qq * CH
                    sp.wait_ge(s_xs, 2 * k + 2)
                    sp.dma_start(xs_d[rows, :, ds(at_l, CH)], xs[:, :, :]).then_inc(s_xsd, 16)
                    sp.dma_start(sres_d[rows, :, ds(at_l, CH)], sres[:, :, :]).then_inc(s_sresd, 16)
                    if has_ln(t, qq) and t == 0:
                        store_hx(k + 1)
                        load_x(t, qq, k + 2)
                    sp.wait_ge(s_ppf, PRE_USES * k + 8)
                    sp.dma_start(brow_d[t * NS:(t + 1) * NS, ds(at_l, CH)], b_T[:, :]).then_inc(s_bTd, 16)
                if has_a(t) and first and t < LAST:
                    load_expert(t)

            def load_expert(t):
                sp.wait_ge(s_si, t - 1)
                e = sp.value_load(sel_i[0:1, 0:1], min_val=0, max_val=NE - 1)
                sp.dma_start(w_1[:, :, :], W1[ds(e, 1), :, :].rearrange("e (k p) f -> p (e k) f", p=P)).then_inc(s_ew, 16)
                sp.dma_start(w_2[:, :, :], W2[ds(e, 1), :, :].rearrange("e (k p) f -> p (e k) f", p=P)).then_inc(s_ew, 16)
                sp.dma_start(b1_c[:, :], b1[ds(e, 1), :].rearrange("e (k p) -> p (e k)", p=P)).then_inc(s_ew, 16)
                sp.dma_start(b2_c[:, :], b2[ds(e, 1), :].rearrange("e (k p) -> p (e k)", p=P)).then_inc(s_ew, 16)

            def store(t, qq):
                if t == LAST and not first_q(qq):
                    tok = (NB - 1) * L + piece_q(qq - 1) * CH
                elif first_q(qq):
                    tok = (t - 3) * L + (NQ - 2) * CH
                else:
                    tok = (t - 2) * L + ((qq + (NQ - 2)) % NQ) * CH
                sp.wait_ge(s_fin, piece(t, qq))
                sp.dma_start(out_rows[ds(tok, CH), :].rearrange("(j p) d -> p j d", p=P), b_work(t, qq).x1[:, :, :]
                             ).then_inc(s_out, 16)

            def ab(step, t, qq):
                if step == "fin" and qq > 0:
                    store(t, qq)

            sections(sp, quarter, ab)
            sp.wait_ge(s_out, 16 * NB * NQ)

        @block.gpsimd
        def _(gp):
            gp.memset(eps_c[:, :], EPS).then_inc(s_const, 1)
            gp.memset(ident[:, :], 0.0).then_inc(s_id0, 1)
            gp.wait_ge(s_id0, 1)
            gp.affine_select(out=ident[:, :], in_=ident[:, :], compare_op=ALU.not_equal, fill=1.0, base=0,
                             pattern=[[-1, P]], channel_multiplier=1).then_inc(s_id, 1)
            gp.iota(iota8[:, :], pattern=[[1, NE]], base=0, channel_multiplier=0,
                    allow_small_or_imprecise_dtypes=True).then_inc(s_const, 1)
            gp.memset(ones[:, :], 1.0).then_inc(s_const, 1)
            gp.memset(diag_gb[:, :, :], 0.0).then_inc(s_dg0, 1)
            gp.wait_ge(s_id, 1)
            gp.wait_ge(s_cw, 16)
            for kk in range(KI):
                for tap in range(KC):
                    last = gp.tensor_scalar(diag_w[:, kk, tap, :], ident[:, :], cw_c[:, kk, tap:tap + 1], None, ALU.mult)
            last.then_inc(s_dgw, 1)

            def residual(k):
                gp.wait_ge(s_hm, k + 1)
                wait(gp, s_hxd, 16 * k)
                for j in range(JC):
                    last = gp.tensor_tensor(hx[:, j, :], hm[:, j, :], pre_row[:, 2 * D:3 * D], ALU.mult)
                last.then_inc(s_hxc, 1)
                gp.wait_ge(s_hxc, k + 1)
                gp.tensor_tensor(hx[:, :, :], hx[:, :, :], x_t[:, :, :], ALU.add).then_inc(s_hx, 1)

            def quarter(t, qq):
                first = first_q(qq)
                k = chunk(t, qq)
                for s in range(SPQ):
                    for p in range(LT):
                        for dt in channels_at(t, DU_B_POS, p):
                            i = slot(t, qq, s)
                            if first and s == 0:
                                if t > 1:
                                    gp.wait_ge(s_dui[dt], 32 * (t - 1))
                                else:
                                    gp.wait_ge(s_du, NQ)
                            if dt == 0:
                                gp.wait_ge(s_b, 16 * (i + 1))
                                wait(gp, s_hT, LT * (i - 1))
                            gp.tensor_tensor(h[:, s % 2, dt, :], du[:, dt, :], b_bc[:, s % 2, :],
                                             ALU.mult).then_inc(s_dbu, 1)
                        for lt in tiles_at(t, qq, s, p - ADD_LAG, ACT_LT):
                            i, rank = slot(t, qq, s) - 1, ACT_LT.index(lt)
                            batch = (t - 2) if first and s == 0 else (t - 1)
                            if not (first and s == 1):
                                gp.wait_ge(s_qa, NA * i + rank + 1)
                                wait(gp, s_yg, NA * (i - batch - 2) + rank + 1)
                                gp.tensor_tensor(y[:, lt, :], y[:, lt, :], q_of(rank, s), ALU.add).then_inc(s_yg, 1)
                        if has_ln(t, qq) and at("hx", t, qq, s, p):
                            residual(ln_piece(t, qq))
                        if has_pre(t) and at("delta", t, qq, s, p):
                            gp.wait_ge(s_lp, 2 * (k + 1))
                            dl, lp = piece_delta(t, qq)
                            gp.tensor_tensor(dl, dl, lp, ALU.add).then_inc(s_dl, 1)
                        if has_pre(t) and at("du", t, qq, s, p):
                            gp.wait_ge(s_dl, k + 1)
                            dl, du_ = piece_delta(t, qq)
                            gp.tensor_tensor(du_, dl, xs[:, :, :], ALU.mult).then_inc(s_du, 1)
                        for step in ab_steps(t, qq, s, p) if t < LAST else ():
                            ab(step, t, qq)

            def ab(step, t, qq):
                m, w = piece(t, qq), a_work(t, qq)
                if step == "w_out":
                    gp.wait_ge(s_qrow, 32 * (t - 1))
                    gp.wait_ge(s_wl, 16 * (t - 1))
                    for kk in range(KI):
                        last = gp.tensor_tensor(w_out[:, kk, :], w_out[:, kk, :], post_row[:, 0:D], ALU.mult)
                    last.then_inc(s_wf, 1)
                if step == "gate":
                    gp.wait_ge(s_ud, KI * (m + 1))
                    gp.wait_ge(s_sc, loaded(t, m))
                    gp.tensor_tensor(w.yg[:, :, :], w.yg[:, :, :], w.sres[:, :, :], ALU.mult).then_inc(s_gate, 1)
                if step == "w_o":
                    gp.wait_ge(s_wo, 16 * (t - 1))
                    for kk in range(KD):
                        last = gp.tensor_tensor(w_o[:, kk, :], w_o[:, kk, :], post_row[:, D:2 * D], ALU.mult)
                    last.then_inc(s_wof, 1)

            gp.wait_ge(s_prow, 16)
            residual(0)
            sections(gp, quarter, ab)
            gp.wait_ge(s_b, 16 * (NB * NS + 1))

        @block.scalar
        def _(act):
            act.wait_ge(s_cT, 16 * KD)
            nc.scalar.activation(c_T[:, :, :], c_T[:, :, :], ACT.Silu).then_inc(s_cs, 1)
            act.wait_ge(s_const, 2)

            def exp_and_ln():
                nc.scalar.preload_act_table_set("natural_log_exp_and_others")

            def rsqrt_guess(mv, rs, s_in, s_out_, n):
                act.wait_ge(s_in, n + 1)
                nc.scalar.activation(rs[:, 0, :], mv[:, :, 1], ACT.Ln, bias=eps_c[:, :]).then_inc(s_out_, 1)
                act.wait_ge(s_out_, 2 * n + 1)
                nc.scalar.activation(rs[:, 1, :], rs[:, 0, :], ACT.Exp, scale=-0.5).then_inc(s_out_, 1)

            def fetch_b(i, s):
                wait(act, s_dbu, KI * (i - 1))
                act.dma_start(b_bc[:, s % 2, :], brow_d[ds(i, 1), :].to_broadcast((P, L))).then_inc(s_b, 16)

            def ab(step, t, qq):
                w, b = a_work(t, qq), b_work(t, qq)
                m = piece(t, qq)
                if step in ("up0_out", "up1_out"):
                    u = 0 if step == "up0_out" else 1
                    if u == 0:
                        act.wait_ge(s_ew, 64 * (t - 2 if first_q(qq) else t - 1))
                    bank = ab_bank(t, f"up{u}")
                    act.wait_ge(s_pq, filled(f"up{u}", t, qq))
                    for kk in (2 * u, 2 * u + 1):
                        last = nc.scalar.activation(b.g[:, kk, :], bank[:, (kk % 2) * CH:(kk % 2 + 1) * CH], ACT.Identity,
                                                    bias=b1_c[:, kk:kk + 1])
                    last.then_inc(s_pqf, 1)
                if step == "gelu":
                    act.wait_ge(s_pqf, b_emptied("up1", t, qq))
                    nc.scalar.activation(b.g[:, :, :], b.g[:, :, :], ACT.Gelu).then_inc(s_g, 1)
                    if t < LAST:
                        exp_and_ln()
                if step == "tables":
                    exp_and_ln()
                if step == "down_out":
                    act.wait_ge(s_pq, filled("down", t, qq))
                    if t == LAST and qq == 1:
                        act.wait_ge(s_x, 16 * (NQ * NB + 1))
                    bank = ab_bank(t, "down")
                    for kk in range(KD):
                        last = nc.scalar.activation(b.r_T[:, kk, :], bank[:, kk * CH:(kk + 1) * CH], ACT.Identity,
                                                    bias=b2_c[:, kk:kk + 1])
                    last.then_inc(s_pqf, 1)
                if step == "diag":
                    act.wait_ge(s_qrow, 32 * (t - 1))
                    act.wait_ge(s_dg0, 1)
                    act.wait_ge(s_fin, m)
                    for kk in range(KD):
                        last = nc.scalar.activation(diag_gb[:, kk, kk * P:(kk + 1) * P], ident[:, :], ACT.Copy,
                                                    scale=post_col[:, 2, kk:kk + 1])
                    last.then_inc(s_dg, 1)
                if step == "x1_rs":
                    rsqrt_guess(mv_a, rs_a, s_ast, s_ars, m)
                if step == "xhT_out":
                    act.wait_ge(s_pq, filled("xhT", t, qq))
                    bank = ab_bank(t, "xhT")
                    for kk in range(KD):
                        last = nc.scalar.activation(w.h2T[:, kk, :], bank[:, kk * CH:(kk + 1) * CH], ACT.Identity,
                                                    scale=post_col[:, 0, kk:kk + 1], bias=post_col[:, 1, kk:kk + 1])
                    last.then_inc(s_h2, 1)
                if step == "sel0_out":
                    act.wait_ge(s_pq, filled("sel0", t, qq))
                    nc.scalar.activation(nav[:, :], ab_bank(t, "sel0")[:, 0:1], ACT.Gelu, bias=bp1_c[:, :]).then_inc(s_nav, 1)
                    exp_and_ln()
                if step == "sel_exp":
                    act.wait_ge(s_schain, SEL_STEPS * (t - 2) + 3)
                    nc.scalar.activation(sel[:, 2, :], sel[:, 1, :], ACT.Exp, accum_out=sel[:, 3, 0:1]).then_inc(s_se, 1)

            def hnT_out(t, k):
                act.wait_ge(s_pp, PRE_USES * k + 1)
                for kk in range(KD):
                    last = nc.scalar.activation(hnT[:, kk, :], pre_bank(t, 0)[:, kk * CH:(kk + 1) * CH], ACT.Identity,
                                                scale=nw_c[:, kk:kk + 1], bias=nb_c[:, kk:kk + 1])
                last.then_inc(s_ppf, 1)

            def quarter(t, qq):
                first = first_q(qq)
                k = chunk(t, qq)
                exp_and_ln()
                for s in range(SPQ):
                    for p in range(LT):
                        for dt in channels_at(t, EXP_POS, p):
                            i = slot(t, qq, s)
                            if first and s == 0:
                                if t == 1 and dt == 0:
                                    act.wait_ge(s_bTd, 16 * NQ)
                                    fetch_b(0, 0)
                                if t > 1:
                                    act.wait_ge(s_dli[dt], 32 * (t - 1))
                                else:
                                    act.wait_ge(s_dl, NQ)
                            wait(act, s_scan, KI * i + dt - 1)
                            nc.scalar.activation(pA[dt % 2][:, :], delta[:, dt, :], ACT.Exp,
                                                 scale=A_c[:, dt, ds(SPQ * qq + s, 1)]).then_inc(s_dA, 1)
                            if dt == 3:
                                if s == SPQ - 1:
                                    act.wait_ge(s_bTd, 16 * (chunk(t, qq) + 1) if has_pre(t) else 16 * NQ * NB)
                                    if t == NB:
                                        act.wait_ge(s_pad, 16)
                                fetch_b(i + 1, s + 1)
                        for lt in tiles_at(t, qq, s, p, ACT_LT):
                            i, rank = slot(t, qq, s) - 1, ACT_LT.index(lt)
                            bb = (t - 2) if first and s == 0 else (t - 1)
                            n = NS - 1 if first and s == 0 else SPQ * qq + s - 1
                            if first and s == 1 and rank == 0:
                                act.wait_ge(s_ppf, PRE_USES * NQ * t - 2)
                            act.wait_ge(s_hT, LT * i + lt + 1)
                            if first and s == 1:
                                wait(act, s_ysp, 16 * LT * (t - 1))
                                into = y[:, lt, :]
                            else:
                                back, last_rank = (rank - QR) // NA, (rank - QR) % NA
                                wait(act, s_yg, added(i + back, n + back, bb, last_rank))
                                into = q_of(rank, s)
                            nc.scalar.activation(into, pH[lt % 2][:, :], ACT.Copy,
                                                 scale=C_t[:, bb % 2, lt, ds(n, 1)]).then_inc(s_qa, 1)
                        if has_pre(t):
                            base = PRE_USES * k
                            if has_ln(t, qq) and at("ln1_rs", t, qq, s, p):
                                rsqrt_guess(mv_p, rs_p, s_pst, s_prs, 2 * ln_piece(t, qq))
                            if has_ln(t, qq) and at("ln2_rs", t, qq, s, p):
                                rsqrt_guess(mv_p, rs_p, s_pst, s_prs, 2 * ln_piece(t, qq) + 1)
                            if has_ln(t, qq) and t > 0 and at("hnT_out", t, qq, s, p):
                                hnT_out(t, k)
                            for u in range(2):
                                if at(f"in{u}_out", t, qq, s, p):
                                    act.wait_ge(s_pp, base + 2 + u)
                                    if u == 0:
                                        act.wait_ge(s_move, k + 1)
                                    nc.scalar.copy(xpre[:, 2 * u:2 * u + 2, KC - 1:],
                                                   pre_bank(t, 1 + u)[:, :].rearrange("p (a c) -> p a c", a=2)).then_inc(s_ppf, 1)
                                if at(f"conv{u}_out", t, qq, s, p):
                                    act.wait_ge(s_pp, base + 4 + u)
                                    if u == 0:
                                        wait(act, s_du, k)
                                        wait(act, s_xsd, 16 * k)
                                    for kk in (2 * u, 2 * u + 1):
                                        last = nc.scalar.activation(xs[:, kk, :],
                                                                    pre_bank(t, 3 + u)[:, (kk % 2) * CH:(kk % 2 + 1) * CH],
                                                                    ACT.Identity, bias=cb_c[:, kk:kk + 1])
                                    last.then_inc(s_ppf, 1)
                                if at(f"res{u}_out", t, qq, s, p):
                                    act.wait_ge(s_pp, base + 6 + u)
                                    if u == 0:
                                        wait(act, s_sresd, 16 * k)
                                    nc.scalar.copy(sres[:, 2 * u:2 * u + 2, :],
                                                   pre_bank(t, 5 + u)[:, :].rearrange("p (a c) -> p a c", a=2)).then_inc(s_ppf, 1)
                            if at("silu_x", t, qq, s, p):
                                act.wait_ge(s_ppf, base + 5)
                                nc.scalar.activation(xs[:, :, :], xs[:, :, :], ACT.Silu).then_inc(s_xs, 1)
                            if at("silu_g", t, qq, s, p):
                                act.wait_ge(s_ppf, base + 7)
                                nc.scalar.activation(sres[:, :, :], sres[:, :, :], ACT.Silu).then_inc(s_xs, 1)
                                exp_and_ln()
                            if at("xproj_out", t, qq, s, p):
                                act.wait_ge(s_pp, base + 8)
                                wait(act, s_bTd, 16 * k)
                                nc.scalar.copy(dr[:, :], pre_bank(t, 7)[:, 0:CH])
                                nc.scalar.copy(b_T[:, :], pre_bank(t, 7)[0:NS, CH:2 * CH]).then_inc(s_ppf, 1)
                            if at("cproj_out", t, qq, s, p):
                                act.wait_ge(s_pp, base + 9)
                                if first and t >= 2:
                                    act.wait_ge(s_yv, NV * NS * (t - 1))
                                nc.scalar.copy(C_t[:, t % 2, ds(JC * qq, JC), :],
                                               pre_bank(t, 8)[:, 0:JC * NS].rearrange("p (j n) -> p j n", j=JC)
                                               ).then_inc(s_ppf, 1)
                            for u in range(2):
                                if at(f"dt{u}_out", t, qq, s, p):
                                    act.wait_ge(s_pp, base + 10 + u)
                                    dl, lp = piece_delta(t, qq)
                                    if u == 0 and t > 0 and not first:
                                        act.wait_ge(s_dud, 16 * ((NQ - 1) * (t - 1) + qq))
                                        act.wait_ge(s_dld, 16 * ((NQ - 1) * (t - 1) + qq))
                                    if u == 0 and t > 1 and first:
                                        for tile in range(KI):
                                            act.wait_ge(s_dli[tile], 32 * (t - 1))
                                            act.wait_ge(s_dui[tile], 32 * (t - 1))
                                    for kk in (2 * u, 2 * u + 1):
                                        half = pre_bank(t, 9 + u)[:, (kk % 2) * CH:(kk % 2 + 1) * CH]
                                        nc.scalar.activation(lp[:, kk], half, ACT.Abs, bias=dtb_c[:, kk:kk + 1])
                                        last = nc.scalar.activation(dl[:, kk], half, ACT.Relu,
                                                                    bias=dtb_c[:, kk:kk + 1])
                                    last.then_inc(s_ppf, 1)
                            if has_ln(t, qq) and t == 0 and at("hnT_out", t, qq, s, p):
                                hnT_out(t, k + 1)
                            if at("softplus", t, qq, s, p):
                                _, lp = piece_delta(t, qq)
                                act.wait_ge(s_ppf, base + PRE_USES)
                                nc.scalar.activation(lp, lp, ACT.Exp, scale=-1.0).then_inc(s_lp, 1)
                                act.wait_ge(s_lp, 2 * k + 1)
                                nc.scalar.activation(lp, lp, ACT.Ln, bias=1.0).then_inc(s_lp, 1)
                        for step in ab_steps(t, qq, s, p) if t < LAST else ():
                            ab(step, t, qq)

            exp_and_ln()
            rsqrt_guess(mv_p, rs_p, s_pst, s_prs, 0)
            rsqrt_guess(mv_p, rs_p, s_pst, s_prs, 1)
            act.wait_ge(s_wt, 16 * WEIGHTS)
            hnT_out(0, 0)
            nc.scalar.activation(A_c[:, :, :], A_c[:, :, :], ACT.Exp).then_inc(s_Aexp, 1)
            act.wait_ge(s_Aexp, 1)
            nc.scalar.mul(A_c[:, :, :], A_c[:, :, :], -1.0).then_inc(s_Aexp, 1)
            act.wait_ge(s_Aexp, 2)
            sections(act, quarter, ab)

        @block.vector
        def _(dve):
            yflat = y[:, :, :].rearrange("p a k -> p (a k)")
            steps = [0]

            def link(ins):
                steps[0] += 1
                ins.then_inc(s_vec0, 1)
                dve.wait_ge(s_vec0, steps[0])

            def mod(i):
                return yflat[0:NB, i * D:(i + 1) * D]

            def keep(i):
                return yflat[0:NB, (6 + i) * D:(7 + i) * D]
            bo4 = yflat[0:NB, 3584:3584 + D]
            tmp = yflat[0:NB, 3840:3840 + D]
            def stats(src, st, mv, rs, s_chain, base, s_done):
                for j in range(JC):
                    last = nc.vector.bn_stats(st[:, j, :], src[:, j, :])
                last.then_inc(s_chain, 1)
                dve.wait_ge(s_chain, base + 1)
                nc.vector.memset(rs[:, 2, :], 0.0)
                for j in range(JC):
                    last = nc.vector.bn_aggr(mv[:, j, :], st[:, j, :])
                last.then_inc(s_done, 1)

            def refine(mv, rs, s_chain, base):
                nc.vector.tensor_tensor(rs[:, 2, :], rs[:, 1, :], rs[:, 1, :], ALU.mult).then_inc(s_chain, 1)
                dve.wait_ge(s_chain, base + 1)
                nc.vector.scalar_tensor_tensor(rs[:, 2, :], mv[:, :, 1], EPS, rs[:, 2, :], ALU.add, ALU.mult).then_inc(s_chain, 1)
                dve.wait_ge(s_chain, base + 2)
                nc.vector.tensor_scalar(rs[:, 2, :], rs[:, 2, :], -0.5, 1.5, ALU.mult, ALU.add).then_inc(s_chain, 1)
                dve.wait_ge(s_chain, base + 3)
                nc.vector.tensor_tensor(rs[:, 1, :], rs[:, 1, :], rs[:, 2, :], ALU.mult).then_inc(s_chain, 1)
                dve.wait_ge(s_chain, base + 4)

            PCH = 12
            ACH = 5

            def ln1(k, t, first):
                dve.wait_ge(s_x, 16 * (k + 1))
                stats(x_t, st_p, mv_p, rs_p, s_pchain, PCH * k, s_pst)

            def ln2(k, t, first):
                base = PCH * k
                dve.wait_ge(s_prs, 4 * k + 2)
                refine(mv_p, rs_p, s_pchain, base + 1)
                if first:
                    dve.wait_ge(s_prow, 16 * (t + 1))
                wait(dve, s_hx, k)
                for j in range(JC):
                    last = nc.vector.tensor_scalar(hm[:, j, :], x_t[:, j, :], mv_p[:, j, 0:1],
                                                   rs_p[:, 1, j:j + 1], ALU.subtract, ALU.mult)
                last.then_inc(s_pchain, 1)
                dve.wait_ge(s_pchain, base + 6)
                for j in range(JC):
                    last = nc.vector.tensor_tensor(hm[:, j, :], hm[:, j, :], pre_row[:, 0:D], ALU.mult)
                last.then_inc(s_pchain, 1)
                dve.wait_ge(s_pchain, base + 7)
                for j in range(JC):
                    last = nc.vector.tensor_tensor(hm[:, j, :], hm[:, j, :], pre_row[:, D:2 * D], ALU.add)
                last.then_inc(s_hm, 1)
                dve.wait_ge(s_hm, k + 1)
                stats(hm, st_p, mv_p, rs_p, s_pchain, base + 7, s_pst)

            def second_ln(k, t, first):
                dve.wait_ge(s_prs, 4 * k + 4)
                refine(mv_p, rs_p, s_pchain, PCH * k + 8)
                wait(dve, s_pp, PRE_USES * (k - 1) + 1)
                for j in range(JC):
                    last = nc.vector.tensor_scalar(hn[:, j, :], hm[:, j, :], mv_p[:, j, 0:1],
                                                   rs_p[:, 1, j:j + 1], ALU.subtract, ALU.mult)
                last.then_inc(s_hn, 1)
                wait(dve, s_pp, PRE_USES * (k - 1) + 5)
                if first:
                    nc.vector.memset(xpre[:, :, 0:KC - 1], 0.0).then_inc(s_move, 1)
                else:
                    nc.vector.tensor_copy(xpre[:, :, 0:KC - 1], xpre[:, :, CH:CH + KC - 1]).then_inc(s_move, 1)

            def quarter(t, qq):
                first = first_q(qq)
                k = chunk(t, qq)
                for s in range(SPQ):
                    for p in range(LT):
                        for dt in channels_at(t, SCAN_POS, p):
                            i = slot(t, qq, s)
                            dve.wait_ge(s_dA, KI * i + dt + 1)
                            dve.wait_ge(s_dbu, KI * i + dt + 1)
                            nc.vector.tensor_tensor_scan(h[:, s % 2, dt, :], pA[dt % 2][:, :], h[:, s % 2, dt, :], 0.0,
                                                         ALU.mult, ALU.add).then_inc(s_scan, 1)
                        for lt in tiles_at(t, qq, s, p, VEC_LT):
                            i, rank = slot(t, qq, s) - 1, VEC_LT.index(lt)
                            bb = (t - 2) if first and s == 0 else (t - 1)
                            n = NS - 1 if first and s == 0 else SPQ * qq + s - 1
                            scale = C_t[:, bb % 2, lt, ds(n, 1)]
                            if first and s == 1 and rank == 0:
                                dve.wait_ge(s_ppf, PRE_USES * NQ * t - 2)
                            dve.wait_ge(s_hT, LT * i + lt + 1)
                            wait(dve, s_yv, NV * (i - 1) + rank + 1)
                            if first and s == 1:
                                wait(dve, s_ysp, 16 * LT * (t - 1))
                                nc.vector.tensor_scalar(y[:, lt, :], pH[lt % 2][:, :], scale, None, ALU.mult).then_inc(s_yv, 1)
                            else:
                                nc.vector.scalar_tensor_tensor(y[:, lt, :], pH[lt % 2][:, :], scale, y[:, lt, :],
                                                               ALU.mult, ALU.add).then_inc(s_yv, 1)
                        if has_ln(t, qq):
                            for step, run in (("ln1", ln1), ("ln2", ln2), ("hn", second_ln)):
                                if at(step, t, qq, s, p):
                                    run(ln_piece(t, qq), t, first and t > 0)
                        for step in ab_steps(t, qq, s, p) if t < LAST else ():
                            ab(step, t, qq)

            def ab(step, t, qq):
                m, w = piece(t, qq), a_work(t, qq)
                if step == "fin":
                    dve.wait_ge(s_pq, filled("eout", t, qq))
                    res = b_work(t, qq).x1
                    nc.vector.tensor_tensor(res[:, :, :], res[:, :, :],
                                            ab_bank(t, "eout")[:, :].rearrange("p (j d) -> p j d", j=JC),
                                            ALU.add).then_inc(s_fin, 1)
                if step in ("yT0_out", "yT1_out"):
                    u = 0 if step == "yT0_out" else 1
                    dve.wait_ge(s_pq, filled(f"yT{u}", t, qq))
                    dve.wait_ge(s_xc, loaded(t, m))
                    bank = ab_bank(t, f"yT{u}")
                    for kk in (2 * u, 2 * u + 1):
                        nc.vector.scalar_tensor_tensor(w.yg[:, kk, :], w.yg[:, kk, :], D_c[:, kk:kk + 1],
                                                       bank[:, (kk % 2) * CH:(kk % 2 + 1) * CH],
                                                       ALU.mult, ALU.add).then_inc(s_ud, 1)
                if step == "x1":
                    dve.wait_ge(s_pq, filled("oproj", t, qq))
                    dve.wait_ge(s_hc, loaded(t, m))
                    if t < LAST:
                        wait(dve, s_out, 16 * m)
                    nc.vector.tensor_tensor(w.x1[:, :, :], w.hx[:, :, :],
                                            ab_bank(t, "oproj")[:, :].rearrange("p (j d) -> p j d", j=JC),
                                            ALU.add).then_inc(s_x1, 1)
                    dve.wait_ge(s_x1, m + 1)
                    stats(w.x1, st_a, mv_a, rs_a, s_achain, ACH * m, s_ast)
                if step == "xh":
                    dve.wait_ge(s_ars, 2 * m + 2)
                    refine(mv_a, rs_a, s_achain, ACH * m + 1)
                    for j in range(JC):
                        last = nc.vector.tensor_scalar(w.xh[:, j, :], w.x1[:, j, :], mv_a[:, j, 0:1],
                                                       rs_a[:, 1, j:j + 1], ALU.subtract, ALU.mult)
                    last.then_inc(s_xh, 1)
                if step == "sel1_out":
                    cbase = SEL_STEPS * (t - 2)
                    dve.wait_ge(s_pq, filled("sel1", t, qq))
                    nc.vector.tensor_tensor(sel[:, 0, :], ab_bank(t, "sel1")[0:1, 0:NE], bp2_r[:, :], ALU.add).then_inc(s_schain, 1)
                    dve.wait_ge(s_schain, cbase + 1)
                    nc.vector.reduce_max(sel[:, 3, 1:2], sel[:, 0, :], AX_X).then_inc(s_schain, 1)
                    dve.wait_ge(s_schain, cbase + 2)
                    nc.vector.tensor_scalar(sel[:, 1, :], sel[:, 0, :], sel[:, 3, 1:2], None, ALU.subtract
                                            ).then_inc(s_schain, 1)
                if step == "sel":
                    cbase = SEL_STEPS * (t - 2)
                    dve.wait_ge(s_se, t - 1)
                    nc.vector.reciprocal(sel[:, 3, 2:3], sel[:, 3, 0:1]).then_inc(s_schain, 1)
                    dve.wait_ge(s_schain, cbase + 4)
                    nc.vector.tensor_scalar(sel[:, 4, :], sel[:, 2, :], sel[:, 3, 2:3], None, ALU.mult).then_inc(s_schain, 1)
                    dve.wait_ge(s_schain, cbase + 5)
                    nc.vector.reduce_max(sel[:, 3, 3:4], sel[:, 4, :], AX_X).then_inc(s_schain, 1)
                    dve.wait_ge(s_schain, cbase + 6)
                    nc.vector.tensor_scalar(sel[:, 5, :], sel[:, 4, :], sel[:, 3, 3:4], None, ALU.is_ge).then_inc(s_schain, 1)
                    dve.wait_ge(s_schain, cbase + 7)
                    nc.vector.scalar_tensor_tensor(sel[:, 6, :], iota8[:, :], -float(NE), sel[:, 5, :],
                                                   ALU.add, ALU.mult).then_inc(s_schain, 1)
                    dve.wait_ge(s_schain, cbase + 8)
                    nc.vector.tensor_reduce(sel[:, 3, 4:5], sel[:, 6, :], AX_X, ALU.min).then_inc(s_schain, 1)
                    dve.wait_ge(s_schain, cbase + 9)
                    nc.vector.tensor_scalar(sel[:, 3, 5:6], sel[:, 3, 4:5], float(NE), None, ALU.add).then_inc(s_schain, 1)
                    dve.wait_ge(s_schain, cbase + 10)
                    nc.vector.tensor_copy(sel_i[:, :], sel[:, 3, 5:6]).then_inc(s_si, 1)

            ln1(0, 0, True)
            dve.wait_ge(s_m0, 1)
            nc.vector.tensor_scalar(pre_row[:, 0:D], mod_bank(3)[:, D:2 * D], 1.0, None, ALU.add).then_inc(s_prow0, 1)
            nc.vector.tensor_copy(pre_row[:, D:2 * D], mod_bank(3)[:, 0:D]).then_inc(s_prow0, 1)
            dve.wait_ge(s_prow0, 2)
            ln2(0, 0, False)
            second_ln(0, 0, True)
            for i in range(3):
                dve.wait_ge(s_mod, i + 1)
                link(nc.vector.tensor_copy(yflat[0:NB, i * 512:(i + 1) * 512], mod_bank(i)[0:NB, :]))
            dve.wait_ge(s_wm2, 32)
            link(nc.vector.tensor_scalar(keep(0), mod(1), 1.0, None, ALU.add))
            link(nc.vector.tensor_copy(keep(1), mod(0)))
            for gate, dst in ((2, 2), (5, 7)):
                link(nc.vector.tensor_scalar(tmp, mod(gate), 0.0, 2.0, ALU.is_ge, ALU.mult))
                link(nc.vector.tensor_scalar(tmp, tmp, -1.0, None, ALU.add))
                link(nc.vector.scalar_tensor_tensor(keep(dst), mod(gate), -1.0, mod(gate), ALU.mult, ALU.max))
                link(nc.vector.scalar_tensor_tensor(keep(dst), keep(dst), 0.25, tmp, ALU.max, ALU.mult))
            link(nc.vector.tensor_scalar(keep(5), mod(4), 1.0, None, ALU.add))
            link(nc.vector.tensor_copy(keep(6), mod(3)))
            link(nc.vector.tensor_scalar(keep(3), keep(7), 0.3, None, ALU.mult))
            nc.vector.tensor_tensor(keep(4), keep(3), bo4, ALU.mult).then_inc(s_modv, 1)

            dve.wait_ge(s_wt, 16 * WEIGHTS)
            sections(dve, quarter, ab)

        @block.tensor
        def _(pe):
            hflat = h[:, :, :, :].rearrange("p a k l -> p (a k l)")
            wm = hflat[:, 0:KD * 6 * D].rearrange("p (k n) -> p k n", k=KD)
            pe.wait_ge(s_cs, 1)
            pe.wait_ge(s_wm, 16)
            for kk in range(KD):
                last = nc.tensor.matmul(mod_bank(3), c_T[:, kk, 0:1].to_broadcast((P, P)), wm[:, kk, 0:512],
                                        start=(kk == 0), stop=(kk == KD - 1))
            last.then_inc(s_m0, 1)
            for i in range(3):
                if i == 1:
                    pe.wait_ge(s_wm2, 32)
                for kk in range(KD):
                    last = nc.tensor.matmul(mod_bank(i)[0:NB, :], c_T[:, kk, :], wm[:, kk, i * 512:(i + 1) * 512],
                                            start=(kk == 0), stop=(kk == KD - 1))
                last.then_inc(s_mod, 1)
            pe.wait_ge(s_id, 1)

            def ab(step, t, qq):
                m, w, b = piece(t, qq), a_work(t, qq), b_work(t, qq)
                if step in ("up0", "up1"):
                    u = 0 if step == "up0" else 1
                    if u == 0:
                        pe.wait_ge(s_ew, 64 * (t - 2 if first_q(qq) else t - 1))
                        pe.wait_ge(s_h2, m)
                    if t == LAST:
                        if not first_q(qq):
                            pe.wait_ge(s_pqf, b_emptied(step, t, qq - 1))
                    elif u == 1 and t < NB:
                        pe.wait_ge(s_pqf, b_emptied("up0", t, qq))
                    bank = ab_bank(t, step)
                    for kk in (2 * u, 2 * u + 1):
                        for kd in range(KD):
                            last = nc.tensor.matmul(bank[:, (kk % 2) * CH:(kk % 2 + 1) * CH], w_1[:, kd, kk * P:(kk + 1) * P],
                                                    b.h2T[:, kd, :], start=(kd == 0), stop=(kd == KD - 1))
                    last.then_inc(s_pq, 1)
                if step in ("down", "downb"):
                    kd = 0 if step == "down" else 1
                    if kd == 0:
                        pe.wait_ge(s_g, m)
                    for kk in range(F // P):
                        last = nc.tensor.matmul(ab_bank(t, "down")[:, kd * CH:(kd + 1) * CH], w_2[:, kk, kd * P:(kd + 1) * P],
                                                b.g[:, kk, :], start=(kk == 0), stop=(kk == F // P - 1))
                    if kd == KD - 1:
                        last.then_inc(s_pq, 1)
                if step in ("eout", "eoutb"):
                    j = 0 if step == "eout" else 1
                    if j == 0:
                        pe.wait_ge(s_pqf, b_emptied("down", t, qq))
                        if t == LAST:
                            pe.wait_ge(s_fin, m - 1)
                        if not first_q(qq):
                            pe.wait_ge(s_wof, t - 1)
                            pe.wait_ge(s_dg, t - 1)
                            pe.wait_ge(s_bo, 16 * (t - 1))
                    into, tok = ab_bank(t, "eout")[:, j * D:(j + 1) * D], slice(j * P, (j + 1) * P)
                    for kd in range(KD):
                        nc.tensor.matmul(into, b.r_T[:, kd, tok], w_o[:, kd, :], start=(kd == 0), stop=False)
                    for kd in range(KD):
                        nc.tensor.matmul(into, b.h2T[:, kd, tok], diag_gb[:, kd, :], start=False, stop=False)
                    last = nc.tensor.matmul(into, ones[:, :], bo_row[:, :], start=False, stop=True)
                    if j == JC - 1:
                        last.then_inc(s_pq, 1)
                if step in ("yT0", "yT1"):
                    u = 0 if step == "yT0" else 1
                    if t == LAST:
                        for lt in range(piece_q(qq) * JC, (piece_q(qq) + 1) * JC):
                            if lt in VEC_LT:
                                pe.wait_ge(s_yv, NV * (NS * NB - 1) + VEC_LT.index(lt) + 1)
                            else:
                                pe.wait_ge(s_yg, NA * ((NS - 1) * NB - 1) + ACT_LT.index(lt) + 1)
                        if first_q(qq):
                            pe.wait_ge(s_scan, KI * NS * NB)
                        else:
                            pe.wait_ge(s_ud, KI * (m - 1) + 2 * u + 2)
                    elif u == 0:
                        pe.wait_ge(s_yc, 16 * (m + 1))
                        if t < NB:
                            wait(pe, s_fin, m)
                    elif t < NB:
                        pe.wait_ge(s_ud, KI * m + 2)
                    else:
                        pe.wait_ge(s_fin, m)
                    for kk in (2 * u, 2 * u + 1):
                        for j in range(JC):
                            last = nc.tensor.transpose(ab_bank(t, step)[:, (kk % 2) * CH + j * P:(kk % 2) * CH + (j + 1) * P],
                                                       w.y[:, j, kk * P:(kk + 1) * P], ident[:, :])
                    last.then_inc(s_pq, 1)
                if step in ("oproj", "oprojb"):
                    j = 0 if step == "oproj" else 1
                    if j == 0:
                        pe.wait_ge(s_gate, m + 1)
                        pe.wait_ge(s_wf, t - 1)
                        if t == LAST:
                            pe.wait_ge(s_x1, m)
                    for kk in range(KI):
                        last = nc.tensor.matmul(ab_bank(t, "oproj")[:, j * D:(j + 1) * D], w.yg[:, kk, j * P:(j + 1) * P],
                                                w_out[:, kk, :], start=(kk == 0), stop=(kk == KI - 1))
                    if j == JC - 1:
                        last.then_inc(s_pq, 1)
                if step == "xhT":
                    pe.wait_ge(s_xh, m + 1)
                    if t == LAST:
                        pe.wait_ge(s_h2, m)
                    for kk in range(KD):
                        for j in range(JC):
                            last = nc.tensor.transpose(ab_bank(t, step)[:, kk * CH + j * P:kk * CH + (j + 1) * P],
                                                       w.xh[:, j, kk * P:(kk + 1) * P], ident[:, :])
                    last.then_inc(s_pq, 1)
                if step == "sel0":
                    pe.wait_ge(s_h2, m + 1)
                    for kk in range(KD):
                        last = nc.tensor.matmul(ab_bank(t, step)[:, 0:1], w_p1[:, kk, :], w.h2T[:, kk, CH - 1:CH],
                                                start=(kk == 0), stop=(kk == KD - 1))
                    last.then_inc(s_pq, 1)
                if step == "sel1":
                    pe.wait_ge(s_nav, t - 1)
                    nc.tensor.matmul(ab_bank(t, step)[0:1, 0:NE], nav[:, :], w_p2[:, :], start=True, stop=True).then_inc(s_pq, 1)

            def hn_transposed(t, k):
                pe.wait_ge(s_hn, k + 1)
                wait(pe, s_ppf, pre_empty(t, k, 0))
                bank = pre_bank(t, 0)
                for kk in range(KD):
                    for j in range(JC):
                        last = nc.tensor.transpose(bank[:, kk * CH + j * P:kk * CH + (j + 1) * P],
                                                   hn[:, j, kk * P:(kk + 1) * P], ident[:, :])
                last.then_inc(s_pp, 1)

            def h_transposed(t, qq, s, lt):
                i = slot(t, qq, s) - 1
                if lt == 0:
                    pe.wait_ge(s_scan, KI * (i + 1))
                prev, n_, rank = consumed((lt - 2) % LT)
                wait(pe, prev, n_ * (i if lt >= 2 else i - 1) + rank + 1)
                for dt in range(KI):
                    last = nc.tensor.transpose(pH[lt % 2][:, dt * P:(dt + 1) * P],
                                               h[:, (s + 1) % 2, dt, lt * P:(lt + 1) * P], ident[:, :])
                last.then_inc(s_hT, 1)

            def quarter(t, qq):
                first = first_q(qq)
                k = chunk(t, qq)
                for s in range(SPQ):
                    for p in range(LT):
                        for lt in range(LT):
                            if has_tail(t, qq, s) and TURN_POS[lt] == p:
                                h_transposed(t, qq, s, lt)
                        if has_pre(t):
                            def fill(use, needs=-PRE_USES):
                                wait(pe, s_ppf, pre_empty(t, k, use, needs))
                                return pre_bank(t, use)

                            if has_ln(t, qq) and at("hnT", t, qq, s, p):
                                hn_transposed(t, ln_piece(t, qq))
                            for u in range(2):
                                if at(f"in{u}", t, qq, s, p) or at(f"res{u}", t, qq, s, p):
                                    gate = at(f"res{u}", t, qq, s, p)
                                    bank = fill((5 if gate else 1) + u, 1)
                                    for half in range(2):
                                        col = (DI if gate else 0) + (2 * u + half) * P
                                        for kk in range(KD):
                                            last = nc.tensor.matmul(bank[:, half * CH:(half + 1) * CH], w_in[:, kk, col:col + P],
                                                                    hnT[:, kk, :], start=(kk == 0), stop=(kk == KD - 1))
                                    last.then_inc(s_pp, 1)
                                for half, step in enumerate((f"conv{u}", f"conv{u}b")):
                                    if at(step, t, qq, s, p):
                                        kk = 2 * u + half
                                        bank = fill(3 + u, 2 + u) if half == 0 else pre_bank(t, 3 + u)
                                        for tap in range(KC):
                                            last = nc.tensor.matmul(bank[:, half * CH:(half + 1) * CH], diag_w[:, kk, tap, :],
                                                                    xpre[:, kk, tap:tap + CH],
                                                                    start=(tap == 0), stop=(tap == KC - 1))
                                        if half:
                                            last.then_inc(s_pp, 1)
                            if at("xproj", t, qq, s, p):
                                bank = fill(7)
                                pe.wait_ge(s_xs, 2 * k + 1)
                                for kk in range(KI):
                                    nc.tensor.matmul(bank[:, 0:CH], w_x[:, kk, 0:R], xs[:, kk, :],
                                                     start=(kk == 0), stop=(kk == KI - 1))
                            if at("xprojb", t, qq, s, p):
                                bank = pre_bank(t, 7)
                                for kk in range(KI):
                                    last = nc.tensor.matmul(bank[0:NS, CH:2 * CH], w_x[:, kk, R:R + NS], xs[:, kk, :],
                                                            start=(kk == 0), stop=(kk == KI - 1))
                                last.then_inc(s_pp, 1)
                            if at("cproj", t, qq, s, p):
                                bank = fill(8)
                                for j in range(JC):
                                    for kk in range(KI):
                                        last = nc.tensor.matmul(bank[:, j * NS:(j + 1) * NS], xs[:, kk, j * P:(j + 1) * P],
                                                                w_x[:, kk, R + NS:R + 2 * NS],
                                                                start=(kk == 0), stop=(kk == KI - 1))
                                last.then_inc(s_pp, 1)
                            for u in range(2):
                                if at(f"dt{u}", t, qq, s, p):
                                    bank = fill(9 + u, 8)
                                    for kk in (2 * u, 2 * u + 1):
                                        last = nc.tensor.matmul(bank[:, (kk % 2) * CH:(kk % 2 + 1) * CH],
                                                                w_dt[:, kk * P:(kk + 1) * P], dr[:, :], start=True, stop=True)
                                    last.then_inc(s_pp, 1)
                        for step in ab_steps(t, qq, s, p) if t < LAST else ():
                            ab(step, t, qq)

            hn_transposed(0, 0)
            pe.wait_ge(s_wt, 16 * WEIGHTS)
            pe.wait_ge(s_dgw, 1)
            pe.wait_ge(s_const, 3)
            sections(pe, quarter, ab)


INPUTS = [
    "L0_attn_x", "L0_attn_norm_w", "L0_attn_norm_b", "L0_attn_in_proj_w", "L0_attn_conv_w", "L0_attn_conv_b",
    "L0_attn_x_proj_w", "L0_attn_dt_proj_w", "L0_attn_dt_proj_b", "L0_attn_A_log", "L0_attn_D_param",
    "L0_attn_out_proj_w", "L0_ffn_Wp1", "L0_ffn_bp1", "L0_ffn_Wp2", "L0_ffn_bp2", "L0_ffn_W1", "L0_ffn_b1",
    "L0_ffn_W2", "L0_ffn_b2", "L0_ffn_Wo", "L0_ffn_bo", "L0_c", "L0_wmod",
]


def kernel(**inputs):
    import numpy as np
    import concourse.bacc as bacc
    from concourse.bass_utils import run_bass_kernel_spmd

    nc = bacc.Bacc("TRN2", target_bir_lowering=False, num_devices=1)
    arrays, args = {}, []
    for name in INPUTS:
        a = np.ascontiguousarray(inputs[name])
        arrays[f"in_{name}"] = a
        args.append(nc.dram_tensor(f"in_{name}", a.shape, mybir.dt.from_np(a.dtype), kind="ExternalInput").ap())
    args.append(nc.dram_tensor("out_0", (NB, L, D), F32, kind="ExternalOutput").ap())
    build(nc, *args)
    result = run_bass_kernel_spmd(nc, [arrays], core_ids=[0])
    return result.results[0]["out_0"]
```
